# Optimizing a Trainium2 kernel written in Bass

```python
import numpy as np
import jax
import jax.numpy as jnp

def _softmax(x, axis=-1):
    return jax.nn.softmax(x, axis=axis)

def _gelu(x):
    return jax.nn.gelu(x, approximate=True)

def _silu(x):
    return jax.nn.silu(x)

def _sigmoid(x):
    return jax.nn.sigmoid(x)

def _layernorm(x, axis=-1, eps=1e-05):
    m = jnp.mean(x, axis=axis, keepdims=True)
    v = jnp.var(x, axis=axis, keepdims=True)
    return (x - m) / jnp.sqrt(v + eps)

def _scatter_add(tgt, idx, src, axis=0):
    return tgt.at[idx].add(src)

def _segment_sum(src, seg, n):
    return jax.ops.segment_sum(src, seg, n)
kernel_name = 'mk_gnn_preln_d4_gnn_r8_3050bd'

def setup_inputs(seed: int=0):
    np.random.seed(seed)
    _w = jnp.asarray

    def _rec_inputs():
        import jax
        import jax.numpy as jnp
        _gk = jax.random.key(seed)
        x = -0.0002117 + 1 * jax.random.normal(jax.random.fold_in(_gk, 1), (6250, 256), jnp.float32)
        _s = jax.random.randint(jax.random.fold_in(_gk, 2), (50000,), 0, 6250, jnp.int32)
        _d = jax.random.randint(jax.random.fold_in(_gk, 3), (50000,), 0, 6250, jnp.int32)
        _loop = jnp.arange(6250, dtype=jnp.int32)
        src = jnp.concatenate([_s, _d, _loop])
        dst = jnp.concatenate([_d, _s, _loop])
        _o = jnp.argsort(dst, stable=True)
        src = src[_o]
        dst = dst[_o]
        edge_attr_16 = -0.000153872 + 1.00011 * jax.random.normal(jax.random.fold_in(_gk, 12), (106250, 16), jnp.float32)
        edge_attr_4 = 0.0007022 + 0.999661 * jax.random.normal(jax.random.fold_in(_gk, 13), (106250, 4), jnp.float32)
        edge_attr_65 = 0.000166551 + 1.00014 * jax.random.normal(jax.random.fold_in(_gk, 14), (106250, 65), jnp.float32)
        edge_weight = jax.random.uniform(jax.random.fold_in(_gk, 16), (106250,), jnp.float32, 0.0, 0.03125)
        return (x, src, dst, edge_attr_16, edge_attr_4, edge_attr_65, edge_weight)
    x, src, dst, edge_attr_16, edge_attr_4, edge_attr_65, edge_weight = _rec_inputs()

    def _L0_gnn_setup():
        import jax, jax.numpy as jnp
        import numpy as np
        N_NODES = 12500
        N_EDGES = 400000
        DIM = 256
        LEAKY_SLOPE = 0.2
        EPS = 1e-12
        key = jax.random.key(seed)
        ks = jax.random.split(key, 8)
        embeddings = jax.random.normal(ks[0], (N_NODES, DIM), dtype=jnp.float32)
        edge_src = jax.random.randint(ks[1], (N_EDGES,), 0, N_NODES, dtype=jnp.int32)
        edge_dst = jax.random.randint(ks[2], (N_EDGES,), 0, N_NODES, dtype=jnp.int32)
        edge_val = jax.random.uniform(ks[3], (N_EDGES,), dtype=jnp.float32) / 32.0
        scale = 1.0 / np.sqrt(DIM)
        W1 = jax.random.normal(ks[4], (DIM, DIM), dtype=jnp.float32) * scale
        b1 = jax.random.normal(ks[5], (DIM,), dtype=jnp.float32) * 0.01
        W2 = jax.random.normal(ks[6], (DIM, DIM), dtype=jnp.float32) * scale
        b2 = jax.random.normal(ks[7], (DIM,), dtype=jnp.float32) * 0.01
        return {'embeddings': embeddings, 'edge_src': edge_src, 'edge_dst': edge_dst, 'edge_val': edge_val, 'W1': W1, 'b1': b1, 'W2': W2, 'b2': b2}
    _L0_gnn_all = _L0_gnn_setup()
    _L0_gnn_in = {k: v for k, v in _L0_gnn_all.items() if k in ('W1', 'b1', 'W2', 'b2')}
    del _L0_gnn_all

    def _L1_gnn_setup():
        import jax, jax.numpy as jnp
        import numpy as np
        N_NODES = 6250
        N_EDGES = 100000
        DIM = 256
        key = jax.random.key(seed)
        k1, k2, k3, k4, k5 = jax.random.split(key, 5)
        x = jax.random.normal(k1, (N_NODES, DIM), dtype=jnp.float32)
        edge_index = jax.random.randint(k2, (2, N_EDGES), 0, N_NODES, dtype=jnp.int64)
        W1 = jax.random.normal(k3, (DIM, DIM), dtype=jnp.float32) / np.sqrt(DIM)
        W2 = jax.random.normal(k4, (DIM, DIM), dtype=jnp.float32) / np.sqrt(DIM)
        return {'x': x, 'edge_index': edge_index, 'W1': W1, 'W2': W2}
    _L1_gnn_all = _L1_gnn_setup()
    _L1_gnn_in = {k: v for k, v in _L1_gnn_all.items() if k in ('W1', 'W2')}
    del _L1_gnn_all

    def _L2_gnn_setup():
        import jax, jax.numpy as jnp
        import numpy as np
        N_NODES = 6250
        N_EDGES = 100000
        D = 256
        F_EDGE = 64
        LN_EPS = 1e-05
        key = jax.random.key(seed)
        ks = jax.random.split(key, 12)
        s = 0.05
        return {'x': jax.random.normal(ks[0], (N_NODES, D), jnp.float32), 'edge_index': jax.random.randint(ks[1], (2, N_EDGES), 0, N_NODES, jnp.int64), 'edge_attr': jax.random.normal(ks[2], (N_EDGES, F_EDGE + 1), jnp.float32), 'W_e1': jax.random.normal(ks[3], (D, F_EDGE), jnp.float32) * s, 'b_e1': jnp.zeros((D,), jnp.float32), 'W_e2': jax.random.normal(ks[4], (D, D), jnp.float32) * s, 'b_e2': jnp.zeros((D,), jnp.float32), 'W_le': jax.random.normal(ks[5], (D, D), jnp.float32) * s, 'b_le': jnp.zeros((D,), jnp.float32), 'W_g1': jax.random.normal(ks[6], (D, D), jnp.float32) * s, 'b_g1': jnp.zeros((D,), jnp.float32), 'ln_g': jnp.ones((D,), jnp.float32), 'ln_b': jnp.zeros((D,), jnp.float32), 'W_g2': jax.random.normal(ks[7], (D, D), jnp.float32) * s, 'b_g2': jnp.zeros((D,), jnp.float32)}
    _L2_gnn_all = _L2_gnn_setup()
    _L2_gnn_in = {k: v for k, v in _L2_gnn_all.items() if k in ('W_e1', 'b_e1', 'W_e2', 'b_e2', 'W_le', 'b_le', 'W_g1', 'b_g1', 'ln_g', 'ln_b', 'W_g2', 'b_g2')}
    del _L2_gnn_all

    def _L3_gnn_setup():
        import jax, jax.numpy as jnp
        import numpy as np
        N, E, C, R, HID = (6250, 62500, 64, 16, 64)
        key = jax.random.key(seed)
        ks = jax.random.split(key, 24)
        g = lambda k, shape, s=1.0: jax.random.normal(k, shape, dtype=jnp.float32) * s
        cs = C ** (-0.5)
        inp = {'h': g(ks[0], (N, 4 * C)), 'edge_index': jax.random.randint(ks[1], (2, E), 0, N), 'edge_sh': g(ks[2], (E, 4)), 'edge_rbf': g(ks[3], (E, R)), 'W_up0': g(ks[4], (C, C), cs), 'W_up1': g(ks[5], (C, C), cs), 'M1': g(ks[6], (R, HID), R ** (-0.5)), 'M2': g(ks[7], (HID, HID), HID ** (-0.5)), 'M3': g(ks[8], (HID, HID), HID ** (-0.5)), 'M4': g(ks[9], (HID, 4 * C), HID ** (-0.5)), 'W_lin0': g(ks[10], (C, C), cs), 'W_lin1': g(ks[11], (C, C), cs), 'Wsc0': g(ks[12], (C, C), cs), 'Wsc1': g(ks[13], (C, C), cs), 'Wc0': g(ks[14], (C, 5)), 'Wc1': g(ks[15], (C, 4)), 'WB0': g(ks[16], (C, C), cs), 'WB1': g(ks[17], (C, C), cs), 'gamma0': jnp.ones((C,), jnp.float32), 'beta0': jnp.zeros((C,), jnp.float32), 'gamma1': jnp.ones((C,), jnp.float32)}
        return inp
    _L3_gnn_all = _L3_gnn_setup()
    _L3_gnn_in = {k: v for k, v in _L3_gnn_all.items() if k in ('W_up0', 'W_up1', 'M1', 'M2', 'M3', 'M4', 'W_lin0', 'W_lin1', 'Wsc0', 'Wsc1', 'Wc0', 'Wc1', 'WB0', 'WB1', 'gamma0', 'beta0', 'gamma1')}
    del _L3_gnn_all
    return {'x': x, 'src': src, 'dst': dst, 'edge_attr_16': edge_attr_16, 'edge_attr_4': edge_attr_4, 'edge_attr_65': edge_attr_65, 'edge_weight': edge_weight, 'L0_gnn_W1': _L0_gnn_in['W1'], 'L0_gnn_b1': _L0_gnn_in['b1'], 'L0_gnn_W2': _L0_gnn_in['W2'], 'L0_gnn_b2': _L0_gnn_in['b2'], 'L1_gnn_W1': _L1_gnn_in['W1'], 'L1_gnn_W2': _L1_gnn_in['W2'], 'L2_gnn_W_e1': _L2_gnn_in['W_e1'], 'L2_gnn_b_e1': _L2_gnn_in['b_e1'], 'L2_gnn_W_e2': _L2_gnn_in['W_e2'], 'L2_gnn_b_e2': _L2_gnn_in['b_e2'], 'L2_gnn_W_le': _L2_gnn_in['W_le'], 'L2_gnn_b_le': _L2_gnn_in['b_le'], 'L2_gnn_W_g1': _L2_gnn_in['W_g1'], 'L2_gnn_b_g1': _L2_gnn_in['b_g1'], 'L2_gnn_ln_g': _L2_gnn_in['ln_g'], 'L2_gnn_ln_b': _L2_gnn_in['ln_b'], 'L2_gnn_W_g2': _L2_gnn_in['W_g2'], 'L2_gnn_b_g2': _L2_gnn_in['b_g2'], 'L3_gnn_W_up0': _L3_gnn_in['W_up0'], 'L3_gnn_W_up1': _L3_gnn_in['W_up1'], 'L3_gnn_M1': _L3_gnn_in['M1'], 'L3_gnn_M2': _L3_gnn_in['M2'], 'L3_gnn_M3': _L3_gnn_in['M3'], 'L3_gnn_M4': _L3_gnn_in['M4'], 'L3_gnn_W_lin0': _L3_gnn_in['W_lin0'], 'L3_gnn_W_lin1': _L3_gnn_in['W_lin1'], 'L3_gnn_Wsc0': _L3_gnn_in['Wsc0'], 'L3_gnn_Wsc1': _L3_gnn_in['Wsc1'], 'L3_gnn_Wc0': _L3_gnn_in['Wc0'], 'L3_gnn_Wc1': _L3_gnn_in['Wc1'], 'L3_gnn_WB0': _L3_gnn_in['WB0'], 'L3_gnn_WB1': _L3_gnn_in['WB1'], 'L3_gnn_gamma0': _L3_gnn_in['gamma0'], 'L3_gnn_beta0': _L3_gnn_in['beta0'], 'L3_gnn_gamma1': _L3_gnn_in['gamma1']}

def reference(x, src, dst, edge_attr_16, edge_attr_4, edge_attr_65, edge_weight, L0_gnn_W1, L0_gnn_b1, L0_gnn_W2, L0_gnn_b2, L1_gnn_W1, L1_gnn_W2, L2_gnn_W_e1, L2_gnn_b_e1, L2_gnn_W_e2, L2_gnn_b_e2, L2_gnn_W_le, L2_gnn_b_le, L2_gnn_W_g1, L2_gnn_b_g1, L2_gnn_ln_g, L2_gnn_ln_b, L2_gnn_W_g2, L2_gnn_b_g2, L3_gnn_W_up0, L3_gnn_W_up1, L3_gnn_M1, L3_gnn_M2, L3_gnn_M3, L3_gnn_M4, L3_gnn_W_lin0, L3_gnn_W_lin1, L3_gnn_Wsc0, L3_gnn_Wsc1, L3_gnn_Wc0, L3_gnn_Wc1, L3_gnn_WB0, L3_gnn_WB1, L3_gnn_gamma0, L3_gnn_beta0, L3_gnn_gamma1):
    import jax
    import jax.numpy as jnp

    def _L0_gnn_ref(embeddings, edge_src, edge_dst, edge_val, W1, b1, W2, b2):
        import jax, jax.numpy as jnp
        import numpy as np
        N_NODES = 12500
        N_EDGES = 400000
        DIM = 256
        LEAKY_SLOPE = 0.2
        EPS = 1e-12
        ego_emb = embeddings @ W1.T + b1
        messages = edge_val[:, None] * embeddings[edge_src]
        neighbor_emb = jax.ops.segment_sum(messages, edge_dst, num_segments=embeddings.shape[0])
        interaction_emb = neighbor_emb * embeddings
        side_emb = (neighbor_emb + interaction_emb) @ W2.T + b2
        out = ego_emb + side_emb
        out = jnp.where(out >= 0, out, LEAKY_SLOPE * out)
        norm = jnp.sqrt(jnp.sum(out * out, axis=1, keepdims=True))
        return out / jnp.maximum(norm, EPS)

    def _L1_gnn_ref(x, edge_index, W1, W2):
        import jax, jax.numpy as jnp
        import numpy as np
        N_NODES = 6250
        N_EDGES = 100000
        DIM = 256
        self_part = x @ W1.T
        proj = x @ W2.T
        src, dst = (edge_index[0], edge_index[1])
        source_feats = proj[src]
        neighbor_part = jax.ops.segment_sum(source_feats, dst, num_segments=x.shape[0])
        return jax.nn.relu(self_part + neighbor_part)

    def _L2_gnn_ref(x, edge_index, edge_attr, W_e1, b_e1, W_e2, b_e2, W_le, b_le, W_g1, b_g1, ln_g, ln_b, W_g2, b_g2):
        import jax, jax.numpy as jnp
        import numpy as np
        N_NODES = 6250
        N_EDGES = 100000
        D = 256
        F_EDGE = 64
        LN_EPS = 1e-05
        polarity = jnp.clip(edge_attr[:, 0:1], 0.0, 1.0)
        raw = edge_attr[:, 1:]
        e = jax.nn.relu(raw @ W_e1.T + b_e1) @ W_e2.T + b_e2
        gated = e * (polarity + 0.01)
        edge_emb = gated @ W_le.T + b_le
        src, dst = (edge_index[0], edge_index[1])
        msg = jax.nn.relu(x[src] + edge_emb)
        aggr = jax.ops.segment_sum(msg, dst, num_segments=x.shape[0])
        h = (x + aggr) @ W_g1.T + b_g1
        mu = jnp.mean(h, axis=-1, keepdims=True)
        var = jnp.mean(jnp.square(h - mu), axis=-1, keepdims=True)
        hn = (h - mu) * jax.lax.rsqrt(var + LN_EPS) * ln_g + ln_b
        return jax.nn.relu(hn) @ W_g2.T + b_g2

    def _L3_gnn_ref(h, edge_index, edge_sh, edge_rbf, W_up0, W_up1, M1, M2, M3, M4, W_lin0, W_lin1, Wsc0, Wsc1, Wc0, Wc1, WB0, WB1, gamma0, beta0, gamma1):
        import jax, jax.numpy as jnp
        import numpy as np
        N, E, C, R, HID = (6250, 62500, 64, 16, 64)
        n = h.shape[0]
        h0 = h[:, :C]
        h1 = h[:, C:].reshape(n, C, 3)
        up0 = h0 @ W_up0
        up1 = jnp.einsum('ncx,cd->ndx', h1, W_up1)
        r = jax.nn.silu(edge_rbf @ M1)
        r = jax.nn.silu(r @ M2)
        r = jax.nn.silu(r @ M3)
        tpw = (r @ M4).reshape(-1, 4, C)
        snd, rcv = (edge_index[0], edge_index[1])
        x0 = up0[snd]
        x1 = up1[snd]
        sh0 = edge_sh[:, 0]
        sh1 = edge_sh[:, 1:]
        inv3 = 1.0 / jnp.sqrt(jnp.float32(3.0))
        m0e = tpw[:, 0] * x0 * sh0[:, None] + tpw[:, 3] * jnp.einsum('ecx,ex->ec', x1, sh1) * inv3
        m1e = tpw[:, 1][:, :, None] * x0[:, :, None] * sh1[:, None, :] + tpw[:, 2][:, :, None] * x1 * sh0[:, None, None]
        msg0 = jax.ops.segment_sum(m0e, rcv, num_segments=n)
        msg1 = jax.ops.segment_sum(m1e, rcv, num_segments=n)
        A0 = msg0 @ W_lin0
        A1 = jnp.einsum('ncx,cd->ndx', msg1, W_lin1)
        sc0 = h0 @ Wsc0
        sc1 = jnp.einsum('ncx,cd->ndx', h1, Wsc1)
        vv = jnp.sum(A1 * A1, -1)
        B0 = Wc0[:, 0] * A0 + Wc0[:, 1] * A0 * A0 + Wc0[:, 2] * vv + Wc0[:, 3] * A0 ** 3 + Wc0[:, 4] * A0 * vv
        B1 = (Wc1[:, 0] + Wc1[:, 1] * A0 + Wc1[:, 2] * A0 * A0 + Wc1[:, 3] * vv)[..., None] * A1
        o0 = B0 @ WB0 + sc0
        o1 = jnp.einsum('ncx,cd->ndx', B1, WB1) + sc1
        eps = jnp.float32(1e-05)
        mu = jnp.mean(o0, 0)
        xc = o0 - mu
        var = jnp.mean(xc * xc, 0)
        n0 = xc * jax.lax.rsqrt(var + eps) * gamma0 + beta0
        nrm1 = jnp.mean(jnp.sum(o1 * o1, -1) / 3.0, 0)
        n1 = o1 * (jax.lax.rsqrt(nrm1 + eps) * gamma1)[None, :, None]
        return jnp.concatenate([n0, n1.reshape(n, 3 * C)], -1)
    edge_index = jnp.stack([src, dst])
    h = jnp.maximum(_layernorm(x, axis=-1), 0.0)
    x = x + _L0_gnn_ref(h, src, dst, edge_weight, L0_gnn_W1, L0_gnn_b1, L0_gnn_W2, L0_gnn_b2)
    h = jnp.maximum(_layernorm(x, axis=-1), 0.0)
    x = x + _L1_gnn_ref(h, edge_index, L1_gnn_W1, L1_gnn_W2)
    h = jnp.maximum(_layernorm(x, axis=-1), 0.0)
    x = x + _L2_gnn_ref(h, edge_index, edge_attr_65, L2_gnn_W_e1, L2_gnn_b_e1, L2_gnn_W_e2, L2_gnn_b_e2, L2_gnn_W_le, L2_gnn_b_le, L2_gnn_W_g1, L2_gnn_b_g1, L2_gnn_ln_g, L2_gnn_ln_b, L2_gnn_W_g2, L2_gnn_b_g2)
    h = jnp.maximum(_layernorm(x, axis=-1), 0.0)
    x = x + _L3_gnn_ref(h, edge_index, edge_attr_4, edge_attr_16, L3_gnn_W_up0, L3_gnn_W_up1, L3_gnn_M1, L3_gnn_M2, L3_gnn_M3, L3_gnn_M4, L3_gnn_W_lin0, L3_gnn_W_lin1, L3_gnn_Wsc0, L3_gnn_Wsc1, L3_gnn_Wc0, L3_gnn_Wc1, L3_gnn_WB0, L3_gnn_WB1, L3_gnn_gamma0, L3_gnn_beta0, L3_gnn_gamma1)
    return x

_drawn_inputs = setup_inputs


def setup_inputs(seed=0):
    import zlib

    import numpy as np

    out = dict(_drawn_inputs(seed))
    spreads = {'L2_gnn_b_e1': (0.0, 0.8),
     'L2_gnn_b_e2': (0.0, 0.8),
     'L2_gnn_b_le': (0.0, 0.8),
     'L2_gnn_b_g1': (0.0, 0.8),
     'L2_gnn_ln_g': (1.0, 0.6),
     'L2_gnn_ln_b': (0.0, 0.714),
     'L2_gnn_b_g2': (0.0, 0.391),
     'L3_gnn_gamma0': (1.0, 0.6),
     'L3_gnn_beta0': (0.0, 0.8),
     'L3_gnn_gamma1': (1.0, 0.2)}
    factors = {'edge_attr_65': 8.0,
     'edge_weight': 8.0,
     'L0_gnn_b1': 8.0,
     'L0_gnn_W2': 3.334,
     'L0_gnn_b2': 8.0,
     'L2_gnn_W_e1': 8.0,
     'L2_gnn_W_e2': 8.0,
     'L2_gnn_W_le': 8.0,
     'L3_gnn_Wsc0': 8.0}
    for name, (base, spread) in spreads.items():
        noise = np.random.default_rng([zlib.crc32(name.encode()), seed]).standard_normal(out[name].shape)
        drawn = base * np.exp(spread * noise) if base else spread * noise
        out[name] = jnp.asarray(drawn.astype(out[name].dtype))
    for name, factor in factors.items():
        out[name] = (out[name] * factor).astype(out[name].dtype)
    return out
```

```python
from contextlib import ExitStack

import numpy as np

import concourse.bass as bass
from concourse import mybir

F32 = mybir.dt.float32
BF16 = mybir.dt.bfloat16
I32 = mybir.dt.int32
ALU = mybir.AluOpType
ACT = mybir.ActivationFunctionType
AX_X = mybir.AxisListType.X
RMAX = bass.bass_isa.ReduceOp.max

P = 128
D = 256
C = 64
LN_EPS = 1e-5
NORM_EPS = 1e-12
LEAKY = 0.2
WIN = 64
GROUPS = [(0, 4), (4, 3), (7, 4), (11, 3), (14, 3)]
TPI = 17
NG = len(GROUPS)
BPAD = 8
NODE_AT = 2
MB = 3
MW = 384

WEIGHTS = ["l0_w1", "l0_w2", "l1_w1", "l1_w2", "g1", "g2", "up", "e2", "le", "lin", "wb", "sc"]
PLACE = {"l0_w1": 0, "l0_w2": 1, "l1_w1": 2, "l1_w2": 3, "g1": 4, "g2": 5, "up": 6, "lin": 0, "wb": 1, "sc": 2}
ROWS = ["b_le", "b_g1", "ln_g", "ln_b", "b_g2", "wc0a", "wc0b", "wc1", "norm"]


def shapes(n_nodes, n_edges):
    nb = -(-n_nodes // P)
    ni = -(-n_edges // (P * TPI))
    assert nb == ni
    return nb, ni


def build(nc, io, n_nodes, n_edges):
    NB, NI = shapes(n_nodes, n_edges)
    T = NI * TPI
    LAST = n_nodes - (NB - 1) * P
    NCOL = NB * P + WIN
    ALLWIN = NCOL // WIN
    CH = max(c for c in range(1, 8) if NB % c == 0)

    with ExitStack() as ctx:
        def sb(name, shape, dt=F32):
            return ctx.enter_context(nc.sbuf_tensor(name, shape, dt))

        def psum(name, shape, dt=F32):
            return ctx.enter_context(nc.psum_tensor(name, shape, dt))

        def sem(name):
            return ctx.enter_context(nc.semaphore(name))

        table = [nc.dram_tensor(f"table{l}", [NB * P, D], F32, kind="Internal").ap() for l in range(4)]
        h_t_dram = [nc.dram_tensor(f"h_t{l}", [NB, P, D], F32, kind="Internal").ap() for l in range(4)]
        r3_dram = nc.dram_tensor("r3", [NI, P, MB * MW], F32, kind="Internal").ap()

        x_all = sb("x_all", [P, NB, D])
        acc = sb("acc", [P, 2, NCOL])
        w_all = sb("w_all", [P, 7, 2, D])
        rowc = sb("rowc", [P, len(ROWS), D])
        rel = sb("rel", [P, T])
        ew = sb("ew", [P, T])
        sh = sb("sh", [P, TPI, 4])
        base_i = sb("base_i", [1, NI * BPAD], I32)
        ident = sb("ident", [P, P])
        iota = sb("iota", [P, WIN])
        ones = sb("ones", [P, P])
        flag_i = sb("flag_i", [P, 1], I32)
        eps = sb("eps", [P, 1])
        zeros = sb("zeros", [P, 2, P])
        bias0 = sb("bias0", [P, D])
        we1 = sb("we1", [C + 1, D])
        wc = sb("wc", [P, 2, D])
        bc3 = sb("bc3", [3, D], BF16)
        ones3 = sb("ones3", [3, P], BF16)
        m1 = sb("m1", [2 * 16, P])
        m2 = sb("m2", [P, P])
        m3 = sb("m3", [P, P])
        m4 = sb("m4", [P, D])
        idx = sb("idx", [P, TPI], I32)
        rows = sb("rows", [P, TPI, D])
        hot = sb("hot", [P, TPI, WIN])
        arena = sb("arena", [P, 8 * 4 * WIN + 8 * 8 * C])
        raw = arena[0:C + 1, 0:TPI * P]
        r_t = arena[:, TPI * P:TPI * P + 2 * 2 * 512].rearrange("p (b c n) -> p b c n", b=2, c=2)
        hot4 = arena[:, 0:8 * 4 * WIN].rearrange("p (t k w) -> p t k w", t=8, k=4)
        u_ring = arena[:, 8 * 4 * WIN:].rearrange("p (t j c) -> p t j c", t=8, j=8)
        rbf = arena[0:32, 0:MB * MW]
        ra = arena[:, MB * MW:MB * MW + 2 * MW].rearrange("p (b n) -> p b n", b=2)
        rb = arena[:, (MB + 2) * MW:(MB + 4) * MW].rearrange("p (b n) -> p b n", b=2)
        rc = arena[:, (MB + 4) * MW:(2 * MB + 4) * MW].rearrange("p (b n) -> p b n", b=MB)
        r3 = sb("r3_sb", [P, MB * MW])
        h_t = sb("h_t_in", [P, 2, P])
        q_t = sb("q_t", [P, 2, P])
        y = sb("y", [P, D])
        y2 = sb("y2", [P, D])
        y_t = sb("y_t", [P, 2, P])
        h_new = sb("h_new", [P, D])
        h_new_t = sb("h_new_t", [P, 2, P])
        t_out = sb("t_out", [P, D])
        small = sb("small", [P, 32])
        poly = sb("poly", [P, 2, C])
        poly2 = sb("poly2", [P, 2, C])
        vv = sb("vv", [P, 2, C])
        o_sum = sb("o_sum", [P, D])
        o_sq = sb("o_sq", [P, D])
        fin = arena[:, 0:8 * D].rearrange("p (j d) -> p j d", d=D)
        wbase = sb("wbase", [P, 1])
        relw = sb("relw", [P, 4])

        def W(name):
            return w_all[:, PLACE[name], :, :]

        def R(name):
            return rowc[:, ROWS.index(name), :]

        ps_even = psum("ps_even", [P, 2, 2 * P])
        ps_odd = psum("ps_odd", [P, 2, 2 * P])
        ps_node = psum("ps_node", [P, 2, D])
        ps_tp = psum("ps_tp", [P, 4, P])
        ps_edge = psum("ps_edge", [P, 4, 512])

        def ps_acc(k):
            return (ps_odd if k % 2 else ps_even)[:, :, 0:WIN]

        ps_z = ps_edge[:, 2:4, 0:D]
        ps_tpw = ps_edge[:, :, 0:D]

        s_weights = sem("s_weights")
        s_scalars = sem("s_scalars")
        s_x = [sem(f"s_x{c}") for c in range(NB // CH)]
        s_const = sem("s_const")
        s_pre = sem("s_pre")
        s_prep_mm = sem("s_prep_mm")
        s_bc = sem("s_bc")
        s_flag_part = sem("s_flag_part")
        s_flag_all = sem("s_flag_all")
        s_flag = sem("s_flag")
        s_root = sem("s_root")
        s_scale = sem("s_scale")
        s_ph = sem("s_ph")
        s_ph_t = sem("s_ph_t")
        s_pht_copied = sem("s_pht_copied")
        s_pstore = sem("s_pstore")
        s_pstore_t = sem("s_pstore_t")
        idx_in = [sem("idx_in0"), sem("idx_in1")]
        rows_in = [sem(f"rows_in{k}") for k in range(NG)]
        hot_ready = sem("hot_ready")
        hot_part = sem("hot_part")
        summed = sem("summed")
        added = sem("added")
        relw_done = sem("relw_done")
        wbase_done = sem("wbase_done")
        rbf_in = [sem(f"rbf_in{m}") for m in range(MB)]
        mlp_mm = [sem(f"mlp_mm{s}") for s in range(3)]
        mlp_act = [sem(f"mlp_act{s}") for s in range(3)]
        r3_out = [sem(f"r3_out{m}") for m in range(MB)]
        r3_in = [sem(f"r3_in{m}") for m in range(MB)]
        raw_in = [sem(f"raw_in{k}") for k in range(NG)]
        a_done = sem("a_done")
        r_done = sem("r_done")
        z_done = sem("z_done")
        z_read = sem("z_read")
        msg_done = sem("msg_done")
        tpw_done = sem("tpw_done")
        u_done = sem("u_done")
        ht_in = sem("ht_in")
        q_ready = sem("q_ready")
        acc_free = sem("acc_free")
        n_mm = sem("n_mm")
        n_y = sem("n_y")
        n_lk = sem("n_lk")
        n_ss = sem("n_ss")
        n_root = sem("n_root")
        n_mx = sem("n_mx")
        n_rn = sem("n_rn")
        x_new = sem("x_new")
        t_bn = sem("t_bn")
        t_mv = sem("t_mv")
        t_root = sem("t_root")
        t_rstd = sem("t_rstd")
        t_scale = sem("t_scale")
        t_h = sem("t_h")
        t_tp = sem("t_tp")
        t_ht = sem("t_ht")
        t_tab = sem("t_tab")
        t_up = sem("t_up")
        table_out = sem("table_out")
        ht_out = sem("ht_out")
        g_bn = sem("g_bn")
        g_mv = sem("g_mv")
        g_root = sem("g_root")
        g_rstd = sem("g_rstd")
        g_scale = sem("g_scale")
        g_hn = sem("g_hn")
        g_lg = sem("g_lg")
        g_lb = sem("g_lb")
        g_tp = sem("g_tp")
        g_yt = sem("g_yt")
        g_mm2 = sem("g_mm2")
        g_x1 = sem("g_x1")
        o_a = sem("o_a")
        o_acopy = sem("o_acopy")
        o_step = sem("o_step")
        o_b = sem("o_b")
        o_tp = sem("o_tp")
        o_bt = sem("o_bt")
        o_mm = sem("o_mm")
        o_copied = sem("o_copied")
        o_sqd = sem("o_sqd")
        o_kept = sem("o_kept")
        o_summed = sem("o_summed")
        f_mm = sem("f_mm")
        f_step = sem("f_step")
        f_root = sem("f_root")
        f_out = sem("f_out")
        s_out = sem("s_out")

        def pass_waits(eng):
            eng.sem_inc(passed, 1)

        def last_use(t, ring, total):
            return t - ring if t >= ring else max(u for u in range(total) if u % ring == t % ring) - total

        def group_of(t):
            g = next(k for k, (t0, n) in enumerate(GROUPS) if t0 <= t % TPI < t0 + n)
            return g - (NG if t < 0 else 0)

        N_WEIGHT_LOADS = 9 + 8
        layer_its = [(l * NI, (l + 1) * NI) for l in range(4)]

        def sp_setup(sp):
            for c in range(NB // CH):
                sp.dma_start(x_all[:, c * CH:(c + 1) * CH, :],
                             io["x"][c * CH * P:(c + 1) * CH * P, :].rearrange("(b p) d -> p b d", p=P)).then_inc(s_x[c], 16)
            for dst, name in ((rel[:, :].bitcast(I32), "dst"), (ew[:, :], "ew"), (base_i[:, :], "base")):
                sp.dma_start(dst, io[name]).then_inc(s_scalars, 16)
            for n, name in enumerate(WEIGHTS[:9]):
                place = {"e2": w_e2, "le": w_le}[name] if name in ("e2", "le") else W(name)
                sp.dma_start(place, io["weights"][n, :, :].rearrange("(c p) d -> p c d", p=P)).then_inc(s_weights, 16)
            sp.dma_start(b12.rearrange("p r d -> p (r d)"), io["b12"].partition_broadcast(P)).then_inc(s_weights, 16)
            sp.dma_start(rowc[:, :, :].rearrange("p r d -> p (r d)"),
                         io["rowc"].partition_broadcast(P)).then_inc(s_weights, 16)
            for dst, name in ((we1[:, :], "we1"), (m1[:, :], "m1"), (m2[:, :], "m2"), (m3[:, :], "m3"), (m4[:, :], "m4"),
                              (be2, "be2")):
                sp.dma_start(dst, io[name]).then_inc(s_weights, 16)
            sp.wait_ge(s_pre, PRE["bc_lo"])
            for j in range(3):
                sp.dma_start(bc3[j:j + 1, :], bc_parts[0:1, j, :]).then_inc(s_bc, 16)
            sp.wait_ge(s_bc, 48)

        HALVES = ((0, 7, (0, 1)), (7, 10, (2, 3, 4)))

        def sp_indices(sp, half, i, landed):
            t0, n, groups = HALVES[half]
            if landed is not None:
                for k in groups:
                    sp.wait_ge(rows_in[k], landed * (16 * GROUPS[k][1]))
                    pass_waits(sp)
            sp.dma_start(idx[:, t0:t0 + n], io["src"][:, bass.ds(i * TPI + t0, n)]).then_inc(idx_in[half], 16)

        def sp_sh(sp, half, i, it, nw):
            t0, n, groups = HALVES[half]
            if it is not None:
                sp.wait_ge(hot_ready, (it * NG + groups[-1] + 1) * nw)
                pass_waits(sp)
            sp.dma_start(sh[:, t0:t0 + n, :], io["sh"][:, bass.ds(i * TPI + t0, n), :]).then_inc(sh_in[half], 16)

        def sp_edges(sp, l, it, i, more, nw):
            if l == 0:
                for m in range(MB):
                    sp.wait_ge(mlp_mm[0], it * MB + m + 1)
                    pass_waits(sp)
                    sp.dma_start(rbf[:, m * MW:(m + 1) * MW],
                                 io["rbf"][bass.ds(i, 1), :, m * MW:(m + 1) * MW].rearrange("a p n -> p (a n)")).then_inc(rbf_in[m], 16)
            if l == 2:
                for k, (t0, n) in enumerate(GROUPS):
                    sp.wait_ge(a_done, i * 2 * NG + 2 * k + 2)
                    pass_waits(sp)
                    sp.dma_start(raw[0:C, t0 * P:(t0 + n) * P],
                                 io["raw"][bass.ds(i, 1), :, t0 * P:(t0 + n) * P].rearrange("a p n -> p (a n)")).then_inc(raw_in[k], 16)
            if l == 3:
                for m in range(MB):
                    sp.wait_ge(tpw_done, i * TPI + min(6 * m + 6, TPI))
                    pass_waits(sp)
                    sp.dma_start(r3[:, m * MW:(m + 1) * MW],
                                 r3_dram[bass.ds(i, 1), :, m * MW:(m + 1) * MW].rearrange("a p n -> p (a n)")).then_inc(r3_in[m], 16)
            if more:
                for half in range(2):
                    sp_indices(sp, half, i + 1, it + 1)
                    if l == 3:
                        sp_sh(sp, half, i + 1, it, nw)

        def sp_layer(sp, l, nw):
            a, z = layer_its[l]
            if l == 0:
                sp.wait_ge(s_pstore_t, 16 * (NB // CH) + 16)
            if l == 1:
                sp.wait_ge(hot_ready, NI * NG * nw)
                sp.dma_start(ew[:, :], io["pol"]).then_inc(s_pol, 16)
            if l == 2:
                sp.wait_ge(table_out, 16 * 2 * NB + 16)
                for name in ("lin", "wb", "sc"):
                    sp.dma_start(W(name), io["weights"][WEIGHTS.index(name), :, :].rearrange("(c p) d -> p c d", p=P)).then_inc(s_w3, 16)
                for m in range(MB):
                    sp.wait_ge(r3_out[m], 16 * NI + 16)
            for half in range(2):
                sp_indices(sp, half, 0, a if l else None)
                if l == 3:
                    sp_sh(sp, half, 0, None, nw)
            with sp.Fori(a, z - 1) as it:
                sp_edges(sp, l, it, it - a, True, nw)
            sp_edges(sp, l, z - 1, z - 1 - a, False, nw)

        def pool_setup(pool):
            pool.memset(ident[:, :], 0.0).then_inc(s_const, 1)
            pool.iota(iota_i[:, :], [[1, WIN]], base=0, channel_multiplier=0).then_inc(s_const, 1)
            pool.memset(ones[:, :], 1.0).then_inc(s_const, 1)
            pool.memset(ones3[:, :], 1.0).then_inc(s_const, 1)
            pool.memset(eps[:, :], LN_EPS).then_inc(s_const, 1)
            pool.wait_ge(s_const, 5)
            pool.affine_select(out=ident[:, :], in_=ident[:, :], compare_op=ALU.not_equal, fill=1.0, base=0,
                               pattern=[[-1, P]], channel_multiplier=1).then_inc(s_const, 1)
            pool.tensor_copy(iota[:, :], iota_i[:, :]).then_inc(s_const, 1)
            pool.wait_ge(s_flag_part, 1)
            pool.partition_all_reduce(flag_f[:, 1:2], flag_f[:, 0:1], P, RMAX).then_inc(s_flag_all, 1)

        def pool_edges(pool, l, it, nw):
            for k, (t0, n) in enumerate(GROUPS):
                if k in (0, 2):
                    pool.wait_ge(idx_in[k // 2], it * 16 + 16)
                pool.wait_ge(summed, (it * NG + k + 1) * nw)
                pass_waits(pool)
                for t in range(t0, t0 + n):
                    pool.indirect_dma_start(rows[:, t, :], None, table[l],
                                            bass.IndirectOffsetOnAxis(ap=idx[:, t:t + 1], axis=0)).then_inc(rows_in[k], 16)

        def pool_layer(pool, l, nw):
            a, z = layer_its[l]
            if l == 0:
                pool.wait_ge(s_pstore, 16 * (NB // CH) + 16)
            else:
                pool.wait_ge(table_out, 16 * l * NB + 16)
            with pool.Fori(a, z) as it:
                pool_edges(pool, l, it, nw)

        def mm2(pe, out, lhs_t, w, start=True, stop=True):
            pe.matmul(out, lhs_t[:, 0, :], w[:, 0, :], start=start, stop=False)
            return pe.matmul(out, lhs_t[:, 1, :], w[:, 1, :], start=False, stop=stop)

        def pe_setup(pe):
            pe.wait_ge(s_weights, 16 * N_WEIGHT_LOADS)
            for c in range(2):
                for j in range(2):
                    mm = pe.matmul(ps_edge[:, c, 0:D], w_e2[:, j, c * P:(c + 1) * P], w_le[:, j, :],
                                   start=(j == 0), stop=(j == 1))
                mm.then_inc(s_prep_mm, 1)
            for j in range(2):
                mm = pe.matmul(ps_edge[0:1, 2, 0:D], be2[:, j:j + 1], w_le[:, j, :], start=(j == 0), stop=(j == 1))
            mm.then_inc(s_prep_mm, 1)
            pe.wait_ge(s_const, 7)
            pe.wait_ge(s_pre, PRE["base_f"])
            pe.matmul(ps_edge[:, 3, 0:NI * BPAD], ones[0:1, :], base_f[0:1, :], start=True, stop=True).then_inc(s_prep_mm, 1)
            pe.wait_ge(s_pre, PRE["early"])
            with pe.Fori(0, NB // CH) as c:
                for j in range(CH):
                    pe.wait_ge(s_ph, c * CH + j + 1)
                    pe.wait_ge(s_pht_copied, c * CH + last_use(j, 4, CH) + 1 + CH)
                    for d in range(2):
                        mm = pe.transpose(tp_of(j, d), rows[:, j, d * P:(d + 1) * P], ident[:, :])
                    mm.then_inc(s_ph_t, 1)

        def tp_of(j, d):
            return ps_edge[:, j % 4, d * P:(d + 1) * P]

        def pe_sum(pe, l, it, k, w, nw):
            t0, n = GROUPS[k]
            a = layer_its[l][0]
            if l < 2:
                pe.wait_ge(rows_in[k], (it + 1) * 16 * n)
            elif l == 2:
                pe.wait_ge(msg_done, (it - a) * NG + k + 1)
            else:
                pe.wait_ge(u_done, (it - a) * TPI + t0 + n + TPI)
            pe.wait_ge(hot_ready, (it * NG + k) * nw + (w + 1))
            if nw == 1:
                pe.wait_ge(added, it * NG + last_use(k, 2, NG) + 1 + NG)
            else:
                pe.wait_ge(added, (it * NG + k) * nw + w + NG * nw)
            out = ps_acc(k)
            for t in range(t0, t0 + n):
                first, last = t == t0, t == t0 + n - 1
                if l < 3:
                    for c in range(2):
                        mm = pe.matmul(out[:, c, :], rows[:, t, c * P:(c + 1) * P], hot[:, t, :],
                                       start=(first and c == 0), stop=last, skip_group_check=True)
                else:
                    u = u_ring[:, t % 8, :, :]
                    s = hot4[:, t % 8, :, :]
                    pe.matmul(out[:, 0, :], u[:, 0:2, :], s[:, 0, :], start=first, stop=False, skip_group_check=True)
                    pe.matmul(out[:, 1, :], u[:, 2:4, :], s[:, 0, :], start=False, stop=False, skip_group_check=True)
                    pe.matmul(out[0:C, 0, :], u[:, 4, :], s[:, 1, :], start=False, stop=False, skip_group_check=True)
                    pe.matmul(out[C:P, 0, :], u[:, 7, :], s[:, 1, :], start=False, stop=False, skip_group_check=True)
                    pe.matmul(out[0:C, 0, :], u[:, 5, :], s[:, 2, :], start=False, stop=False, skip_group_check=True)
                    pe.matmul(out[0:C, 1, :], u[:, 7, :], s[:, 2, :], start=False, stop=False, skip_group_check=True)
                    pe.matmul(out[0:C, 0, :], u[:, 6, :], s[:, 3, :], start=False, stop=last, skip_group_check=True)
                    mm = pe.matmul(out[C:P, 1, :], u[:, 7, :], s[:, 3, :], start=False, stop=last, skip_group_check=True)
            mm.then_inc(summed, 1)

        def pe_mlp(pe, it, stage, m):
            if stage == 0:
                pe.wait_ge(rbf_in[m], it * 16 + 16)
                src, w = rbf[:, m * MW:(m + 1) * MW], m1
            else:
                pe.wait_ge(mlp_act[stage - 1], it * MB + m + 1)
                src, w = (ra, rb)[stage - 1][:, m % 2, :], (m2, m3)[stage - 1]
            if stage == 0:
                pe.wait_ge(mlp_act[2], it * MB + (3, 2, MB + 1)[m])
            pe.matmul(ps_edge[:, m % 2, 0:MW], w[:, :], src, start=True, stop=True).then_inc(mlp_mm[stage], 1)

        def pe_a(pe, i, k):
            t0, n = GROUPS[k]
            pe.wait_ge(raw_in[k], i * 16 + 16)
            for c in range(2):
                pe.wait_ge(r_done, (i * NG + k) * 2 + c + 1)
                pe.matmul(ps_edge[:, c, 0:n * P], we1[:, c * P:(c + 1) * P], raw[:, t0 * P:(t0 + n) * P],
                          start=True, stop=True).then_inc(a_done, 1)

        def pe_z(pe, i, k):
            t0, n = GROUPS[k]
            pe.wait_ge(r_done, (i * NG + k) * 2 + 2 + 2)
            for t in range(t0, t0 + n):
                pe.wait_ge(z_read, i * TPI + last_use(t, 2, TPI) + 1 + TPI)
                z = ps_z[:, t % 2, :]
                pe.matmul(z, ones3[:, :], bc3[:, :], start=True, stop=False)
                for c in range(2):
                    mm = pe.matmul(z, r_t[:, k % 2, c, (t - t0) * P:(t - t0 + 1) * P], wc[:, c, :],
                                   start=False, stop=(c == 1))
                mm.then_inc(z_done, 1)

        def pe_tpw(pe, i, k):
            t0, n = GROUPS[k]
            for t in range(t0, t0 + n):
                if t in (0, 6, 12):
                    pe.wait_ge(r3_in[t // 6], i * 16 + 16)
                pe.wait_ge(u_done, i * TPI + last_use(t, 4, TPI) + 1 + TPI)
                q = C * (t % 2)
                pe.matmul(ps_tpw[:, t % 4, :], r3[q:q + C, (t // 2) * P:(t // 2 + 1) * P], m4[q:q + C, :],
                          start=True, stop=True).then_inc(tpw_done, 1)

        def pe_node_a(pe, l, b):
            n = b + (l * NB + 1)
            pe.wait_ge(q_ready, n)
            pe.wait_ge(ht_in, n * 16)
            out = ps_node[:, 0, :]
            if l < 3:
                pe.wait_ge(x_new, n)
            if l < 2:
                mm2(pe, out, h_t, W(f"l{l}_w1"), stop=False)
                mm2(pe, out, q_t, W(f"l{l}_w2"), start=False).then_inc(n_mm, 1)
            elif l == 2:
                pe.wait_ge(t_up, b + 1)
                mm2(pe, out, q_t, W("g1")).then_inc(n_mm, 1)
            else:
                pe.wait_ge(o_acopy, b + 1)
                pe.wait_ge(o_kept, b + 1)
                for c in range(2):
                    mm = pe.matmul(ps_node[:, 0, c * P:(c + 1) * P], q_t[:, c, :], W("lin")[:, c, c * P:(c + 1) * P],
                                   start=True, stop=True)
                mm.then_inc(n_mm, 1)

        def pe_transpose(pe, out, src):
            for c in range(2):
                mm = pe.transpose(out[:, c, :], src[:, c * P:(c + 1) * P], ident[:, :])
            return mm

        def pe_node_b(pe, l, b):
            if l == 2:
                pe.wait_ge(g_lb, b + 1)
                pe.wait_ge(g_yt, b + 1)
                pe_transpose(pe, ps_tp[:, 2:4, :], y2).then_inc(g_tp, 1)
                pe.wait_ge(g_yt, b + 2)
                pe.wait_ge(g_x1, b + 1)
                mm2(pe, ps_node[:, 1, :], y_t, W("g2")).then_inc(g_mm2, 1)
            if l == 3:
                pe.wait_ge(o_b, b + 1)
                pe.wait_ge(o_bt, b + 1)
                pe_transpose(pe, ps_tp[:, 2:4, :], y2).then_inc(o_tp, 1)
                pe.wait_ge(o_bt, b + 2)
                pe.wait_ge(o_kept, b + 1)
                mm2(pe, ps_node[:, 1, :], h_t, W("sc"), stop=False)
                mm2(pe, ps_node[:, 1, :], y_t, W("wb"), start=False).then_inc(o_mm, 1)

        def pe_node_c(pe, l, b):
            n = b + (l * NB + 1)
            if l < 3:
                pe.wait_ge(t_h, n)
                pe.wait_ge(t_ht, n)
                pe_transpose(pe, ps_tp[:, 0:2, :], h_new).then_inc(t_tp, 1)
            if l == 2:
                pe.wait_ge(t_ht, n + 1)
                mm2(pe, ps_node[:, 0, :], h_new_t, W("up")).then_inc(t_tab, 1)

        def pe_edges(pe, l, it, nw, b):
            i = it - layer_its[l][0]

            def node(k):
                if b is not None:
                    if k == 3:
                        pe_node_a(pe, l, b)
                    if k == 4:
                        pe_node_b(pe, l, b)

            if nw > 1:
                for k in range(NG):
                    if l == 0:
                        for stage, m in MLP_AT[k]:
                            pe_mlp(pe, it, stage, m)
                    if l == 2:
                        pe_a(pe, i, k)
                        pe_z(pe, i, k)
                    if l == 3:
                        pe_tpw(pe, i, k)
                    with pe.Fori(0, nw) as w:
                        pe_sum(pe, l, it, k, w, nw)
                return
            if l == 2:
                pe_a(pe, i, 0)
            for k in range(NG):
                if l == 0:
                    for stage, m in MLP_AT[k]:
                        pe_mlp(pe, it, stage, m)
                if l == 2:
                    if k + 1 < NG:
                        pe_a(pe, i, k + 1)
                    pe_z(pe, i, k)
                if l == 3:
                    pe_tpw(pe, i, k)
                if l < 2:
                    pe_sum(pe, l, it, k, 0, 1)
                elif k:
                    pe_sum(pe, l, it, k - 1, 0, 1)
                node(k)
            if l >= 2:
                pe_sum(pe, l, it, NG - 1, 0, 1)
            if b is not None:
                pe_node_c(pe, l, b)

        def run_layer(eng, l, nw, edges, node_parts, before=None):
            a, z = layer_its[l]
            if nw == 1:
                edges(eng, l, a, nw, None)
                with eng.Fori(a + 1, z) as it:
                    edges(eng, l, it, nw, it - (a + 1))
                for part in node_parts:
                    part(eng, l, NB - 1)
            else:
                with eng.Fori(a, z) as it:
                    edges(eng, l, it, nw, None)
                with eng.Fori(0, NB - 1) as b:
                    for part in node_parts:
                        part(eng, l, b)
                for part in node_parts:
                    part(eng, l, NB - 1)

        def pe_final(pe):
            pe.wait_ge(o_summed, 2 * NB + 2)
            pe.matmul(ps_edge[:, 0, 0:D], ones[:, :], o_sum[:, :], start=True, stop=True)
            pe.matmul(ps_edge[:, 1, 0:D], ones[:, :], o_sq[:, :], start=True, stop=True).then_inc(f_mm, 1)
            pe.wait_ge(f_step, FIN["var_part"])
            pe.matmul(ps_edge[:, 2, 0:C], ones[:, :], fin[:, 2, 0:C], start=True, stop=True).then_inc(f_mm, 1)

        def ve_setup(ve):
            steps = []

            def step(name, ins):
                steps.append(name)
                assert PRE[name] == len(steps)
                ins.then_inc(s_pre, 1)

            step("o_sum", ve.memset(o_sum[:, :], 0.0))
            step("o_sq", ve.memset(o_sq[:, :], 0.0))
            step("zeros", ve.memset(zeros[:, :, :], 0.0))
            step("base0", ve.memset(base_f, 0.0))
            step("acc0", ve.memset(acc[:, :, :], 0.0))
            ve.wait_ge(s_scalars, 16 * 3)
            step("dst_f", ve.tensor_copy(rel[:, :], rel[:, :].bitcast(I32)))
            ve.wait_ge(s_pre, PRE["dst_f"])
            step("base_f", ve.tensor_copy(base_f[0:1, :], base_i[:, :]))
            ve.wait_ge(s_weights, 16 * N_WEIGHT_LOADS)
            step("m4", ve.tensor_scalar(m4[:, 3 * C:4 * C], m4[:, 3 * C:4 * C], float(1.0 / np.sqrt(np.float32(3.0))), None, ALU.mult))
            step("bias0", ve.tensor_tensor(bias0[:, :], b12[:, 0, :], b12[:, 1, :], ALU.add))
            ve.wait_ge(s_prep_mm, 2)
            step("wc", ve.tensor_copy(wc[:, :, :], ps_edge[:, 0:2, 0:D]))
            ve.wait_ge(s_prep_mm, 3)
            bc = ps_edge[0:1, 2, 0:D]
            step("bc_hi", ve.tensor_copy(bc_parts[0:1, 0, :], bc))
            ve.wait_ge(s_pre, PRE["bc_hi"])
            step("bc_r1", ve.tensor_tensor(bc_rest[0:1, 0, :], bc, bc_parts[0:1, 0, :], ALU.subtract))
            ve.wait_ge(s_pre, PRE["bc_r1"])
            step("bc_mid", ve.tensor_copy(bc_parts[0:1, 1, :], bc_rest[0:1, 0, :]))
            ve.wait_ge(s_pre, PRE["bc_mid"])
            step("bc_r2", ve.tensor_tensor(bc_rest[0:1, 1, :], bc_rest[0:1, 0, :], bc_parts[0:1, 1, :], ALU.subtract))
            ve.wait_ge(s_pre, PRE["bc_r2"])
            step("bc_lo", ve.tensor_copy(bc_parts[0:1, 2, :], bc_rest[0:1, 1, :]))
            ve.wait_ge(s_prep_mm, 4)
            bases = ps_edge[:, 3, 0:NI * BPAD].rearrange("p (i g) -> p i g", g=BPAD)
            for k, (t0, n) in enumerate(GROUPS):
                step(f"rel{k}", ve.tensor_tensor(
                    rel[:, :].rearrange("p (i t) -> p i t", t=TPI)[:, :, t0:t0 + n],
                    rel[:, :].rearrange("p (i t) -> p i t", t=TPI)[:, :, t0:t0 + n],
                    bases[:, :, k:k + 1].broadcast_to([P, NI, n]), ALU.subtract))
            ve.wait_ge(s_pre, PRE[f"rel{NG - 1}"])
            step("rel_max", ve.tensor_reduce(fl[:, 0:1], rel[:, :], AX_X, ALU.max))
            step("rel_min", ve.tensor_reduce(fl[:, 1:2], rel[:, :], AX_X, ALU.min))
            ve.wait_ge(s_pre, PRE["rel_min"])
            step("over", ve.tensor_scalar(fl[:, 2:3], fl[:, 0:1], float(1 - WIN), None, ALU.add))
            step("under", ve.tensor_scalar(fl[:, 3:4], fl[:, 1:2], -1.0, None, ALU.mult))
            step("early", ve.tensor_tensor(early, early, ps_edge[:, 3, 0:NI * BPAD], ALU.subtract))
            ve.wait_ge(s_pre, PRE["early"])
            step("early_max", ve.tensor_reduce(fl[:, 4:5], early, AX_X, ALU.max))
            ve.wait_ge(s_pre, PRE["early_max"])
            ve.tensor_reduce(flag_f[:, 0:1], fl[:, 2:5], AX_X, ALU.max).then_inc(s_flag_part, 1)
            for c in range(NB // CH):
                ve.wait_ge(s_x[c], 16)
            with ve.Fori(0, NB // CH) as c:
                ve.wait_ge(t_mv, c + 1)
                for j in range(CH):
                    pass_waits(ve)
                    ve.bn_stats(bn_c[:, j, :], x_all[:, bass.ds(c * CH + j, 1), :].rearrange("p a d -> p (a d)")).then_inc(bn_part, 1)
                ve.wait_ge(bn_part, (c + 1) * CH)
                pass_waits(ve)
                for j in range(CH):
                    ve.bn_aggr(mv_c[:, j, :], bn_c[:, j, :]).then_inc(mv_part, 1)
                ve.wait_ge(mv_part, (c + 1) * CH)
                pass_waits(ve)
                ve.tensor_copy(mv_all[:, bass.ds(c * CH, CH), :], mv_c[:, :, :]).then_inc(t_mv, 1)
            ve.wait_ge(s_root, 1)
            ve.reciprocal(stats_all[:, 1, :], stats_all[:, 0, :]).then_inc(s_scale, 1)
            ve.wait_ge(s_scale, 1)
            ve.scalar_tensor_tensor(out=stats_all[:, 2, :], in0=mv_all[:, :, 0], scalar=-1.0, in1=stats_all[:, 1, :],
                                    op0=ALU.mult, op1=ALU.mult).then_inc(s_scale, 1)
            with ve.Fori(0, NB // CH) as c:
                for j in range(CH):
                    ve.wait_ge(s_ph_t, c * CH + j + 1 + CH)
                    if j == 0:
                        ve.wait_ge(s_pstore_t, c * 16 + 16)
                    ve.tensor_copy(pt[:, j, :], tp_both(j)).then_inc(s_pht_copied, 1)
            ve.wait_ge(s_flag_all, 1)
            ve.tensor_copy(flag_i[:, :], flag_f[:, 1:2]).then_inc(s_flag, 1)

        def tp_both(j):
            return ps_edge[:, j % 4, 0:D]

        def ve_hot(ve, l, it, k, w, nw):
            t0, n = GROUPS[k]
            i = it - layer_its[l][0]
            if nw == 1:
                users = [k - NG] + [group_of(last_use(t, 8, TPI)) for t in range(t0, t0 + n) if l == 3]
                ve.wait_ge(summed, it * NG + (max(users) + 1 + NG))
                where = rel[:, bass.ds(i * TPI + t0, n)]
            else:
                g = (it * NG + k) * nw + w
                ve.wait_ge(summed, g + NG * nw)
                ve.wait_ge(wbase_done, g + (it * NG + k) + 2)
                ve.tensor_scalar(relw[:, 0:n], rel[:, bass.ds(i * TPI + t0, n)], wbase[:, 0:1], None,
                                 ALU.subtract).then_inc(relw_done, 1)
                ve.wait_ge(relw_done, g + 1)
                ve.tensor_scalar(wbase[:, :], wbase[:, :], float(WIN), None, ALU.add).then_inc(wbase_done, 1)
                where = relw[:, 0:n]
            ready = hot_ready if l in (1, 2) else hot_part
            ve.tensor_tensor(hot[:, t0:t0 + n, :], iota[:, :].unsqueeze(1).broadcast_to([P, n, WIN]),
                             where.unsqueeze(2).broadcast_to([P, n, WIN]), ALU.is_equal).then_inc(ready, 1)
            q = i * NG + k + (0 if l == 0 else NI * NG)
            part = q * nw + (w + 1)
            if l == 0:
                ve.wait_ge(hot_part, part)
                ve.tensor_tensor(hot[:, t0:t0 + n, :], hot[:, t0:t0 + n, :],
                                 ew[:, bass.ds(i * TPI + t0, n)].unsqueeze(2).broadcast_to([P, n, WIN]),
                                 ALU.mult).then_inc(hot_ready, 1)
            if l == 3:
                ve.wait_ge(sh_in[0 if k < 2 else 1], i * 16 + 16)
                ve.wait_ge(hot_part, part)
                for t in range(t0, t0 + n):
                    ins = ve.tensor_tensor(hot4[:, t % 8, :, :], hot[:, t:t + 1, :].broadcast_to([P, 4, WIN]),
                                           sh[:, t, :].unsqueeze(2).broadcast_to([P, 4, WIN]), ALU.mult)
                ins.then_inc(hot_ready, 1)

        def ve_add(ve, l, it, k, w, nw, start):
            if nw == 1:
                g = it * NG + k
                ve.wait_ge(summed, g + 1 + NG)
                ve.wait_ge(added, g + NG)
            else:
                g = (it * NG + k) * nw + w
                ve.wait_ge(summed, g + 1 + NG * nw)
                ve.wait_ge(added, g + NG * nw)
            ve.tensor_tensor(acc[:, :, bass.ds(start, WIN)], acc[:, :, bass.ds(start, WIN)], ps_acc(k),
                             ALU.add).then_inc(added, 1)

        def ve_msg(ve, i, it, k):
            t0, n = GROUPS[k]
            ve.wait_ge(rows_in[k], (it + 1) * 16 * n)
            for t in range(t0, t0 + n):
                ve.wait_ge(z_done, i * TPI + t + 1 + TPI)
                ve.scalar_tensor_tensor(out=rows[:, t, :], in0=ps_z[:, t % 2, :], scalar=ew[:, bass.ds(i * TPI + t, 1)],
                                        in1=rows[:, t, :], op0=ALU.mult, op1=ALU.add).then_inc(z_read, 1)

        def ve_u(ve, i, it, k, nw):
            t0, n = GROUPS[k]
            ve.wait_ge(rows_in[k], (it + 1) * 16 * n)
            for t in range(t0, t0 + n):
                ve.wait_ge(summed, (it * NG + group_of(last_use(t, 8, TPI)) + 1 + NG) * nw)
                ve.wait_ge(tpw_done, i * TPI + t + 1 + TPI)
                tp = ps_tpw[:, t % 4, :].rearrange("p (k c) -> p k c", k=4)
                x = rows[:, t, :].rearrange("p (k c) -> p k c", k=4)
                u = u_ring[:, t % 8, :, :]
                ve.tensor_tensor(u[:, 0:8:7, :], tp[:, 0:2, :], x[:, 0:1, :].broadcast_to([P, 2, C]), ALU.mult)
                ve.tensor_tensor(u[:, 1:7, :].rearrange("p (k x) c -> p k x c", k=2),
                                 tp[:, 2:4, :].unsqueeze(2).broadcast_to([P, 2, 3, C]),
                                 x[:, 1:4, :].unsqueeze(1).broadcast_to([P, 2, 3, C]), ALU.mult).then_inc(u_done, 1)

        def ve_node_a(ve, l, b):
            n = b + (l * NB + 1)
            cols = acc[:, :, bass.ds(b * P, P)]
            ve.wait_ge(ht_in, n * 16)
            ve.wait_ge(n_mm, n)
            pass_waits(ve)
            if l == 0:
                ins = ve.scalar_tensor_tensor(out=q_t[:, :, :], in0=h_t[:, :, :], scalar=1.0, in1=cols, op0=ALU.add, op1=ALU.mult)
            elif l == 2:
                ins = ve.tensor_tensor(q_t[:, :, :], h_t[:, :, :], cols, ALU.add)
            else:
                ins = ve.tensor_copy(q_t[:, :, :], cols)
            ins.then_inc(q_ready, 1)
            if l < 3:
                ve.wait_ge(q_ready, n)
                pass_waits(ve)
                ve.tensor_copy(cols, zeros[:, :, :]).then_inc(acc_free, 1)

        def ve_tail(ve, l, b):
            n = b + (l * NB + 1)
            xb = x_all[:, bass.ds(b, 1), :].rearrange("p a d -> p (a d)")
            ve.wait_ge(x_new, n + 1)
            pass_waits(ve)
            ve.bn_stats(small[:, 8:14], xb).then_inc(t_bn, 1)
            ve.wait_ge(t_bn, n)
            pass_waits(ve)
            ve.bn_aggr(small[:, 14:16], small[:, 8:14]).then_inc(t_mv, 1)
            ve.wait_ge(t_root, n)
            ve.reciprocal(small[:, 17:18], small[:, 16:17]).then_inc(t_rstd, 1)
            ve.wait_ge(t_rstd, n)
            ve.scalar_tensor_tensor(out=small[:, 18:19], in0=small[:, 14:15], scalar=-1.0, in1=small[:, 17:18],
                                    op0=ALU.mult, op1=ALU.mult).then_inc(t_scale, 1)
            if l == 1:
                ve.wait_ge(t_h, n)
                ve.wait_ge(table_out, n * 16)
                ve.tensor_tensor(t_out[:, :], h_new[:, :], R("b_le"), ALU.add).then_inc(t_lb, 1)

        t_lb = sem("t_lb")

        def ve_node_b(ve, l, b):
            n = b + (l * NB + 1)
            xb = x_all[:, bass.ds(b, 1), :].rearrange("p a d -> p (a d)")
            no = ps_node[:, 0, :]
            ve.wait_ge(n_mm, n + 1)
            if l == 0:
                ve.tensor_tensor(y[:, :], no, bias0[:, :], ALU.add).then_inc(n_y, 1)
                ve.wait_ge(n_y, b + 1)
                ve.scalar_tensor_tensor(out=y2[:, :], in0=y[:, :], scalar=LEAKY, in1=y[:, :], op0=ALU.mult,
                                        op1=ALU.max).then_inc(n_lk, 1)
                ve.wait_ge(n_root, b + 1)
                ve.tensor_scalar(small[:, 22:23], small[:, 21:22], NORM_EPS, None, ALU.max).then_inc(n_mx, 1)
                ve.wait_ge(n_mx, b + 1)
                ve.reciprocal(small[:, 23:24], small[:, 22:23]).then_inc(n_rn, 1)
                ve.wait_ge(n_rn, b + 1)
                ve.scalar_tensor_tensor(out=xb, in0=y2[:, :], scalar=small[:, 23:24], in1=xb, op0=ALU.mult,
                                        op1=ALU.add).then_inc(x_new, 1)
            if l == 1:
                ve.scalar_tensor_tensor(out=xb, in0=no, scalar=0.0, in1=xb, op0=ALU.max, op1=ALU.add).then_inc(x_new, 1)
            if l == 2:
                ve.tensor_tensor(y[:, :], no, R("b_g1"), ALU.add).then_inc(g_y, 1)
                ve.wait_ge(g_y, b + 1)
                ve.bn_stats(small[:, 8:14], y[:, :]).then_inc(g_bn, 1)
                ve.wait_ge(g_bn, b + 1)
                pass_waits(ve)
                ve.bn_aggr(small[:, 24:26], small[:, 8:14]).then_inc(g_mv, 1)
                ve.wait_ge(g_root, b + 1)
                ve.reciprocal(small[:, 27:28], small[:, 26:27]).then_inc(g_rstd, 1)
                ve.wait_ge(g_rstd, b + 1)
                ve.tensor_scalar(y[:, :], y[:, :], small[:, 24:25], small[:, 27:28], ALU.subtract, ALU.mult).then_inc(g_hn, 1)
                ve.wait_ge(g_hn, b + 1)
                ve.tensor_tensor(y[:, :], y[:, :], R("ln_g"), ALU.mult).then_inc(g_lg, 1)
                ve.wait_ge(g_lg, b + 1)
                ve.tensor_tensor(y2[:, :], y[:, :], R("ln_b"), ALU.add).then_inc(g_lb, 1)
                ve.wait_ge(g_mm2, b + 1)
                ve.tensor_tensor(y[:, :], ps_node[:, 1, :], R("b_g2"), ALU.add).then_inc(g_x1, 1)
                ve.wait_ge(g_x1, b + 2)
                ve.tensor_tensor(xb, xb, y[:, :], ALU.add).then_inc(x_new, 1)
            if l == 3:
                ve_node_poly(ve, b)

        g_y = sem("g_y")

        def ve_node_poly(ve, b):
            count = [0]

            def step(ins):
                count[0] += 1
                ins.then_inc(o_step, 1)
                ve.wait_ge(o_step, b * POLY + count[0])

            a0 = y[:, 0:C]
            a0b = a0.unsqueeze(1).broadcast_to([P, 2, C])
            a1 = y[:, C:D].rearrange("p (x c) -> p x c", x=3)
            pairs = [R(n).rearrange("p (j c) -> p j c", c=C) for n in ("wc0a", "wc0b", "wc1")]
            c3, c1 = pairs[0][:, 0:2, :], pairs[0][:, 2:4, :]
            c0, cv = pairs[1][:, 0:2, :], pairs[1][:, 2:4, :]
            w2 = pairs[2][:, 0, :]
            ve.wait_ge(o_acopy, b + 2)
            sq = y2[:, C:D].rearrange("p (x c) -> p x c", x=3)
            ve.wait_ge(o_tp, b + 1)
            step(ve.tensor_tensor(sq, a1, a1, ALU.mult))
            step(ve.tensor_tensor(vv[:, 1, :], sq[:, 0, :], sq[:, 1, :], ALU.add))
            step(ve.tensor_tensor(vv[:, 0, :], vv[:, 1, :], sq[:, 2, :], ALU.add))
            step(ve.tensor_tensor(poly[:, :, :], c3, a0b, ALU.mult))
            step(ve.tensor_tensor(poly[:, :, :], poly[:, :, :], c1, ALU.add))
            step(ve.tensor_tensor(poly[:, :, :], poly[:, :, :], a0b, ALU.mult))
            step(ve.tensor_tensor(poly[:, :, :], poly[:, :, :], c0, ALU.add))
            step(ve.tensor_tensor(poly2[:, :, :], cv, vv[:, 0:1, :].broadcast_to([P, 2, C]), ALU.mult))
            step(ve.tensor_tensor(poly[:, :, :], poly[:, :, :], poly2[:, :, :], ALU.add))
            step(ve.tensor_tensor(poly2[:, 0, :], poly[:, 0, :], a0, ALU.mult))
            step(ve.tensor_tensor(poly2[:, 1, :], w2, vv[:, 0, :], ALU.mult))
            step(ve.tensor_tensor(y2[:, 0:C], poly2[:, 0, :], poly2[:, 1, :], ALU.add))
            ve.tensor_tensor(sq, a1, poly[:, 1:2, :].broadcast_to([P, 3, C]), ALU.mult).then_inc(o_b, 1)

        def ve_node_c(ve, l, b):
            if l < 3:
                ve_tail(ve, l, b)
            else:
                m = LAST if isinstance(b, int) else P
                ve.wait_ge(o_copied, b + 1)
                ve.wait_ge(o_summed, (b + 1) * 2)
                ve.tensor_tensor(o_sum[0:m, :], o_sum[0:m, :], t_out[0:m, :], ALU.add).then_inc(o_summed, 1)
                ve.wait_ge(o_sqd, b + 1)
                ve.tensor_tensor(o_sq[0:m, :], o_sq[0:m, :], h_new[0:m, :], ALU.add).then_inc(o_summed, 1)

        def ve_edges(ve, l, it, nw, b):
            i = it - layer_its[l][0]
            if nw > 1:
                for k in range(NG):
                    if l == 2:
                        ve_msg(ve, i, it, k)
                    if l == 3:
                        ve_u(ve, i, it, k, nw)
                    g = it * NG + k
                    ve.wait_ge(wbase_done, g * (nw + 1) + 1)
                    ve.memset(wbase[:, :], 0.0).then_inc(wbase_done, 1)
                    with ve.Fori(0, nw) as w:
                        ve_hot(ve, l, it, k, w, nw)
                        ve_add(ve, l, it, k, w, nw, w * WIN)
                return
            regs = ve_base_regs
            ve.reg_load(regs[0:4], base_i[0:1, bass.ds(i * BPAD, 4)])
            ve.reg_load(regs[4:5], base_i[0:1, bass.ds(i * BPAD + 4, 1)])
            starts = [ve.snap(r, min_val=0, max_val=NCOL - WIN) for r in regs]
            if l < 3:
                ve_hot(ve, l, it, 0, 0, 1)
            for k in range(NG):
                if l < 3 and k + 1 < NG:
                    ve_hot(ve, l, it, k + 1, 0, 1)
                if l == 2:
                    ve_msg(ve, i, it, k)
                if l == 3:
                    ve_u(ve, i, it, k, 1)
                    ve_hot(ve, l, it, k, 0, 1)
                if k:
                    ve_add(ve, l, it, k - 1, 0, 1, starts[k - 1])
                if b is not None:
                    if k == NODE_AT:
                        ve.wait_ge(added, it * NG + k + NG)
                        ve_node_a(ve, l, b)
                    if k == 4:
                        ve_node_b(ve, l, b)
            ve_add(ve, l, it, NG - 1, 0, 1, starts[NG - 1])
            if b is not None:
                ve_node_c(ve, l, b)

        def ve_final(ve):
            o4 = acc[:, :, 0:NB * P].rearrange("p h (b c) -> p b h c", c=P)
            o0 = o4[:, :, 0, 0:C]
            done = []

            def step(name, ins):
                done.append(name)
                assert FIN[name] == len(done)
                ins.then_inc(f_step, 1)
                ve.wait_ge(f_step, len(done))

            inv_n = float(np.float32(1.0) / np.float32(n_nodes))
            mu, a0, b0, s1 = fin[:, 0, 0:C], fin[:, 1, 0:C], fin[:, 1, C:2 * C], fin[:, 3, 0:C]
            gam0, bet0, gam1 = R("norm")[:, 0:C], R("norm")[:, C:2 * C], R("norm")[:, 2 * C:3 * C]
            ve.wait_ge(o_kept, NB + 1)
            ve.wait_ge(f_mm, 1)
            step("mu", ve.tensor_scalar(mu, ps_edge[:, 0, 0:C], inv_n, None, ALU.mult))
            step("centre", ve.tensor_tensor(o0, o0, mu.unsqueeze(1).broadcast_to([P, NB, C]), ALU.subtract))
            sq = rows[:, 0:-(-NB * C // D), :].rearrange("p t d -> p (t d)")[:, 0:NB * C].rearrange("p (b c) -> p b c", c=C)
            step("square", ve.tensor_tensor(sq, o0, o0, ALU.mult))
            step("var_sum", ve.tensor_reduce(fin[:, 2, 0:C], sq[:, 0:NB - 1, :].rearrange("p b c -> p c b"), AX_X, ALU.add))
            step("var_part", ve.tensor_tensor(fin[0:LAST, 2, 0:C], fin[0:LAST, 2, 0:C], sq[0:LAST, NB - 1, :], ALU.add))
            step("nrm", ve.tensor_reduce(fin[:, 4, C:2 * C], ps_edge[:, 1, C:D].rearrange("p (c x) -> p c x", x=3), AX_X, ALU.add))
            step("nrm_mean", ve.tensor_scalar(fin[:, 4, C:2 * C], fin[:, 4, C:2 * C], float(1.0 / (3.0 * n_nodes)), None, ALU.mult))
            ve.wait_ge(f_mm, 2)
            step("var_mean", ve.tensor_scalar(fin[:, 4, 0:C], ps_edge[:, 2, 0:C], inv_n, None, ALU.mult))
            ve.wait_ge(f_root, 1)
            step("rstd", ve.reciprocal(fin[:, 6, 0:2 * C], fin[:, 5, 0:2 * C]))
            step("a0", ve.tensor_tensor(a0, fin[:, 6, 0:C], gam0, ALU.mult))
            step("s1", ve.tensor_tensor(s1, fin[:, 6, C:2 * C], gam1, ALU.mult))
            step("n0", ve.tensor_tensor(o0, o0, a0.unsqueeze(1).broadcast_to([P, NB, C]), ALU.mult))
            step("x0", ve.tensor_tensor(x_all[:, :, 0:C], x_all[:, :, 0:C], o0, ALU.add))
            step("x0b", ve.tensor_tensor(x_all[:, :, 0:C], x_all[:, :, 0:C], bet0.unsqueeze(1).broadcast_to([P, NB, C]), ALU.add))
            step("s1x", ve.tensor_copy(fin[:, 7, 0:3 * C].rearrange("p (c x) -> p c x", x=3), s1.unsqueeze(2).broadcast_to([P, C, 3])))
            o1a, o1b = o4[:, :, 0, C:P], o4[:, :, 1, :]
            sa, sb_ = fin[:, 7, 0:C], fin[:, 7, C:3 * C]
            step("n1a", ve.tensor_tensor(o1a, o1a, sa.unsqueeze(1).broadcast_to([P, NB, C]), ALU.mult))
            step("n1b", ve.tensor_tensor(o1b, o1b, sb_.unsqueeze(1).broadcast_to([P, NB, P]), ALU.mult))
            step("x1a", ve.tensor_tensor(x_all[:, :, C:P], x_all[:, :, C:P], o1a, ALU.add))
            step("x1b", ve.tensor_tensor(x_all[:, :, P:D], x_all[:, :, P:D], o1b, ALU.add))

        def act_setup(act):
            act.wait_ge(s_const, 7)
            act.wait_ge(t_mv, NB // CH + 1)
            act.activation(stats_all[:, 0, :], mv_all[:, :, 1], ACT.Sqrt, bias=eps[:, 0:1]).then_inc(s_root, 1)
            act.wait_ge(s_scale, 2)
            with act.Fori(0, NB // CH) as c:
                act.wait_ge(s_pstore, c * 16 + 16)
                act.wait_ge(s_ph_t, c * CH + CH)
                for j in range(CH):
                    b = c * CH + j
                    act.activation(rows[:, j, :], x_all[:, bass.ds(b, 1), :].rearrange("p a d -> p (a d)"), ACT.Relu,
                                   bias=stats_all[:, 2, bass.ds(b, 1)], scale=stats_all[:, 1, bass.ds(b, 1)]).then_inc(s_ph, 1)
                act.wait_ge(s_ph, c * CH + CH)
                act.dma_start(table[0][bass.ds(c * (CH * P), CH * P), :].rearrange("(b p) d -> p b d", p=P),
                              rows[:, 0:CH, :]).then_inc(s_pstore, 16)
                act.wait_ge(s_pht_copied, c * CH + CH + CH)
                act.dma_start(h_t_dram[0][bass.ds(c * CH, CH), :, :].rearrange("b p d -> p b d"),
                              pt[:, 0:CH, :]).then_inc(s_pstore_t, 16)

        def act_mlp(act, it, stage, m):
            act.wait_ge(mlp_mm[stage], it * MB + m + 1 + (MB if stage == 0 else 0))
            dst = (ra, rb)[stage][:, m % 2, :] if stage < 2 else rc[:, m, :]
            if stage == 2:
                act.wait_ge(r3_out[m], it * 16 + 16)
            act.activation(dst, ps_edge[:, m % 2, 0:MW], ACT.Silu).then_inc(mlp_act[stage], 1)
            if stage == 2:
                act.wait_ge(mlp_act[2], it * MB + m + 1 + MB)
                act.dma_start(r3_dram[bass.ds(it, 1), :, m * MW:(m + 1) * MW].rearrange("a p n -> p (a n)"),
                              rc[:, m, :]).then_inc(r3_out[m], 16)

        def act_relu_a(act, i, k):
            t0, n = GROUPS[k]
            for c in range(2):
                act.wait_ge(a_done, (i * NG + k) * 2 + c + 1 + 2 * NG)
                u = last_use(k, 2, NG)
                ug = u % NG
                tiles = GROUPS[ug][0] + GROUPS[ug][1] - (TPI if u < 0 else 0)
                act.wait_ge(z_done, i * TPI + tiles + TPI)
                act.activation(r_t[:, k % 2, c, 0:n * P], ps_edge[:, c, 0:n * P], ACT.Relu).then_inc(r_done, 1)

        def act_relu_msg(act, i, k):
            t0, n = GROUPS[k]
            act.wait_ge(z_read, i * TPI + t0 + n + TPI)
            act.activation(rows[:, t0:t0 + n, :], rows[:, t0:t0 + n, :], ACT.Relu).then_inc(msg_done, 1)

        def act_load_ht(act, l, b):
            n = b + (l * NB + 1)
            act.wait_ge(n_mm, n)
            if l == 3:
                act.wait_ge(o_mm, b + 1)
            act.dma_start(h_t[:, :, :].rearrange("p c n -> p (c n)"),
                          h_t_dram[l][bass.ds(b, 1), :, :].rearrange("a p d -> p (a d)")).then_inc(ht_in, 16)

        def act_node_b(act, l, b):
            if l == 0:
                act.wait_ge(n_lk, b + 1)
                act.activation(y[:, :], y2[:, :], ACT.Square, accum_out=small[:, 20:21]).then_inc(n_ss, 1)
                act.wait_ge(n_ss, b + 1)
                act.activation(small[:, 21:22], small[:, 20:21], ACT.Sqrt).then_inc(n_root, 1)
            if l == 2:
                act.wait_ge(g_mv, b + 1)
                act.activation(small[:, 26:27], small[:, 25:26], ACT.Sqrt, bias=eps[:, 0:1]).then_inc(g_root, 1)
                act.wait_ge(g_tp, b + 1)
                act.activation(y_t[:, :, :], ps_tp[:, 2:4, :], ACT.Relu).then_inc(g_yt, 1)
            if l == 3:
                act.wait_ge(n_mm, b + (3 * NB + 2))
                act.copy(y[:, :], ps_node[:, 0, :]).then_inc(o_acopy, 1)
                act.wait_ge(o_tp, b + 2)
                act.copy(y_t[:, :, :], ps_tp[:, 2:4, :]).then_inc(o_bt, 1)

        def act_node_c(act, l, b):
            n = b + (l * NB + 1)
            if l < 3:
                xb = x_all[:, bass.ds(b, 1), :].rearrange("p a d -> p (a d)")
                act.wait_ge(t_mv, n + (NB // CH + 1))
                act.activation(small[:, 16:17], small[:, 15:16], ACT.Sqrt, bias=eps[:, 0:1]).then_inc(t_root, 1)
                act.wait_ge(t_scale, n)
                act.wait_ge(table_out, n * 16)
                act.activation(h_new[:, :], xb, ACT.Relu, bias=small[:, 18:19], scale=small[:, 17:18]).then_inc(t_h, 1)
                if l == 0:
                    act.wait_ge(t_h, n)
                    act.dma_start(table[1][bass.ds(b * P, P), :], h_new[:, :]).then_inc(table_out, 16)
                if l == 1:
                    act.wait_ge(t_lb, b + 1)
                    act.dma_start(table[2][bass.ds(b * P, P), :], t_out[:, :]).then_inc(table_out, 16)
                act.wait_ge(t_tp, n)
                act.wait_ge(ht_out, n * 16)
                act.copy(h_new_t[:, :, :], ps_tp[:, 0:2, :]).then_inc(t_ht, 1)
                act.wait_ge(t_ht, n + 1)
                act.dma_start(h_t_dram[l + 1][bass.ds(b, 1), :, :].rearrange("a p d -> p (a d)"),
                              h_new_t[:, :, :].rearrange("p c n -> p (c n)")).then_inc(ht_out, 16)
                if l == 2:
                    act.wait_ge(t_tab, b + 1)
                    act.copy(t_out[:, :], ps_node[:, 0, :]).then_inc(t_up, 1)
                    act.wait_ge(t_up, b + 2)
                    act.dma_start(table[3][bass.ds(b * P, P), :], t_out[:, :]).then_inc(table_out, 16)
            else:
                act.wait_ge(o_mm, b + 2)
                act.wait_ge(o_summed, (b + 1) * 2)
                act.copy(t_out[:, :], ps_node[:, 1, :]).then_inc(o_copied, 1)
                act.activation(h_new[:, :], ps_node[:, 1, :], ACT.Square).then_inc(o_sqd, 1)
                act.copy(acc[:, :, bass.ds(b * P, P)], ps_node[:, 1, :].rearrange("p (h c) -> p h c", h=2)).then_inc(o_kept, 1)

        def act_edges(act, l, it, nw, b):
            i = it - layer_its[l][0]
            if l == 2 and nw == 1:
                act_relu_a(act, i, 0)
            for k in range(NG):
                if l == 0:
                    for stage, m in MLP_AT[k]:
                        act_mlp(act, it, stage, m)
                if l == 2:
                    if nw > 1:
                        act_relu_a(act, i, k)
                    elif k + 1 < NG:
                        act_relu_a(act, i, k + 1)
                    act_relu_msg(act, i, k)
                if b is not None:
                    if k == 0:
                        act_load_ht(act, l, b)
                    if k == 4:
                        act_node_b(act, l, b)
            if b is not None:
                act_node_c(act, l, b)

        def act_layer(act, l, nw):
            if l:
                act.wait_ge(ht_out, 16 * l * NB + 16)
            else:
                act.wait_ge(s_pstore_t, 16 * (NB // CH) + 16)
            if l == 2:
                for m in range(MB):
                    act.wait_ge(r3_out[m], 16 * NI + 16)
            if l == 3:
                act.wait_ge(table_out, 16 * 3 * NB + 16)
            run_layer(act, l, nw, act_edges, [act_load_ht, act_node_b, act_node_c])

        def act_final(act):
            act.wait_ge(f_step, FIN["var_mean"])
            act.activation(fin[:, 5, 0:2 * C], fin[:, 4, 0:2 * C], ACT.Sqrt, bias=eps[:, 0:1]).then_inc(f_root, 1)

        taken = [0]

        def carve(*dims):
            n = int(np.prod(dims))
            piece = arena[:, taken[0]:taken[0] + n]
            taken[0] += n + n % 2
            return piece if len(dims) == 1 else piece.rearrange("p (a b) -> p a b", a=dims[0])

        early = carve(NI * BPAD)
        base_f = carve(NI * BPAD)
        bn_c = carve(CH, 6)
        mv_c = carve(CH, 2)
        mv_all = carve(NB, 2)
        stats_all = carve(3, NB)
        pt = carve(CH, D)
        w_e2 = carve(2, D)
        w_le = carve(2, D)
        b12 = carve(2, D)
        be2 = carve(2)
        bc_rest = carve(2, D)
        bc_parts = carve(3, D // 2).bitcast(BF16)
        iota_i = sb("iota_i", [P, WIN], I32)
        spare = sb("spare", [1, 8])
        fl = sb("fl", [P, 8])
        flag_f = sb("flag_f", [P, 2])
        s_pol = sem("s_pol")
        s_w3 = sem("s_w3")
        s_dst_again = sem("s_dst_again")
        gate_step = sem("gate_step")
        dst_step = sem("dst_step")
        sh_in = [sem("sh_in0"), sem("sh_in1")]
        passed = sem("passed")
        bn_part = sem("bn_part")
        mv_part = sem("mv_part")
        early_in = sem("early_in")
        raw_ones = sem("raw_ones")
        ve_base_regs = []

        MLP_AT = [[(0, 0), (0, 1)], [(1, 0), (1, 1)], [(2, 0), (2, 1), (0, 2)], [(1, 2)], [(2, 2)]]
        PRE = {n: i + 1 for i, n in enumerate(
            ["o_sum", "o_sq", "zeros", "base0", "acc0", "dst_f", "base_f", "m4", "bias0", "wc", "bc_hi", "bc_r1",
             "bc_mid", "bc_r2", "bc_lo"] + [f"rel{k}" for k in range(NG)] +
            ["rel_max", "rel_min", "over", "under", "early", "early_max"])}
        FIN = {n: i + 1 for i, n in enumerate(
            ["mu", "centre", "square", "var_sum", "var_part", "nrm", "nrm_mean", "var_mean", "rstd", "a0", "s1", "n0", "x0",
             "x0b", "s1x", "n1a", "n1b", "x1a", "x1b"])}
        POLY = 12

        block = ctx.enter_context(nc.Block())
        paths = ((1, "a window for each group"), (ALLWIN, "all windows"))

        def credits(nw):
            return {
                "pe": [(summed, NG * nw), (a_done, 2 * NG), (tpw_done, TPI), (z_done, TPI), (mlp_mm[0], MB), (n_mm, 1), (o_tp, 1), (o_mm, 1)],
                "ve": [(added, NG * nw), (z_read, TPI), (u_done, TPI), (x_new, 1), (wbase_done, 1), (g_x1, 1), (o_summed, 2)],
                "act": [(r_done, 2), (mlp_act[2], MB), (t_up, 1), (o_acopy, 1), (g_yt, 1), (o_bt, 1), (t_ht, 1), (o_kept, 1)],
            }

        def branch(eng, program):
            eng.wait_ge(s_flag, 1)
            reg = eng.value_load(flag_i[0:1, 0:1], min_val=-(1 << 24), max_val=1 << 24)
            with eng.If(reg < 1):
                program(1)
            with eng.Else():
                program(ALLWIN)

        @block.sync
        def _(sp):
            sp.dma_start(early, io["early"].partition_broadcast(P)).then_inc(early_in, 16)
            for j, s in enumerate([s_pstore, s_pstore_t, table_out, ht_out, *r3_out]):
                sp.dma_start(spare[0:1, j:j + 1], io["early"][0:1]).then_inc(s, 16)
            sp_setup(sp)

            def program(nw):
                if nw > 1:
                    sp.dma_start(rel[:, :].bitcast(I32), io["dst"]).then_inc(s_dst_again, 16)
                for l in range(4):
                    sp_layer(sp, l, nw)

            branch(sp, program)
            sp.wait_ge(f_step, FIN["x1b"])
            sp.dma_start(io["out"].rearrange("(b p) d -> p b d", p=P), x_all[:, :, :]).then_inc(s_out, 16)
            sp.wait_ge(s_out, 16)

        @block.gpsimd
        def _(pool):
            pool_setup(pool)

            def program(nw):
                for l in range(4):
                    pool_layer(pool, l, nw)

            branch(pool, program)

        @block.tensor
        def _(pe):
            pe_setup(pe)

            def program(nw):
                for s, v in credits(nw)["pe"]:
                    pe.sem_inc(s, v)
                for l in range(4):
                    if l == 2:
                        pe.wait_ge(s_bc, 48)
                        pe.wait_ge(raw_ones, 1)
                    if l == 3:
                        pe.wait_ge(t_up, NB + 1)
                        pe.wait_ge(s_w3, 48)
                    run_layer(pe, l, nw, pe_edges, [pe_node_a, pe_node_b, pe_node_c])

            branch(pe, program)
            pe_final(pe)

        @block.vector
        def _(ve):
            ve.sem_inc(s_pht_copied, CH)
            ve.sem_inc(t_mv, 1)
            ve.wait_ge(early_in, 16)
            ve_setup(ve)
            ve_base_regs.extend(ve.alloc_register(f"window_start{k}") for k in range(NG))

            def program(nw):
                for s, v in credits(nw)["ve"]:
                    ve.sem_inc(s, v)
                if nw > 1:
                    ve.wait_ge(s_dst_again, 16)
                    ve.tensor_copy(rel[:, :], rel[:, :].bitcast(I32)).then_inc(dst_step, 1)
                    ve.wait_ge(dst_step, 1)

                def ve_node_first(ve, l, b):
                    ve.wait_ge(added, ((l + 1) * NI * NG + NG) * nw)
                    ve_node_a(ve, l, b)

                for l in range(4):
                    if l == 2:
                        ve.wait_ge(s_pol, 16)
                        ve.tensor_scalar(ew[:, :], ew[:, :], 0.0, 1.0, ALU.max, ALU.min).then_inc(gate_step, 1)
                        ve.wait_ge(gate_step, 1)
                        ve.tensor_scalar(ew[:, :], ew[:, :], 0.01, None, ALU.add).then_inc(gate_step, 1)
                        ve.wait_ge(gate_step, 2)
                        ve.memset(raw[C:C + 1, :], 1.0).then_inc(raw_ones, 1)
                    run_layer(ve, l, nw, ve_edges, [ve_node_first, ve_node_b, ve_node_c])

            branch(ve, program)
            ve_final(ve)

        @block.scalar
        def _(act):
            act.sem_inc(s_ph_t, CH)
            act_setup(act)

            def program(nw):
                for s, v in credits(nw)["act"]:
                    act.sem_inc(s, v)
                for l in range(4):
                    act_layer(act, l, nw)

            branch(act, program)
            act_final(act)


def layouts(a, n_nodes, n_edges):
    f = {k: np.asarray(v) for k, v in a.items()}
    NB, NI = shapes(n_nodes, n_edges)
    ep = NI * TPI * P

    def edges(v, fill=0):
        out = np.full((ep,) + v.shape[1:], fill, v.dtype)
        out[:n_edges] = v
        return out

    def tiles(v):
        return np.ascontiguousarray(np.moveaxis(v.reshape((NI * TPI, P) + v.shape[1:]), 0, 1))

    d = {}
    x = np.zeros((NB * P, D), np.float32)
    x[:n_nodes] = f["x"]
    d["x"] = x
    src = edges(f["src"])
    dst = edges(f["dst"], n_nodes)
    d["src"], d["dst"] = tiles(src), tiles(dst)
    base = np.zeros((NI, BPAD), np.int32)
    for k, (t0, n) in enumerate(GROUPS):
        base[:, k] = dst.reshape(NI, TPI, P)[:, t0, 0]
    d["base"] = base.reshape(1, NI * BPAD)
    early = np.zeros((NI, BPAD), np.float32)
    for k in range(NG):
        early[:, k] = np.maximum(0, P * (np.arange(NI) - (0 if k >= NODE_AT else 1)))
    d["early"] = early.reshape(NI * BPAD)
    d["ew"] = tiles(edges(f["edge_weight"]))
    d["sh"] = tiles(edges(f["edge_attr_4"]))
    d["pol"] = tiles(edges(np.ascontiguousarray(f["edge_attr_65"][:, 0])))
    raw = edges(np.ascontiguousarray(f["edge_attr_65"][:, 1:]))
    d["raw"] = np.ascontiguousarray(raw.reshape(NI, TPI * P, C).transpose(0, 2, 1))
    rbf = np.zeros((NI, TPI + 1, P, 16), np.float32)
    rbf[:, :TPI] = edges(f["edge_attr_16"]).reshape(NI, TPI, P, 16)
    d["rbf"] = np.ascontiguousarray(rbf.reshape(NI, 9, 2, P, 16).transpose(0, 2, 4, 1, 3)).reshape(NI, 32, 9 * P)
    L0, L1, L2, L3 = "L0_gnn_", "L1_gnn_", "L2_gnn_", "L3_gnn_"

    def blocks(w0, w1, rows_mixed, cols_mixed):
        m = np.zeros((D, D), np.float32)
        m[:C, :C] = w0
        for q in range(3):
            r = C + q + 3 * np.arange(C) if rows_mixed else C + C * q + np.arange(C)
            c = C + q + 3 * np.arange(C) if cols_mixed else C + C * q + np.arange(C)
            m[np.ix_(r, c)] = w1
        return m

    by_name = {
        "l0_w1": f[L0 + "W1"].T, "l0_w2": f[L0 + "W2"].T, "l1_w1": f[L1 + "W1"].T, "l1_w2": f[L1 + "W2"].T,
        "e2": f[L2 + "W_e2"], "le": f[L2 + "W_le"].T, "g1": f[L2 + "W_g1"].T, "g2": f[L2 + "W_g2"].T,
        "up": blocks(f[L3 + "W_up0"], f[L3 + "W_up1"], True, False),
        "lin": blocks(f[L3 + "W_lin0"], f[L3 + "W_lin1"], False, False),
        "wb": blocks(f[L3 + "WB0"], f[L3 + "WB1"], False, True),
        "sc": blocks(f[L3 + "Wsc0"], f[L3 + "Wsc1"], True, True),
    }
    d["weights"] = np.stack([by_name[n] for n in WEIGHTS])
    w0, w1, z = f[L3 + "Wc0"], f[L3 + "Wc1"], np.zeros(C, np.float32)
    rowd = {
        "b_le": f[L2 + "b_le"], "b_g1": f[L2 + "b_g1"],
        "ln_g": f[L2 + "ln_g"], "ln_b": f[L2 + "ln_b"], "b_g2": f[L2 + "b_g2"],
        "wc0a": np.concatenate([w0[:, 3], w1[:, 2], w0[:, 1], w1[:, 1]]),
        "wc0b": np.concatenate([w0[:, 0], w1[:, 0], w0[:, 4], w1[:, 3]]),
        "wc1": np.concatenate([w0[:, 2], z, z, z]),
        "norm": np.concatenate([f[L3 + "gamma0"], f[L3 + "beta0"], f[L3 + "gamma1"], z]),
    }
    d["b12"] = np.concatenate([f[L0 + "b1"], f[L0 + "b2"]])
    d["rowc"] = np.concatenate([rowd[n] for n in ROWS])
    d["we1"] = np.concatenate([f[L2 + "W_e1"].T, f[L2 + "b_e1"][None, :]])
    d["be2"] = f[L2 + "b_e2"].reshape(2, P).T

    def twice(w):
        r, c = w.shape
        m = np.zeros((2 * r, 2 * c), np.float32)
        m[:r, :c] = w
        m[r:, c:] = w
        return m

    d["m1"], d["m2"], d["m3"] = twice(f[L3 + "M1"]), twice(f[L3 + "M2"]), twice(f[L3 + "M3"])
    d["m4"] = np.concatenate([f[L3 + "M4"], f[L3 + "M4"]])
    return {k: np.ascontiguousarray(v) for k, v in d.items()}


def kernel(**inputs):
    import concourse.bacc as _bacc
    from concourse import mybir as _mybir
    from concourse.bass_utils import run_bass_kernel_spmd as _run

    n_nodes, n_edges = inputs["x"].shape[0], inputs["src"].shape[0]
    nb, _ = shapes(n_nodes, n_edges)
    nc = _bacc.Bacc("TRN2", target_bir_lowering=False, num_devices=1)
    arrays, io = {}, {}
    for name, a in layouts(inputs, n_nodes, n_edges).items():
        arrays[f"in_{name}"] = a
        io[name] = nc.dram_tensor(f"in_{name}", a.shape, _mybir.dt.from_np(a.dtype), kind="ExternalInput").ap()
    io["out"] = nc.dram_tensor("out_x", (nb * P, D), _mybir.dt.float32, kind="ExternalOutput").ap()
    build(nc, io, n_nodes, n_edges)
    r = _run(nc, [arrays], core_ids=[0])
    return r.results[0]["out_x"][:n_nodes]
```

```python
from contextlib import ExitStack

import numpy as np

import concourse.bass as bass
from concourse import mybir

F32 = mybir.dt.float32
BF16 = mybir.dt.bfloat16
I32 = mybir.dt.int32
ALU = mybir.AluOpType
ACT = mybir.ActivationFunctionType
AX_X = mybir.AxisListType.X
RMAX = bass.bass_isa.ReduceOp.max

P = 128
D = 256
C = 64
LN_EPS = 1e-5
NORM_EPS = 1e-12
LEAKY = 0.2
WIN = 64
GROUPS = [(0, 3), (3, 3), (6, 3), (9, 3), (12, 3), (15, 2)]
TPI = 17
NG = len(GROUPS)
BPAD = 8
NODE_AT = 2
LAG = 2
HALVES = ((0, 9, (0, 1, 2)), (9, 8, (3, 4, 5)))
MB = 3
MW = 384

WEIGHTS = ["l0_w1", "l0_w2", "l1_w1", "l1_w2", "g1", "g2", "up", "e2", "le", "lin", "wb", "sc"]
PLACE = {"l0_w1": 0, "l0_w2": 1, "l1_w1": 2, "l1_w2": 3, "g1": 4, "g2": 5, "up": 6, "lin": 0, "wb": 1, "sc": 2}
ROWS = ["b_le", "b_g1", "ln_g", "ln_b", "b_g2", "wc0a", "wc0b", "wc1", "norm"]


def shapes(n_nodes, n_edges):
    nb = -(-n_nodes // P)
    ni = -(-n_edges // (P * TPI))
    assert nb == ni
    return nb, ni


def build(nc, io, n_nodes, n_edges):
    NB, NI = shapes(n_nodes, n_edges)
    T = NI * TPI
    LAST = n_nodes - (NB - 1) * P
    NCOL = NB * P + WIN
    ALLWIN = NCOL // WIN
    CH = max(c for c in range(1, 8) if NB % c == 0)

    with ExitStack() as ctx:
        def sb(name, shape, dt=F32):
            return ctx.enter_context(nc.sbuf_tensor(name, shape, dt))

        def psum(name, shape, dt=F32):
            return ctx.enter_context(nc.psum_tensor(name, shape, dt))

        def sem(name):
            return ctx.enter_context(nc.semaphore(name))

        table = [nc.dram_tensor(f"table{l}", [NB * P, D], F32, kind="Internal").ap() for l in range(4)]
        h_t_dram = [nc.dram_tensor(f"h_t{l}", [NB, P, D], F32, kind="Internal").ap() for l in range(4)]
        r3_dram = nc.dram_tensor("r3", [NI, P, MB * MW], F32, kind="Internal").ap()

        x_all = sb("x_all", [P, NB, D])
        acc = sb("acc", [P, 2, NCOL])
        w_all = sb("w_all", [P, 7, 2, D])
        rowc = sb("rowc", [P, len(ROWS), D])
        rel = sb("rel", [P, T])
        ew = sb("ew", [P, T])
        sh = sb("sh", [P, TPI, 4])
        base_i = sb("base_i", [1, (NI + 1) * BPAD], I32)
        ident = sb("ident", [P, P])
        iota = sb("iota", [P, WIN])
        ones = sb("ones", [P, P])
        flag_i = sb("flag_i", [P, 1], I32)
        eps = sb("eps", [P, 1])
        zeros = sb("zeros", [P, 2, P])
        bias0 = sb("bias0", [P, D])
        we1 = sb("we1", [C + 1, D])
        wc = sb("wc", [P, 2, D])
        bc3 = sb("bc3", [3, D], BF16)
        ones3 = sb("ones3", [3, P], BF16)
        m1 = sb("m1", [2 * 16, P])
        m2 = sb("m2", [P, P])
        m3 = sb("m3", [P, P])
        m4 = sb("m4", [P, D])
        idx = sb("idx", [P, TPI], I32)
        rows = sb("rows", [P, TPI, D])
        hot = sb("hot", [P, TPI, WIN])
        arena = sb("arena", [P, 8 * 4 * WIN + 8 * 8 * C])
        raw = arena[0:C + 1, 0:TPI * P]
        r_t = arena[:, TPI * P:TPI * P + 2 * 2 * MW].rearrange("p (b c n) -> p b c n", b=2, c=2)
        hot4 = arena[:, 0:8 * 4 * WIN].rearrange("p (t k w) -> p t k w", t=8, k=4)
        u_ring = arena[:, 8 * 4 * WIN:].rearrange("p (t j c) -> p t j c", t=8, j=8)
        rbf = arena[0:32, 0:MB * MW]
        ra = arena[:, MB * MW:MB * MW + 2 * MW].rearrange("p (b n) -> p b n", b=2)
        rb = arena[:, (MB + 2) * MW:(MB + 4) * MW].rearrange("p (b n) -> p b n", b=2)
        rc = arena[:, (MB + 4) * MW:(2 * MB + 4) * MW].rearrange("p (b n) -> p b n", b=MB)
        r3 = sb("r3_sb", [P, MB * MW])
        h_t = sb("h_t_in", [P, 2, P])
        q_t = sb("q_t", [P, 2, P])
        y = sb("y", [P, D])
        y2 = sb("y2", [P, D])
        y_t = sb("y_t", [P, 2, P])
        h_new = sb("h_new", [P, D])
        h_new_t = sb("h_new_t", [P, 2, P])
        t_out = sb("t_out", [P, D])
        small = sb("small", [P, 32])
        poly = sb("poly", [P, 2, C])
        poly2 = sb("poly2", [P, 2, C])
        vv = sb("vv", [P, 2, C])
        o_sum = sb("o_sum", [P, D])
        o_sq = sb("o_sq", [P, D])
        fin = arena[:, 0:8 * D].rearrange("p (j d) -> p j d", d=D)
        wbase = sb("wbase", [P, 1])
        relw = sb("relw", [P, 4])

        def W(name):
            return w_all[:, PLACE[name], :, :]

        def R(name):
            return rowc[:, ROWS.index(name), :]

        ps_even = psum("ps_even", [P, 2, 2 * P])
        ps_odd = psum("ps_odd", [P, 2, 2 * P])
        ps_node = psum("ps_node", [P, 2, D])
        ps_tp = psum("ps_tp", [P, 4, P])
        ps_edge = psum("ps_edge", [P, 4, 512])

        def ps_acc(k):
            return (ps_odd if k % 2 else ps_even)[:, :, 0:WIN]

        ps_z = ps_edge[:, 2:4, 0:D]
        ps_tpw = ps_edge[:, :, 0:D]

        s_weights = sem("s_weights")
        s_scalars = sem("s_scalars")
        s_x = [sem(f"s_x{c}") for c in range(NB // CH)]
        s_const = sem("s_const")
        s_pre = sem("s_pre")
        s_prep_mm = sem("s_prep_mm")
        s_bc = sem("s_bc")
        s_flag_part = sem("s_flag_part")
        s_flag_all = sem("s_flag_all")
        s_flag = sem("s_flag")
        s_root = sem("s_root")
        s_scale = sem("s_scale")
        s_ph = sem("s_ph")
        s_ph_t = sem("s_ph_t")
        s_pht_copied = sem("s_pht_copied")
        s_pstore = sem("s_pstore")
        s_pstore_t = sem("s_pstore_t")
        idx_in = [sem("idx_in0"), sem("idx_in1")]
        rows_in = [sem(f"rows_in{k}") for k in range(NG)]
        hot_ready = sem("hot_ready")
        hot_part = sem("hot_part")
        summed = sem("summed")
        added = sem("added")
        relw_done = sem("relw_done")
        wbase_done = sem("wbase_done")
        rbf_in = [sem(f"rbf_in{m}") for m in range(MB)]
        mlp_mm = [sem(f"mlp_mm{s}") for s in range(3)]
        mlp_act = [sem(f"mlp_act{s}") for s in range(3)]
        r3_out = [sem(f"r3_out{m}") for m in range(MB)]
        r3_in = [sem(f"r3_in{m}") for m in range(MB)]
        raw_in = [sem(f"raw_in{k}") for k in range(NG)]
        a_done = sem("a_done")
        r_done = sem("r_done")
        z_done = sem("z_done")
        z_read = sem("z_read")
        msg_done = sem("msg_done")
        tpw_done = sem("tpw_done")
        u_done = sem("u_done")
        ht_in = sem("ht_in")
        q_ready = sem("q_ready")
        acc_free = sem("acc_free")
        n_mm = sem("n_mm")
        n_y = sem("n_y")
        n_lk = sem("n_lk")
        n_ss = sem("n_ss")
        n_root = sem("n_root")
        n_mx = sem("n_mx")
        n_rn = sem("n_rn")
        x_new = sem("x_new")
        t_bn = sem("t_bn")
        t_mv = sem("t_mv")
        t_root = sem("t_root")
        t_rstd = sem("t_rstd")
        t_scale = sem("t_scale")
        t_h = sem("t_h")
        t_tp = sem("t_tp")
        t_ht = sem("t_ht")
        t_tab = sem("t_tab")
        t_up = sem("t_up")
        table_out = sem("table_out")
        ht_out = sem("ht_out")
        g_bn = sem("g_bn")
        g_mv = sem("g_mv")
        g_root = sem("g_root")
        g_rstd = sem("g_rstd")
        g_scale = sem("g_scale")
        g_hn = sem("g_hn")
        g_lg = sem("g_lg")
        g_lb = sem("g_lb")
        g_tp = sem("g_tp")
        g_yt = sem("g_yt")
        g_mm2 = sem("g_mm2")
        g_x1 = sem("g_x1")
        o_a = sem("o_a")
        o_acopy = sem("o_acopy")
        o_step = sem("o_step")
        o_b = sem("o_b")
        o_tp = sem("o_tp")
        o_bt = sem("o_bt")
        o_mm = sem("o_mm")
        o_copied = sem("o_copied")
        o_sqd = sem("o_sqd")
        o_kept = sem("o_kept")
        o_summed = sem("o_summed")
        f_mm = sem("f_mm")
        f_step = sem("f_step")
        f_root = sem("f_root")
        f_out = sem("f_out")
        s_out = sem("s_out")

        def pass_waits(eng):
            eng.sem_inc(passed, 1)

        def last_use(t, ring, total):
            return t - ring if t >= ring else max(u for u in range(total) if u % ring == t % ring) - total

        def group_of(t):
            g = next(k for k, (t0, n) in enumerate(GROUPS) if t0 <= t % TPI < t0 + n)
            return g - (NG if t < 0 else 0)

        N_WEIGHT_LOADS = 9 + 8
        MLP_IN = [(0, 1), (2,), (), ()]
        MLP_AT = [[[(0, 0), (0, 1)], [(1, 0)], [(1, 1)], [(2, 0)], [(2, 1)], []],
                  [[(0, 2)], [], [(1, 2)], [], [(2, 2)], []], [[]] * NG, [[]] * NG]

        def mlp_number(l, i, m):
            return i * 2 + m if l == 0 else NI * 2 + i
        layer_its = [(l * NI, (l + 1) * NI) for l in range(4)]

        def sp_setup(sp):
            for c in range(NB // CH):
                sp.dma_start(x_all[:, c * CH:(c + 1) * CH, :],
                             io["x"][c * CH * P:(c + 1) * CH * P, :].rearrange("(b p) d -> p b d", p=P)).then_inc(s_x[c], 16)
            for dst, name in ((rel[:, :].bitcast(I32), "dst"), (ew[:, :], "ew"), (base_i[:, :], "base")):
                sp.dma_start(dst, io[name]).then_inc(s_scalars, 16)
            for n, name in enumerate(WEIGHTS[:9]):
                place = {"e2": w_e2, "le": w_le}[name] if name in ("e2", "le") else W(name)
                sp.dma_start(place, io["weights"][n, :, :].rearrange("(c p) d -> p c d", p=P)).then_inc(s_weights, 16)
            sp.dma_start(b12.rearrange("p r d -> p (r d)"), io["b12"].partition_broadcast(P)).then_inc(s_weights, 16)
            sp.dma_start(rowc[:, :, :].rearrange("p r d -> p (r d)"),
                         io["rowc"].partition_broadcast(P)).then_inc(s_weights, 16)
            for dst, name in ((we1[:, :], "we1"), (m1[:, :], "m1"), (m2[:, :], "m2"), (m3[:, :], "m3"), (m4[:, :], "m4"),
                              (be2, "be2")):
                sp.dma_start(dst, io[name]).then_inc(s_weights, 16)
            sp.wait_ge(s_pre, PRE["bc_lo"])
            for j in range(3):
                sp.dma_start(bc3[j:j + 1, :], bc_parts[0:1, j, :]).then_inc(s_bc, 16)
            sp.wait_ge(s_bc, 48)

        def sp_indices(sp, half, i, landed):
            t0, n, groups = HALVES[half]
            if landed is not None:
                for k in groups:
                    sp.wait_ge(rows_in[k], landed * (16 * GROUPS[k][1]))
                    pass_waits(sp)
            sp.dma_start(idx[:, t0:t0 + n], io["src"][:, bass.ds(i * TPI + t0, n)]).then_inc(idx_in[half], 16)

        def sp_sh(sp, half, i, it, nw):
            t0, n, groups = HALVES[half]
            if it is not None:
                sp.wait_ge(hot_ready, (it * NG + groups[-1] + 1) * nw)
                pass_waits(sp)
            sp.dma_start(sh[:, t0:t0 + n, :], io["sh"][:, bass.ds(i * TPI + t0, n), :]).then_inc(sh_in[half], 16)

        def sp_edges(sp, l, it, i, more, nw):
            if l < 2:
                for m in MLP_IN[l]:
                    sp.wait_ge(mlp_mm[0], mlp_number(l, i, m) + (1 if l == 0 else 2))
                    pass_waits(sp)
                    sp.dma_start(rbf[:, m * MW:(m + 1) * MW],
                                 io["rbf"][bass.ds(i, 1), :, m * MW:(m + 1) * MW].rearrange("a p n -> p (a n)")).then_inc(rbf_in[m], 16)
            if l == 2:
                for k, (t0, n) in enumerate(GROUPS):
                    sp.wait_ge(a_done, i * 2 * NG + 2 * k + 2)
                    pass_waits(sp)
                    sp.dma_start(raw[0:C, t0 * P:(t0 + n) * P],
                                 io["raw"][bass.ds(i, 1), :, t0 * P:(t0 + n) * P].rearrange("a p n -> p (a n)")).then_inc(raw_in[k], 16)
            if l == 3:
                for m in range(MB):
                    sp.wait_ge(tpw_done, i * TPI + min(6 * m + 6, TPI))
                    pass_waits(sp)
                    sp.dma_start(r3[:, m * MW:(m + 1) * MW],
                                 r3_dram[bass.ds(i, 1), :, m * MW:(m + 1) * MW].rearrange("a p n -> p (a n)")).then_inc(r3_in[m], 16)
            if more:
                for half in range(2):
                    sp_indices(sp, half, i + 1, it + 1)
                    if l == 3:
                        sp_sh(sp, half, i + 1, it, nw)

        def sp_layer(sp, l, nw):
            a, z = layer_its[l]
            if l == 0:
                sp.wait_ge(s_pstore_t, 16 * (NB // CH) + 16)
            if l == 1:
                sp.wait_ge(hot_ready, NI * NG * nw)
                sp.dma_start(ew[:, :], io["pol"]).then_inc(s_pol, 16)
            if l == 2:
                sp.wait_ge(table_out, 16 * 2 * NB + 16)
                for name in ("lin", "wb", "sc"):
                    sp.dma_start(W(name), io["weights"][WEIGHTS.index(name), :, :].rearrange("(c p) d -> p c d", p=P)).then_inc(s_w3, 16)
                for m in range(MB):
                    sp.wait_ge(r3_out[m], 16 * NI + 16)
            for half in range(2):
                sp_indices(sp, half, 0, a if l else None)
                if l == 3:
                    sp_sh(sp, half, 0, None, nw)
            with sp.Fori(a, z - 1) as it:
                sp_edges(sp, l, it, it - a, True, nw)
            sp_edges(sp, l, z - 1, z - 1 - a, False, nw)

        def pool_setup(pool):
            pool.memset(ident[:, :], 0.0).then_inc(s_const, 1)
            pool.iota(iota_i[:, :], [[1, WIN]], base=0, channel_multiplier=0).then_inc(s_const, 1)
            pool.memset(ones[:, :], 1.0).then_inc(s_const, 1)
            pool.memset(ones3[:, :], 1.0).then_inc(s_const, 1)
            pool.memset(eps[:, :], LN_EPS).then_inc(s_const, 1)
            pool.wait_ge(s_const, 5)
            pool.affine_select(out=ident[:, :], in_=ident[:, :], compare_op=ALU.not_equal, fill=1.0, base=0,
                               pattern=[[-1, P]], channel_multiplier=1).then_inc(s_const, 1)
            pool.tensor_copy(iota[:, :], iota_i[:, :]).then_inc(s_const, 1)
            pool.wait_ge(s_flag_part, 1)
            pool.partition_all_reduce(flag_f[:, 1:2], flag_f[:, 0:1], P, RMAX).then_inc(s_flag_all, 1)

        def pool_edges(pool, l, it, nw):
            for k, (t0, n) in enumerate(GROUPS):
                if k % 3 == 0:
                    pool.wait_ge(idx_in[k // 3], it * 16 + 16)
                pool.wait_ge(summed, (it * NG + k + 1) * nw)
                pass_waits(pool)
                for t in range(t0, t0 + n):
                    pool.indirect_dma_start(rows[:, t, :], None, table[l],
                                            bass.IndirectOffsetOnAxis(ap=idx[:, t:t + 1], axis=0)).then_inc(rows_in[k], 16)

        def pool_layer(pool, l, nw):
            a, z = layer_its[l]
            if l == 0:
                pool.wait_ge(s_pstore, 16 * (NB // CH) + 16)
            else:
                pool.wait_ge(table_out, 16 * l * NB + 16)
            with pool.Fori(a, z) as it:
                pool_edges(pool, l, it, nw)

        def mm2(pe, out, lhs_t, w, start=True, stop=True):
            pe.matmul(out, lhs_t[:, 0, :], w[:, 0, :], start=start, stop=False)
            return pe.matmul(out, lhs_t[:, 1, :], w[:, 1, :], start=False, stop=stop)

        def pe_setup(pe):
            pe.wait_ge(s_weights, 16 * N_WEIGHT_LOADS)
            for c in range(2):
                for j in range(2):
                    mm = pe.matmul(ps_edge[:, c, 0:D], w_e2[:, j, c * P:(c + 1) * P], w_le[:, j, :],
                                   start=(j == 0), stop=(j == 1))
                mm.then_inc(s_prep_mm, 1)
            for j in range(2):
                mm = pe.matmul(ps_edge[0:1, 2, 0:D], be2[:, j:j + 1], w_le[:, j, :], start=(j == 0), stop=(j == 1))
            mm.then_inc(s_prep_mm, 1)
            pe.wait_ge(s_const, 7)
            pe.wait_ge(s_pre, PRE["base_f"])
            pe.matmul(ps_edge[:, 3, 0:(NI + 1) * BPAD], ones[0:1, :], base_f[0:1, :], start=True, stop=True).then_inc(s_prep_mm, 1)
            pe.wait_ge(s_pre, PRE["early"])
            with pe.Fori(0, NB // CH) as c:
                for j in range(CH):
                    pe.wait_ge(s_ph, c * CH + j + 1)
                    pe.wait_ge(s_pht_copied, c * CH + last_use(j, 4, CH) + 1 + CH)
                    for d in range(2):
                        mm = pe.transpose(tp_of(j, d), rows[:, j, d * P:(d + 1) * P], ident[:, :])
                    mm.then_inc(s_ph_t, 1)

        def tp_of(j, d):
            return ps_edge[:, j % 4, d * P:(d + 1) * P]

        def pe_sum(pe, l, it, k, w, nw):
            t0, n = GROUPS[k]
            a = layer_its[l][0]
            if l < 2:
                pe.wait_ge(rows_in[k], (it + 1) * 16 * n)
            elif l == 2:
                pe.wait_ge(msg_done, (it - a) * NG + k + 1)
            else:
                pe.wait_ge(u_done, (it - a) * TPI + t0 + n + TPI)
            pe.wait_ge(hot_ready, (it * NG + k) * nw + (w + 1))
            if nw == 1:
                pe.wait_ge(added, it * NG + k - 1 + NG)
            else:
                pe.wait_ge(added, (it * NG + k) * nw + w + NG * nw)
            out = ps_acc(k)
            for t in range(t0, t0 + n):
                first, last = t == t0, t == t0 + n - 1
                if l < 3:
                    for c in range(2):
                        mm = pe.matmul(out[:, c, :], rows[:, t, c * P:(c + 1) * P], hot[:, t, :],
                                       start=(first and c == 0), stop=last, skip_group_check=True)
                else:
                    u = u_ring[:, t % 8, :, :]
                    s = hot4[:, t % 8, :, :]
                    pe.matmul(out[:, 0, :], u[:, 0:2, :], s[:, 0, :], start=first, stop=False, skip_group_check=True)
                    pe.matmul(out[:, 1, :], u[:, 2:4, :], s[:, 0, :], start=False, stop=False, skip_group_check=True)
                    pe.matmul(out[0:C, 0, :], u[:, 4, :], s[:, 1, :], start=False, stop=False, skip_group_check=True)
                    pe.matmul(out[C:P, 0, :], u[:, 7, :], s[:, 1, :], start=False, stop=False, skip_group_check=True)
                    pe.matmul(out[0:C, 0, :], u[:, 5, :], s[:, 2, :], start=False, stop=False, skip_group_check=True)
                    pe.matmul(out[0:C, 1, :], u[:, 7, :], s[:, 2, :], start=False, stop=False, skip_group_check=True)
                    pe.matmul(out[0:C, 0, :], u[:, 6, :], s[:, 3, :], start=False, stop=last, skip_group_check=True)
                    mm = pe.matmul(out[C:P, 1, :], u[:, 7, :], s[:, 3, :], start=False, stop=last, skip_group_check=True)
            mm.then_inc(summed, 1)

        def pe_mlp(pe, l, i, stage, m):
            q = mlp_number(l, i, m)
            if stage == 0:
                pe.wait_ge(rbf_in[m], i * 16 + 16)
                src, w = rbf[:, m * MW:(m + 1) * MW], m1
            else:
                pe.wait_ge(mlp_act[stage - 1], q + 1)
                src, w = (ra, rb)[stage - 1][:, m % 2, :], (m2, m3)[stage - 1]
            if stage == 0:
                pe.wait_ge(mlp_act[2], q + (1 if l == 0 else 2))
            pe.matmul(ps_edge[:, m % 2, 0:MW], w[:, :], src, start=True, stop=True).then_inc(mlp_mm[stage], 1)

        def pe_a(pe, i, k):
            t0, n = GROUPS[k]
            pe.wait_ge(raw_in[k], i * 16 + 16)
            for c in range(2):
                pe.wait_ge(r_done, (i * NG + k) * 2 + c + 1)
                pe.matmul(ps_edge[:, c, 0:n * P], we1[:, c * P:(c + 1) * P], raw[:, t0 * P:(t0 + n) * P],
                          start=True, stop=True).then_inc(a_done, 1)

        def pe_z(pe, i, k):
            t0, n = GROUPS[k]
            pe.wait_ge(r_done, (i * NG + k) * 2 + 2 + 2)
            for t in range(t0, t0 + n):
                pe.wait_ge(z_read, i * TPI + last_use(t, 2, TPI) + 1 + TPI)
                z = ps_z[:, t % 2, :]
                pe.matmul(z, ones3[:, :], bc3[:, :], start=True, stop=False)
                for c in range(2):
                    mm = pe.matmul(z, r_t[:, k % 2, c, (t - t0) * P:(t - t0 + 1) * P], wc[:, c, :],
                                   start=False, stop=(c == 1))
                mm.then_inc(z_done, 1)

        def pe_tpw(pe, i, k):
            t0, n = GROUPS[k]
            for t in range(t0, t0 + n):
                if t in (0, 6, 12):
                    pe.wait_ge(r3_in[t // 6], i * 16 + 16)
                pe.wait_ge(u_done, i * TPI + last_use(t, 4, TPI) + 1 + TPI)
                q = C * (t % 2)
                pe.matmul(ps_tpw[:, t % 4, :], r3[q:q + C, (t // 2) * P:(t // 2 + 1) * P], m4[q:q + C, :],
                          start=True, stop=True).then_inc(tpw_done, 1)

        def pe_node_a(pe, l, b):
            n = b + (l * NB + 1)
            pe.wait_ge(q_ready, n)
            pe.wait_ge(ht_in, n * 16)
            out = ps_node[:, 0, :]
            if l < 3:
                pe.wait_ge(x_new, n)
            if l < 2:
                mm2(pe, out, h_t, W(f"l{l}_w1"), stop=False)
                mm2(pe, out, q_t, W(f"l{l}_w2"), start=False).then_inc(n_mm, 1)
            elif l == 2:
                pe.wait_ge(t_up, b + 1)
                mm2(pe, out, q_t, W("g1")).then_inc(n_mm, 1)
            else:
                pe.wait_ge(o_acopy, b + 1)
                pe.wait_ge(o_kept, b + 1)
                for c in range(2):
                    mm = pe.matmul(ps_node[:, 0, c * P:(c + 1) * P], q_t[:, c, :], W("lin")[:, c, c * P:(c + 1) * P],
                                   start=True, stop=True)
                mm.then_inc(n_mm, 1)

        def pe_transpose(pe, out, src):
            for c in range(2):
                mm = pe.transpose(out[:, c, :], src[:, c * P:(c + 1) * P], ident[:, :])
            return mm

        def pe_turn_y(pe, l, b):
            if l == 2:
                pe.wait_ge(g_lb, b + 1)
                pe.wait_ge(g_yt, b + 1)
            else:
                pe.wait_ge(o_b, b + 1)
                pe.wait_ge(o_bt, b + 1)
            pe_transpose(pe, ps_tp[:, 2:4, :], y2).then_inc(g_tp if l == 2 else o_tp, 1)

        def pe_second(pe, l, b):
            if l == 2:
                pe.wait_ge(g_yt, b + 2)
                pe.wait_ge(g_x1, b + 1)
                mm2(pe, ps_node[:, 1, :], y_t, W("g2")).then_inc(g_mm2, 1)
            else:
                pe.wait_ge(o_bt, b + 2)
                pe.wait_ge(o_kept, b + 1)
                mm2(pe, ps_node[:, 1, :], h_t, W("sc"), stop=False)
                mm2(pe, ps_node[:, 1, :], y_t, W("wb"), start=False).then_inc(o_mm, 1)

        def pe_turn(pe, l, b):
            n = b + (l * NB + 1)
            pe.wait_ge(t_h, n)
            pe.wait_ge(t_ht, n)
            pe_transpose(pe, ps_tp[:, 0:2, :], h_new).then_inc(t_tp, 1)

        def pe_up(pe, l, b):
            pe.wait_ge(t_ht, b + (l * NB + 2))
            mm2(pe, ps_node[:, 0, :], h_new_t, W("up")).then_inc(t_tab, 1)

        def pe_edges(pe, l, it, nw, node, first):
            i = it - layer_its[l][0]
            if nw > 1:
                for k in range(NG):
                    for stage, m in MLP_AT[l][k]:
                        pe_mlp(pe, l, i, stage, m)
                    if l == 2:
                        pe_a(pe, i, k)
                        pe_z(pe, i, k)
                    if l == 3:
                        pe_tpw(pe, i, k)
                    with pe.Fori(0, nw) as w:
                        pe_sum(pe, l, it, k, w, nw)
                return
            if l == 2:
                pe_a(pe, i, 0)
            for k in range(NG):
                for stage, m in MLP_AT[l][k]:
                    pe_mlp(pe, l, i, stage, m)
                if l == 2:
                    if k + 1 < NG:
                        pe_a(pe, i, k + 1)
                    pe_z(pe, i, k)
                if l == 3:
                    pe_tpw(pe, i, k)
                node(2 * k)
                if l < 2:
                    pe_sum(pe, l, it, k, 0, 1)
                elif k:
                    pe_sum(pe, l, it, k - 1, 0, 1)
                elif not first:
                    pe_sum(pe, l, it - 1, NG - 1, 0, 1)
                node(2 * k + 1)

        def pe_close(pe, l):
            if l >= 2:
                pe_sum(pe, l, layer_its[l][1] - 1, NG - 1, 0, 1)

        def run_layer(eng, l, nw, edges, parts, close=None):
            a, z = layer_its[l]

            def among(early, late):
                def node(p):
                    for position, part in parts:
                        if position == p + 2 * NG and late is not None:
                            part(eng, l, late)
                    for position, part in parts:
                        if position == p and early is not None:
                            part(eng, l, early)
                return node

            if nw == 1:
                edges(eng, l, a, nw, among(None, None), True)
                edges(eng, l, a + 1, nw, among(0, None), False)
                with eng.Fori(a + 2, z) as it:
                    edges(eng, l, it, nw, among(it - (a + 1), it - (a + 2)), False)
                if close:
                    close(eng, l)
                for position, part in parts:
                    if position >= 2 * NG:
                        part(eng, l, NB - 2)
                for _, part in parts:
                    part(eng, l, NB - 1)
            else:
                with eng.Fori(a, z) as it:
                    edges(eng, l, it, nw, None, False)
                with eng.Fori(0, NB - 1) as b:
                    for _, part in parts:
                        part(eng, l, b)
                for _, part in parts:
                    part(eng, l, NB - 1)

        PE_PARTS = [[(8, pe_node_a), (15, pe_turn)], [(8, pe_node_a), (13, pe_turn)],
                    [(8, pe_node_a), (12, pe_turn_y), (14, pe_second), (17, pe_turn), (18, pe_up)],
                    [(8, pe_node_a), (12, pe_turn_y), (14, pe_second)]]

        def pe_final(pe):
            pe.wait_ge(o_summed, 2 * NB + 2)
            pe.matmul(ps_edge[:, 0, 0:D], ones[:, :], o_sum[:, :], start=True, stop=True)
            pe.matmul(ps_edge[:, 1, 0:D], ones[:, :], o_sq[:, :], start=True, stop=True).then_inc(f_mm, 1)
            pe.wait_ge(f_step, FIN["var_part"])
            pe.matmul(ps_edge[:, 2, 0:C], ones[:, :], fin[:, 2, 0:C], start=True, stop=True).then_inc(f_mm, 1)

        def ve_setup(ve):
            steps = []

            def step(name, ins):
                steps.append(name)
                assert PRE[name] == len(steps)
                ins.then_inc(s_pre, 1)

            step("o_sum", ve.memset(o_sum[:, :], 0.0))
            step("o_sq", ve.memset(o_sq[:, :], 0.0))
            step("zeros", ve.memset(zeros[:, :, :], 0.0))
            step("base0", ve.memset(base_f, 0.0))
            step("acc0", ve.memset(acc[:, :, :], 0.0))
            ve.wait_ge(s_scalars, 16 * 3)
            step("dst_f", ve.tensor_copy(rel[:, :], rel[:, :].bitcast(I32)))
            ve.wait_ge(s_pre, PRE["dst_f"])
            step("base_f", ve.tensor_copy(base_f[0:1, :], base_i[:, :]))
            ve.wait_ge(s_weights, 16 * N_WEIGHT_LOADS)
            step("m4", ve.tensor_scalar(m4[:, 3 * C:4 * C], m4[:, 3 * C:4 * C], float(1.0 / np.sqrt(np.float32(3.0))), None, ALU.mult))
            step("bias0", ve.tensor_tensor(bias0[:, :], b12[:, 0, :], b12[:, 1, :], ALU.add))
            ve.wait_ge(s_prep_mm, 2)
            step("wc", ve.tensor_copy(wc[:, :, :], ps_edge[:, 0:2, 0:D]))
            ve.wait_ge(s_prep_mm, 3)
            bc = ps_edge[0:1, 2, 0:D]
            step("bc_hi", ve.tensor_copy(bc_parts[0:1, 0, :], bc))
            ve.wait_ge(s_pre, PRE["bc_hi"])
            step("bc_r1", ve.tensor_tensor(bc_rest[0:1, 0, :], bc, bc_parts[0:1, 0, :], ALU.subtract))
            ve.wait_ge(s_pre, PRE["bc_r1"])
            step("bc_mid", ve.tensor_copy(bc_parts[0:1, 1, :], bc_rest[0:1, 0, :]))
            ve.wait_ge(s_pre, PRE["bc_mid"])
            step("bc_r2", ve.tensor_tensor(bc_rest[0:1, 1, :], bc_rest[0:1, 0, :], bc_parts[0:1, 1, :], ALU.subtract))
            ve.wait_ge(s_pre, PRE["bc_r2"])
            step("bc_lo", ve.tensor_copy(bc_parts[0:1, 2, :], bc_rest[0:1, 1, :]))
            ve.wait_ge(s_prep_mm, 4)
            bases = ps_edge[:, 3, 0:(NI + 1) * BPAD].rearrange("p (i g) -> p i g", g=BPAD)
            for k, (t0, n) in enumerate(GROUPS):
                step(f"rel{k}", ve.tensor_tensor(
                    rel[:, :].rearrange("p (i t) -> p i t", t=TPI)[:, :, t0:t0 + n],
                    rel[:, :].rearrange("p (i t) -> p i t", t=TPI)[:, :, t0:t0 + n],
                    bases[:, (k + LAG) // NG:NI + (k + LAG) // NG, (k + LAG) % NG:(k + LAG) % NG + 1].broadcast_to([P, NI, n]), ALU.subtract))
            ve.wait_ge(s_pre, PRE[f"rel{NG - 1}"])
            step("rel_max", ve.tensor_reduce(fl[:, 0:1], rel[:, :], AX_X, ALU.max))
            step("rel_min", ve.tensor_reduce(fl[:, 1:2], rel[:, :], AX_X, ALU.min))
            ve.wait_ge(s_pre, PRE["rel_min"])
            step("over", ve.tensor_scalar(fl[:, 2:3], fl[:, 0:1], float(1 - WIN), None, ALU.add))
            step("under", ve.tensor_scalar(fl[:, 3:4], fl[:, 1:2], -1.0, None, ALU.mult))
            step("early", ve.tensor_tensor(early, early, ps_edge[:, 3, 0:(NI + 1) * BPAD], ALU.subtract))
            ve.wait_ge(s_pre, PRE["early"])
            step("early_max", ve.tensor_reduce(fl[:, 4:5], early, AX_X, ALU.max))
            ve.wait_ge(s_pre, PRE["early_max"])
            ve.tensor_reduce(flag_f[:, 0:1], fl[:, 2:5], AX_X, ALU.max).then_inc(s_flag_part, 1)
            for c in range(NB // CH):
                ve.wait_ge(s_x[c], 16)
            with ve.Fori(0, NB // CH) as c:
                ve.wait_ge(t_mv, c + 1)
                for j in range(CH):
                    pass_waits(ve)
                    ve.bn_stats(bn_c[:, j, :], x_all[:, bass.ds(c * CH + j, 1), :].rearrange("p a d -> p (a d)")).then_inc(bn_part, 1)
                ve.wait_ge(bn_part, (c + 1) * CH)
                pass_waits(ve)
                for j in range(CH):
                    ve.bn_aggr(mv_c[:, j, :], bn_c[:, j, :]).then_inc(mv_part, 1)
                ve.wait_ge(mv_part, (c + 1) * CH)
                pass_waits(ve)
                ve.tensor_copy(mv_all[:, bass.ds(c * CH, CH), :], mv_c[:, :, :]).then_inc(t_mv, 1)
            ve.wait_ge(s_root, 1)
            ve.reciprocal(stats_all[:, 1, :], stats_all[:, 0, :]).then_inc(s_scale, 1)
            ve.wait_ge(s_scale, 1)
            ve.scalar_tensor_tensor(out=stats_all[:, 2, :], in0=mv_all[:, :, 0], scalar=-1.0, in1=stats_all[:, 1, :],
                                    op0=ALU.mult, op1=ALU.mult).then_inc(s_scale, 1)
            with ve.Fori(0, NB // CH) as c:
                for j in range(CH):
                    ve.wait_ge(s_ph_t, c * CH + j + 1 + CH)
                    if j == 0:
                        ve.wait_ge(s_pstore_t, c * 16 + 16)
                    ve.tensor_copy(pt[:, j, :], tp_both(j)).then_inc(s_pht_copied, 1)
            ve.wait_ge(s_flag_all, 1)
            ve.tensor_copy(flag_i[:, :], flag_f[:, 1:2]).then_inc(s_flag, 1)

        def tp_both(j):
            return ps_edge[:, j % 4, 0:D]

        def ve_hot(ve, l, it, k, w, nw):
            t0, n = GROUPS[k]
            i = it - layer_its[l][0]
            if nw == 1:
                users = [k - NG] + [group_of(last_use(t, 8, TPI)) for t in range(t0, t0 + n) if l == 3]
                ve.wait_ge(summed, it * NG + (max(users) + 1 + NG))
                where = rel[:, bass.ds(i * TPI + t0, n)]
            else:
                g = (it * NG + k) * nw + w
                ve.wait_ge(summed, g + NG * nw)
                ve.wait_ge(wbase_done, g + (it * NG + k) + 2)
                ve.tensor_scalar(relw[:, 0:n], rel[:, bass.ds(i * TPI + t0, n)], wbase[:, 0:1], None,
                                 ALU.subtract).then_inc(relw_done, 1)
                ve.wait_ge(relw_done, g + 1)
                ve.tensor_scalar(wbase[:, :], wbase[:, :], float(WIN), None, ALU.add).then_inc(wbase_done, 1)
                where = relw[:, 0:n]
            ready = hot_ready if l in (1, 2) else hot_part
            ve.tensor_tensor(hot[:, t0:t0 + n, :], iota[:, :].unsqueeze(1).broadcast_to([P, n, WIN]),
                             where.unsqueeze(2).broadcast_to([P, n, WIN]), ALU.is_equal).then_inc(ready, 1)
            q = i * NG + k + (0 if l == 0 else NI * NG)
            part = q * nw + (w + 1)
            if l == 0:
                ve.wait_ge(hot_part, part)
                ve.tensor_tensor(hot[:, t0:t0 + n, :], hot[:, t0:t0 + n, :],
                                 ew[:, bass.ds(i * TPI + t0, n)].unsqueeze(2).broadcast_to([P, n, WIN]),
                                 ALU.mult).then_inc(hot_ready, 1)
            if l == 3:
                ve.wait_ge(sh_in[k // 3], i * 16 + 16)
                ve.wait_ge(hot_part, part)
                for t in range(t0, t0 + n):
                    ins = ve.tensor_tensor(hot4[:, t % 8, :, :], hot[:, t:t + 1, :].broadcast_to([P, 4, WIN]),
                                           sh[:, t, :].unsqueeze(2).broadcast_to([P, 4, WIN]), ALU.mult)
                ins.then_inc(hot_ready, 1)

        def ve_add(ve, l, it, k, w, nw, start):
            if nw == 1:
                g = it * NG + k
                ve.wait_ge(summed, g + 1 + NG)
                ve.wait_ge(added, g + NG)
            else:
                g = (it * NG + k) * nw + w
                ve.wait_ge(summed, g + 1 + NG * nw)
                ve.wait_ge(added, g + NG * nw)
            ve.tensor_tensor(acc[:, :, bass.ds(start, WIN)], acc[:, :, bass.ds(start, WIN)], ps_acc(k),
                             ALU.add).then_inc(added, 1)

        def ve_msg(ve, i, it, k):
            t0, n = GROUPS[k]
            ve.wait_ge(rows_in[k], (it + 1) * 16 * n)
            for t in range(t0, t0 + n):
                ve.wait_ge(z_done, i * TPI + t + 1 + TPI)
                ve.scalar_tensor_tensor(out=rows[:, t, :], in0=ps_z[:, t % 2, :], scalar=ew[:, bass.ds(i * TPI + t, 1)],
                                        in1=rows[:, t, :], op0=ALU.mult, op1=ALU.add).then_inc(z_read, 1)

        def ve_u(ve, i, it, k, nw):
            t0, n = GROUPS[k]
            ve.wait_ge(rows_in[k], (it + 1) * 16 * n)
            for t in range(t0, t0 + n):
                ve.wait_ge(summed, (it * NG + group_of(last_use(t, 8, TPI)) + 1 + NG) * nw)
                ve.wait_ge(tpw_done, i * TPI + t + 1 + TPI)
                tp = ps_tpw[:, t % 4, :].rearrange("p (k c) -> p k c", k=4)
                x = rows[:, t, :].rearrange("p (k c) -> p k c", k=4)
                u = u_ring[:, t % 8, :, :]
                ve.tensor_tensor(u[:, 0:8:7, :], tp[:, 0:2, :], x[:, 0:1, :].broadcast_to([P, 2, C]), ALU.mult)
                ve.tensor_tensor(u[:, 1:7, :].rearrange("p (k x) c -> p k x c", k=2),
                                 tp[:, 2:4, :].unsqueeze(2).broadcast_to([P, 2, 3, C]),
                                 x[:, 1:4, :].unsqueeze(1).broadcast_to([P, 2, 3, C]), ALU.mult).then_inc(u_done, 1)

        def ve_sums_in(ve, l, b, nw):
            n = b + (l * NB + 1)
            cols = acc[:, :, bass.ds(b * P, P)]
            if nw == 1 and not (isinstance(b, int) and b == NB - 1):
                ve.wait_ge(added, (b + (l * NI + 1)) * NG + (NODE_AT + NG))
            else:
                ve.wait_ge(added, ((l + 1) * NI * NG + NG) * nw)
            ve.wait_ge(ht_in, n * 16)
            ve.wait_ge(n_mm, n)
            pass_waits(ve)
            if l == 0:
                ins = ve.scalar_tensor_tensor(out=q_t[:, :, :], in0=h_t[:, :, :], scalar=1.0, in1=cols, op0=ALU.add, op1=ALU.mult)
            elif l == 2:
                ins = ve.tensor_tensor(q_t[:, :, :], h_t[:, :, :], cols, ALU.add)
            else:
                ins = ve.tensor_copy(q_t[:, :, :], cols)
            ins.then_inc(q_ready, 1)
            if l < 3:
                ve.wait_ge(q_ready, n)
                pass_waits(ve)
                ve.tensor_copy(cols, zeros[:, :, :]).then_inc(acc_free, 1)

        def block_of(b):
            return x_all[:, bass.ds(b, 1), :].rearrange("p a d -> p (a d)")

        def ve_stats(ve, l, b):
            n = b + (l * NB + 1)
            ve.wait_ge(x_new, n + 1)
            pass_waits(ve)
            ve.bn_stats(small[:, 8:14], block_of(b)).then_inc(t_bn, 1)
            ve.wait_ge(t_bn, n)
            pass_waits(ve)
            ve.bn_aggr(small[:, 14:16], small[:, 8:14]).then_inc(t_mv, 1)

        def ve_scale(ve, l, b):
            n = b + (l * NB + 1)
            ve.wait_ge(t_root, n)
            ve.reciprocal(small[:, 17:18], small[:, 16:17]).then_inc(t_rstd, 1)
            ve.wait_ge(t_rstd, n)
            ve.scalar_tensor_tensor(out=small[:, 18:19], in0=small[:, 14:15], scalar=-1.0, in1=small[:, 17:18],
                                    op0=ALU.mult, op1=ALU.mult).then_inc(t_scale, 1)

        def ve_table(ve, l, b):
            n = b + (l * NB + 1)
            ve.wait_ge(t_h, n)
            ve.wait_ge(table_out, n * 16)
            ve.tensor_tensor(t_out[:, :], h_new[:, :], R("b_le"), ALU.add).then_inc(t_lb, 1)

        t_lb = sem("t_lb")

        def ve_first(ve, l, b):
            no = ps_node[:, 0, :]
            ve.wait_ge(n_mm, b + (l * NB + 2))
            if l == 0:
                ve.tensor_tensor(y[:, :], no, bias0[:, :], ALU.add).then_inc(n_y, 1)
                ve.wait_ge(n_y, b + 1)
                ve.scalar_tensor_tensor(out=y2[:, :], in0=y[:, :], scalar=LEAKY, in1=y[:, :], op0=ALU.mult,
                                        op1=ALU.max).then_inc(n_lk, 1)
            if l == 1:
                xb = block_of(b)
                ve.scalar_tensor_tensor(out=xb, in0=no, scalar=0.0, in1=xb, op0=ALU.max, op1=ALU.add).then_inc(x_new, 1)
                ve_stats(ve, l, b)
            if l == 2:
                ve.tensor_tensor(y[:, :], no, R("b_g1"), ALU.add).then_inc(g_y, 1)
                ve.wait_ge(g_y, b + 1)
                ve.bn_stats(small[:, 8:14], y[:, :]).then_inc(g_bn, 1)
                ve.wait_ge(g_bn, b + 1)
                pass_waits(ve)
                ve.bn_aggr(small[:, 24:26], small[:, 8:14]).then_inc(g_mv, 1)

        def ve_norm(ve, l, b):
            xb = block_of(b)
            ve.wait_ge(n_root, b + 1)
            ve.tensor_scalar(small[:, 22:23], small[:, 21:22], NORM_EPS, None, ALU.max).then_inc(n_mx, 1)
            ve.wait_ge(n_mx, b + 1)
            ve.reciprocal(small[:, 23:24], small[:, 22:23]).then_inc(n_rn, 1)
            ve.wait_ge(n_rn, b + 1)
            ve.scalar_tensor_tensor(out=xb, in0=y2[:, :], scalar=small[:, 23:24], in1=xb, op0=ALU.mult,
                                    op1=ALU.add).then_inc(x_new, 1)
            ve_stats(ve, l, b)

        def ve_layer_norm(ve, l, b):
            ve.wait_ge(g_root, b + 1)
            ve.reciprocal(small[:, 27:28], small[:, 26:27]).then_inc(g_rstd, 1)
            ve.scalar_tensor_tensor(out=y[:, :], in0=y[:, :], scalar=small[:, 24:25], in1=R("ln_g"), op0=ALU.subtract,
                                    op1=ALU.mult).then_inc(g_lg, 1)
            ve.wait_ge(g_rstd, b + 1)
            ve.wait_ge(g_lg, b + 1)
            ve.scalar_tensor_tensor(out=y2[:, :], in0=y[:, :], scalar=small[:, 27:28], in1=R("ln_b"), op0=ALU.mult,
                                    op1=ALU.add).then_inc(g_lb, 1)

        def ve_second(ve, l, b):
            xb = block_of(b)
            ve.wait_ge(g_mm2, b + 1)
            ve.tensor_tensor(y[:, :], ps_node[:, 1, :], R("b_g2"), ALU.add).then_inc(g_x1, 1)
            ve.wait_ge(g_x1, b + 2)
            ve.tensor_tensor(xb, xb, y[:, :], ALU.add).then_inc(x_new, 1)
            ve_stats(ve, l, b)

        g_y = sem("g_y")

        def ve_poly(ve, l, b):
            count = [0]

            def step(ins):
                count[0] += 1
                ins.then_inc(o_step, 1)
                ve.wait_ge(o_step, b * POLY + count[0])

            a0 = y[:, 0:C]
            a0b = a0.unsqueeze(1).broadcast_to([P, 2, C])
            a1 = y[:, C:D].rearrange("p (x c) -> p x c", x=3)
            pairs = [R(n).rearrange("p (j c) -> p j c", c=C) for n in ("wc0a", "wc0b", "wc1")]
            c3, c1 = pairs[0][:, 0:2, :], pairs[0][:, 2:4, :]
            c0, cv = pairs[1][:, 0:2, :], pairs[1][:, 2:4, :]
            w2 = pairs[2][:, 0, :]
            ve.wait_ge(o_acopy, b + 2)
            sq = y2[:, C:D].rearrange("p (x c) -> p x c", x=3)
            ve.wait_ge(o_tp, b + 1)
            step(ve.tensor_tensor(sq, a1, a1, ALU.mult))
            step(ve.tensor_tensor(vv[:, 1, :], sq[:, 0, :], sq[:, 1, :], ALU.add))
            step(ve.tensor_tensor(vv[:, 0, :], vv[:, 1, :], sq[:, 2, :], ALU.add))
            step(ve.tensor_tensor(poly[:, :, :], c3, a0b, ALU.mult))
            step(ve.tensor_tensor(poly[:, :, :], poly[:, :, :], c1, ALU.add))
            step(ve.tensor_tensor(poly[:, :, :], poly[:, :, :], a0b, ALU.mult))
            step(ve.tensor_tensor(poly[:, :, :], poly[:, :, :], c0, ALU.add))
            step(ve.tensor_tensor(poly2[:, :, :], cv, vv[:, 0:1, :].broadcast_to([P, 2, C]), ALU.mult))
            step(ve.tensor_tensor(poly[:, :, :], poly[:, :, :], poly2[:, :, :], ALU.add))
            step(ve.tensor_tensor(poly2[:, 0, :], poly[:, 0, :], a0, ALU.mult))
            step(ve.tensor_tensor(poly2[:, 1, :], w2, vv[:, 0, :], ALU.mult))
            step(ve.tensor_tensor(y2[:, 0:C], poly2[:, 0, :], poly2[:, 1, :], ALU.add))
            ve.tensor_tensor(sq, a1, poly[:, 1:2, :].broadcast_to([P, 3, C]), ALU.mult).then_inc(o_b, 1)

        def ve_node_sums(ve, l, b):
            m = LAST if isinstance(b, int) and b == NB - 1 else P
            ve.wait_ge(o_copied, b + 1)
            ve.wait_ge(o_summed, (b + 1) * 2)
            ve.tensor_tensor(o_sum[0:m, :], o_sum[0:m, :], t_out[0:m, :], ALU.add).then_inc(o_summed, 1)
            ve.wait_ge(o_sqd, b + 1)
            ve.tensor_tensor(o_sq[0:m, :], o_sq[0:m, :], h_new[0:m, :], ALU.add).then_inc(o_summed, 1)

        def ve_parts(l, nw):
            def sums_in(ve, l, b):
                ve_sums_in(ve, l, b, nw)

            return [[(7, sums_in), (9, ve_first), (11, ve_norm), (13, ve_scale)],
                    [(7, sums_in), (9, ve_first), (11, ve_scale), (13, ve_table)],
                    [(7, sums_in), (9, ve_first), (11, ve_layer_norm), (15, ve_second), (16, ve_scale)],
                    [(7, sums_in), (10, ve_poly), (16, ve_node_sums)]][l]

        def load_starts(ve, i, n):
            regs = ve_base_regs
            ve.reg_load(regs[0:min(n, 4)], base_i[0:1, bass.ds(i * BPAD, min(n, 4))])
            if n > 4:
                ve.reg_load(regs[4:n], base_i[0:1, bass.ds(i * BPAD + 4, n - 4)])
            return [ve.snap(r, min_val=0, max_val=NCOL - WIN) for r in regs[0:n]]

        def ve_edges(ve, l, it, nw, node, first):
            i = it - layer_its[l][0]
            if nw > 1:
                for k in range(NG):
                    if l == 2:
                        ve_msg(ve, i, it, k)
                    if l == 3:
                        ve_u(ve, i, it, k, nw)
                    g = it * NG + k
                    ve.wait_ge(wbase_done, g * (nw + 1) + 1)
                    ve.memset(wbase[:, :], 0.0).then_inc(wbase_done, 1)
                    with ve.Fori(0, nw) as w:
                        ve_hot(ve, l, it, k, w, nw)
                        ve_add(ve, l, it, k, w, nw, w * WIN)
                return
            starts = load_starts(ve, i, NG)
            if l < 3:
                ve_hot(ve, l, it, 0, 0, 1)
            for k in range(NG):
                if l < 3 and k + 1 < NG:
                    ve_hot(ve, l, it, k + 1, 0, 1)
                if l == 2:
                    ve_msg(ve, i, it, k)
                if l == 3:
                    ve_u(ve, i, it, k, 1)
                node(2 * k)
                if l == 3:
                    ve_hot(ve, l, it, k, 0, 1)
                if k >= LAG or not first:
                    ve_add(ve, l, it, k - LAG, 0, 1, starts[k])
                node(2 * k + 1)

        def ve_close(ve, l):
            starts = load_starts(ve, NI, LAG)
            for k in range(LAG):
                ve_add(ve, l, layer_its[l][1], k - LAG, 0, 1, starts[k])

        def ve_final(ve):
            o4 = acc[:, :, 0:NB * P].rearrange("p h (b c) -> p b h c", c=P)
            o0 = o4[:, :, 0, 0:C]
            done = []

            def step(name, ins):
                done.append(name)
                assert FIN[name] == len(done)
                ins.then_inc(f_step, 1)
                ve.wait_ge(f_step, len(done))

            inv_n = float(np.float32(1.0) / np.float32(n_nodes))
            mu, a0, b0, s1 = fin[:, 0, 0:C], fin[:, 1, 0:C], fin[:, 1, C:2 * C], fin[:, 3, 0:C]
            gam0, bet0, gam1 = R("norm")[:, 0:C], R("norm")[:, C:2 * C], R("norm")[:, 2 * C:3 * C]
            ve.wait_ge(o_kept, NB + 1)
            ve.wait_ge(f_mm, 1)
            step("mu", ve.tensor_scalar(mu, ps_edge[:, 0, 0:C], inv_n, None, ALU.mult))
            step("centre", ve.tensor_tensor(o0, o0, mu.unsqueeze(1).broadcast_to([P, NB, C]), ALU.subtract))
            sq = rows[:, 0:-(-NB * C // D), :].rearrange("p t d -> p (t d)")[:, 0:NB * C].rearrange("p (b c) -> p b c", c=C)
            step("square", ve.tensor_tensor(sq, o0, o0, ALU.mult))
            step("var_sum", ve.tensor_reduce(fin[:, 2, 0:C], sq[:, 0:NB - 1, :].rearrange("p b c -> p c b"), AX_X, ALU.add))
            step("var_part", ve.tensor_tensor(fin[0:LAST, 2, 0:C], fin[0:LAST, 2, 0:C], sq[0:LAST, NB - 1, :], ALU.add))
            step("nrm", ve.tensor_reduce(fin[:, 4, C:2 * C], ps_edge[:, 1, C:D].rearrange("p (c x) -> p c x", x=3), AX_X, ALU.add))
            step("nrm_mean", ve.tensor_scalar(fin[:, 4, C:2 * C], fin[:, 4, C:2 * C], float(1.0 / (3.0 * n_nodes)), None, ALU.mult))
            ve.wait_ge(f_mm, 2)
            step("var_mean", ve.tensor_scalar(fin[:, 4, 0:C], ps_edge[:, 2, 0:C], inv_n, None, ALU.mult))
            ve.wait_ge(f_root, 1)
            step("rstd", ve.reciprocal(fin[:, 6, 0:2 * C], fin[:, 5, 0:2 * C]))
            step("a0", ve.tensor_tensor(a0, fin[:, 6, 0:C], gam0, ALU.mult))
            step("s1", ve.tensor_tensor(s1, fin[:, 6, C:2 * C], gam1, ALU.mult))
            step("n0", ve.tensor_tensor(o0, o0, a0.unsqueeze(1).broadcast_to([P, NB, C]), ALU.mult))
            step("x0", ve.tensor_tensor(x_all[:, :, 0:C], x_all[:, :, 0:C], o0, ALU.add))
            step("x0b", ve.tensor_tensor(x_all[:, :, 0:C], x_all[:, :, 0:C], bet0.unsqueeze(1).broadcast_to([P, NB, C]), ALU.add))
            step("s1x", ve.tensor_copy(fin[:, 7, 0:3 * C].rearrange("p (c x) -> p c x", x=3), s1.unsqueeze(2).broadcast_to([P, C, 3])))
            o1a, o1b = o4[:, :, 0, C:P], o4[:, :, 1, :]
            sa, sb_ = fin[:, 7, 0:C], fin[:, 7, C:3 * C]
            step("n1a", ve.tensor_tensor(o1a, o1a, sa.unsqueeze(1).broadcast_to([P, NB, C]), ALU.mult))
            step("n1b", ve.tensor_tensor(o1b, o1b, sb_.unsqueeze(1).broadcast_to([P, NB, P]), ALU.mult))
            step("x1a", ve.tensor_tensor(x_all[:, :, C:P], x_all[:, :, C:P], o1a, ALU.add))
            step("x1b", ve.tensor_tensor(x_all[:, :, P:D], x_all[:, :, P:D], o1b, ALU.add))

        def act_setup(act):
            act.wait_ge(s_const, 7)
            act.wait_ge(t_mv, NB // CH + 1)
            act.activation(stats_all[:, 0, :], mv_all[:, :, 1], ACT.Sqrt, bias=eps[:, 0:1]).then_inc(s_root, 1)
            act.wait_ge(s_scale, 2)
            with act.Fori(0, NB // CH) as c:
                act.wait_ge(s_pstore, c * 16 + 16)
                act.wait_ge(s_ph_t, c * CH + CH)
                for j in range(CH):
                    b = c * CH + j
                    act.activation(rows[:, j, :], x_all[:, bass.ds(b, 1), :].rearrange("p a d -> p (a d)"), ACT.Relu,
                                   bias=stats_all[:, 2, bass.ds(b, 1)], scale=stats_all[:, 1, bass.ds(b, 1)]).then_inc(s_ph, 1)
                act.wait_ge(s_ph, c * CH + CH)
                act.dma_start(table[0][bass.ds(c * (CH * P), CH * P), :].rearrange("(b p) d -> p b d", p=P),
                              rows[:, 0:CH, :]).then_inc(s_pstore, 16)
                act.wait_ge(s_pht_copied, c * CH + CH + CH)
                act.dma_start(h_t_dram[0][bass.ds(c * CH, CH), :, :].rearrange("b p d -> p b d"),
                              pt[:, 0:CH, :]).then_inc(s_pstore_t, 16)

        def act_mlp(act, l, i, stage, m):
            q = mlp_number(l, i, m)
            act.wait_ge(mlp_mm[stage], q + 1 + (2 if stage == 0 else 0))
            dst = (ra, rb)[stage][:, m % 2, :] if stage < 2 else rc[:, m, :]
            if stage == 2:
                act.wait_ge(r3_out[m], i * 16 + 16)
            act.activation(dst, ps_edge[:, m % 2, 0:MW], ACT.Silu).then_inc(mlp_act[stage], 1)
            if stage == 2:
                act.wait_ge(mlp_act[2], q + 1 + 2)
                act.dma_start(r3_dram[bass.ds(i, 1), :, m * MW:(m + 1) * MW].rearrange("a p n -> p (a n)"),
                              rc[:, m, :]).then_inc(r3_out[m], 16)

        def act_relu_a(act, i, k):
            t0, n = GROUPS[k]
            for c in range(2):
                act.wait_ge(a_done, (i * NG + k) * 2 + c + 1 + 2 * NG)
                u = last_use(k, 2, NG)
                ug = u % NG
                tiles = GROUPS[ug][0] + GROUPS[ug][1] - (TPI if u < 0 else 0)
                act.wait_ge(z_done, i * TPI + tiles + TPI)
                act.activation(r_t[:, k % 2, c, 0:n * P], ps_edge[:, c, 0:n * P], ACT.Relu).then_inc(r_done, 1)

        def act_relu_msg(act, i, k):
            t0, n = GROUPS[k]
            act.wait_ge(z_read, i * TPI + t0 + n + TPI)
            act.activation(rows[:, t0:t0 + n, :], rows[:, t0:t0 + n, :], ACT.Relu).then_inc(msg_done, 1)

        def act_load_ht(act, l, b):
            n = b + (l * NB + 1)
            act.wait_ge(n_mm, n)
            if l == 3:
                act.wait_ge(o_mm, b + 1)
            act.dma_start(h_t[:, :, :].rearrange("p c n -> p (c n)"),
                          h_t_dram[l][bass.ds(b, 1), :, :].rearrange("a p d -> p (a d)")).then_inc(ht_in, 16)

        def act_square(act, l, b):
            act.wait_ge(n_lk, b + 1)
            act.activation(y[:, :], y2[:, :], ACT.Square, accum_out=small[:, 20:21]).then_inc(n_ss, 1)
            act.wait_ge(n_ss, b + 1)
            act.activation(small[:, 21:22], small[:, 20:21], ACT.Sqrt).then_inc(n_root, 1)

        def act_g_root(act, l, b):
            act.wait_ge(g_mv, b + 1)
            act.activation(small[:, 26:27], small[:, 25:26], ACT.Sqrt, bias=eps[:, 0:1]).then_inc(g_root, 1)

        def act_y_t(act, l, b):
            if l == 2:
                act.wait_ge(g_tp, b + 1)
                act.activation(y_t[:, :, :], ps_tp[:, 2:4, :], ACT.Relu).then_inc(g_yt, 1)
            else:
                act.wait_ge(o_tp, b + 2)
                act.copy(y_t[:, :, :], ps_tp[:, 2:4, :]).then_inc(o_bt, 1)

        def act_a(act, l, b):
            act.wait_ge(n_mm, b + (3 * NB + 2))
            act.copy(y[:, :], ps_node[:, 0, :]).then_inc(o_acopy, 1)

        def act_root(act, l, b):
            act.wait_ge(t_mv, b + (l * NB + 1) + (NB // CH + 1))
            act.activation(small[:, 16:17], small[:, 15:16], ACT.Sqrt, bias=eps[:, 0:1]).then_inc(t_root, 1)

        def act_h(act, l, b):
            n = b + (l * NB + 1)
            act.wait_ge(t_scale, n)
            act.wait_ge(table_out, n * 16)
            act.activation(h_new[:, :], block_of(b), ACT.Relu, bias=small[:, 18:19], scale=small[:, 17:18]).then_inc(t_h, 1)
            if l == 0:
                act.wait_ge(t_h, n)
                act.dma_start(table[1][bass.ds(b * P, P), :], h_new[:, :]).then_inc(table_out, 16)

        def act_h_t(act, l, b):
            n = b + (l * NB + 1)
            if l == 1:
                act.wait_ge(t_lb, b + 1)
                act.dma_start(table[2][bass.ds(b * P, P), :], t_out[:, :]).then_inc(table_out, 16)
            act.wait_ge(t_tp, n)
            act.wait_ge(ht_out, n * 16)
            act.copy(h_new_t[:, :, :], ps_tp[:, 0:2, :]).then_inc(t_ht, 1)
            act.wait_ge(t_ht, n + 1)
            act.dma_start(h_t_dram[l + 1][bass.ds(b, 1), :, :].rearrange("a p d -> p (a d)"),
                          h_new_t[:, :, :].rearrange("p c n -> p (c n)")).then_inc(ht_out, 16)

        def act_up(act, l, b):
            act.wait_ge(t_tab, b + 1)
            act.copy(t_out[:, :], ps_node[:, 0, :]).then_inc(t_up, 1)
            act.wait_ge(t_up, b + 2)
            act.dma_start(table[3][bass.ds(b * P, P), :], t_out[:, :]).then_inc(table_out, 16)

        def act_o(act, l, b):
            act.wait_ge(o_mm, b + 2)
            act.wait_ge(o_summed, (b + 1) * 2)
            act.copy(t_out[:, :], ps_node[:, 1, :]).then_inc(o_copied, 1)
            act.activation(h_new[:, :], ps_node[:, 1, :], ACT.Square).then_inc(o_sqd, 1)
            act.copy(acc[:, :, bass.ds(b * P, P)], ps_node[:, 1, :].rearrange("p (h c) -> p h c", h=2)).then_inc(o_kept, 1)

        ACT_PARTS = [[(4, act_load_ht), (10, act_square), (12, act_root), (14, act_h), (16, act_h_t)],
                     [(4, act_load_ht), (10, act_root), (12, act_h), (14, act_h_t)],
                     [(4, act_load_ht), (10, act_g_root), (13, act_y_t), (15, act_root), (16, act_h), (17, act_h_t), (18, act_up)],
                     [(4, act_load_ht), (9, act_a), (13, act_y_t), (15, act_o)]]

        def act_edges(act, l, it, nw, node, first):
            i = it - layer_its[l][0]
            if l == 2 and nw == 1:
                act_relu_a(act, i, 0)
            for k in range(NG):
                for stage, m in MLP_AT[l][k]:
                    act_mlp(act, l, i, stage, m)
                if l == 2:
                    if nw > 1:
                        act_relu_a(act, i, k)
                    elif k + 1 < NG:
                        act_relu_a(act, i, k + 1)
                    if nw == 1:
                        node(2 * k)
                    act_relu_msg(act, i, k)
                elif nw == 1:
                    node(2 * k)
                if nw == 1:
                    node(2 * k + 1)

        def act_layer(act, l, nw):
            if l:
                act.wait_ge(ht_out, 16 * l * NB + 16)
            else:
                act.wait_ge(s_pstore_t, 16 * (NB // CH) + 16)
            if l == 2:
                for m in range(MB):
                    act.wait_ge(r3_out[m], 16 * NI + 16)
            if l == 3:
                act.wait_ge(table_out, 16 * 3 * NB + 16)
            run_layer(act, l, nw, act_edges, ACT_PARTS[l])

        def act_final(act):
            act.wait_ge(f_step, FIN["var_mean"])
            act.activation(fin[:, 5, 0:2 * C], fin[:, 4, 0:2 * C], ACT.Sqrt, bias=eps[:, 0:1]).then_inc(f_root, 1)

        taken = [0]

        def carve(*dims):
            n = int(np.prod(dims))
            piece = arena[:, taken[0]:taken[0] + n]
            taken[0] += n + n % 2
            return piece if len(dims) == 1 else piece.rearrange("p (a b) -> p a b", a=dims[0])

        early = carve((NI + 1) * BPAD)
        base_f = carve((NI + 1) * BPAD)
        bn_c = carve(CH, 6)
        mv_c = carve(CH, 2)
        mv_all = carve(NB, 2)
        stats_all = carve(3, NB)
        pt = carve(CH, D)
        w_e2 = carve(2, D)
        w_le = carve(2, D)
        b12 = carve(2, D)
        be2 = carve(2)
        bc_rest = carve(2, D)
        bc_parts = carve(3, D // 2).bitcast(BF16)
        iota_i = sb("iota_i", [P, WIN], I32)
        spare = sb("spare", [1, 8])
        fl = sb("fl", [P, 8])
        flag_f = sb("flag_f", [P, 2])
        s_pol = sem("s_pol")
        s_w3 = sem("s_w3")
        s_dst_again = sem("s_dst_again")
        gate_step = sem("gate_step")
        dst_step = sem("dst_step")
        sh_in = [sem("sh_in0"), sem("sh_in1")]
        passed = sem("passed")
        bn_part = sem("bn_part")
        mv_part = sem("mv_part")
        early_in = sem("early_in")
        raw_ones = sem("raw_ones")
        ve_base_regs = []

        PRE = {n: i + 1 for i, n in enumerate(
            ["o_sum", "o_sq", "zeros", "base0", "acc0", "dst_f", "base_f", "m4", "bias0", "wc", "bc_hi", "bc_r1",
             "bc_mid", "bc_r2", "bc_lo"] + [f"rel{k}" for k in range(NG)] +
            ["rel_max", "rel_min", "over", "under", "early", "early_max"])}
        FIN = {n: i + 1 for i, n in enumerate(
            ["mu", "centre", "square", "var_sum", "var_part", "nrm", "nrm_mean", "var_mean", "rstd", "a0", "s1", "n0", "x0",
             "x0b", "s1x", "n1a", "n1b", "x1a", "x1b"])}
        POLY = 12

        block = ctx.enter_context(nc.Block())
        paths = ((1, "a window for each group"), (ALLWIN, "all windows"))

        def credits(nw):
            return {
                "pe": [(summed, NG * nw), (a_done, 2 * NG), (tpw_done, TPI), (z_done, TPI), (mlp_mm[0], 2), (n_mm, 1), (o_tp, 1), (o_mm, 1)],
                "ve": [(added, NG * nw), (z_read, TPI), (u_done, TPI), (x_new, 1), (wbase_done, 1), (g_x1, 1), (o_summed, 2)],
                "act": [(r_done, 2), (mlp_act[2], 2), (t_up, 1), (o_acopy, 1), (g_yt, 1), (o_bt, 1), (t_ht, 1), (o_kept, 1)],
            }

        def branch(eng, program):
            eng.wait_ge(s_flag, 1)
            reg = eng.value_load(flag_i[0:1, 0:1], min_val=-(1 << 24), max_val=1 << 24)
            with eng.If(reg < 1):
                program(1)
            with eng.Else():
                program(ALLWIN)

        @block.sync
        def _(sp):
            sp.dma_start(early, io["early"].partition_broadcast(P)).then_inc(early_in, 16)
            for j, s in enumerate([s_pstore, s_pstore_t, table_out, ht_out, *r3_out]):
                sp.dma_start(spare[0:1, j:j + 1], io["early"][0:1]).then_inc(s, 16)
            sp_setup(sp)

            def program(nw):
                if nw > 1:
                    sp.dma_start(rel[:, :].bitcast(I32), io["dst"]).then_inc(s_dst_again, 16)
                for l in range(4):
                    sp_layer(sp, l, nw)

            branch(sp, program)
            sp.wait_ge(f_step, FIN["x1b"])
            sp.dma_start(io["out"].rearrange("(b p) d -> p b d", p=P), x_all[:, :, :]).then_inc(s_out, 16)
            sp.wait_ge(s_out, 16)

        @block.gpsimd
        def _(pool):
            pool_setup(pool)

            def program(nw):
                for l in range(4):
                    pool_layer(pool, l, nw)

            branch(pool, program)

        @block.tensor
        def _(pe):
            pe_setup(pe)

            def program(nw):
                for s, v in credits(nw)["pe"]:
                    pe.sem_inc(s, v)
                for l in range(4):
                    if l == 2:
                        pe.wait_ge(s_bc, 48)
                        pe.wait_ge(raw_ones, 1)
                    if l == 3:
                        pe.wait_ge(t_up, NB + 1)
                        pe.wait_ge(s_w3, 48)
                    run_layer(pe, l, nw, pe_edges, PE_PARTS[l], pe_close)

            branch(pe, program)
            pe_final(pe)

        @block.vector
        def _(ve):
            ve.sem_inc(s_pht_copied, CH)
            ve.sem_inc(t_mv, 1)
            ve.wait_ge(early_in, 16)
            ve_setup(ve)
            ve_base_regs.extend(ve.alloc_register(f"window_start{k}") for k in range(NG))

            def program(nw):
                for s, v in credits(nw)["ve"]:
                    ve.sem_inc(s, v)
                if nw > 1:
                    ve.wait_ge(s_dst_again, 16)
                    ve.tensor_copy(rel[:, :], rel[:, :].bitcast(I32)).then_inc(dst_step, 1)
                    ve.wait_ge(dst_step, 1)

                for l in range(4):
                    if l == 2:
                        ve.wait_ge(s_pol, 16)
                        ve.tensor_scalar(ew[:, :], ew[:, :], 0.0, 1.0, ALU.max, ALU.min).then_inc(gate_step, 1)
                        ve.wait_ge(gate_step, 1)
                        ve.tensor_scalar(ew[:, :], ew[:, :], 0.01, None, ALU.add).then_inc(gate_step, 1)
                        ve.wait_ge(gate_step, 2)
                        ve.wait_ge(r3_out[0], 16 * NI + 16)
                        ve.wait_ge(r3_out[1], 16 * NI + 16)
                        ve.wait_ge(r3_out[2], 16 * NI + 16)
                        ve.memset(raw[C:C + 1, :], 1.0).then_inc(raw_ones, 1)
                    run_layer(ve, l, nw, ve_edges, ve_parts(l, nw), ve_close)

            branch(ve, program)
            ve_final(ve)

        @block.scalar
        def _(act):
            act.sem_inc(s_ph_t, CH)
            act_setup(act)

            def program(nw):
                for s, v in credits(nw)["act"]:
                    act.sem_inc(s, v)
                for l in range(4):
                    act_layer(act, l, nw)

            branch(act, program)
            act_final(act)


def layouts(a, n_nodes, n_edges):
    f = {k: np.asarray(v) for k, v in a.items()}
    NB, NI = shapes(n_nodes, n_edges)
    ep = NI * TPI * P

    def edges(v, fill=0):
        out = np.full((ep,) + v.shape[1:], fill, v.dtype)
        out[:n_edges] = v
        return out

    def tiles(v):
        return np.ascontiguousarray(np.moveaxis(v.reshape((NI * TPI, P) + v.shape[1:]), 0, 1))

    d = {}
    x = np.zeros((NB * P, D), np.float32)
    x[:n_nodes] = f["x"]
    d["x"] = x
    src = edges(f["src"])
    dst = edges(f["dst"], n_nodes)
    d["src"], d["dst"] = tiles(src), tiles(dst)
    base = np.zeros((NI + 1, BPAD), np.int32)
    early = np.zeros((NI + 1, BPAD), np.float32)
    for k, (t0, n) in enumerate(GROUPS):
        row, slot = (k + LAG) // NG, (k + LAG) % NG
        base[row:NI + row, slot] = dst.reshape(NI, TPI, P)[:, t0, 0]
        early[row:NI + row, slot] = np.maximum(0, P * (np.arange(NI) - (0 if k >= NODE_AT else 1)))
    d["base"] = base.reshape(1, (NI + 1) * BPAD)
    d["early"] = early.reshape((NI + 1) * BPAD)
    d["ew"] = tiles(edges(f["edge_weight"]))
    d["sh"] = tiles(edges(f["edge_attr_4"]))
    d["pol"] = tiles(edges(np.ascontiguousarray(f["edge_attr_65"][:, 0])))
    raw = edges(np.ascontiguousarray(f["edge_attr_65"][:, 1:]))
    d["raw"] = np.ascontiguousarray(raw.reshape(NI, TPI * P, C).transpose(0, 2, 1))
    rbf = np.zeros((NI, TPI + 1, P, 16), np.float32)
    rbf[:, :TPI] = edges(f["edge_attr_16"]).reshape(NI, TPI, P, 16)
    d["rbf"] = np.ascontiguousarray(rbf.reshape(NI, 9, 2, P, 16).transpose(0, 2, 4, 1, 3)).reshape(NI, 32, 9 * P)
    L0, L1, L2, L3 = "L0_gnn_", "L1_gnn_", "L2_gnn_", "L3_gnn_"

    def blocks(w0, w1, rows_mixed, cols_mixed):
        m = np.zeros((D, D), np.float32)
        m[:C, :C] = w0
        for q in range(3):
            r = C + q + 3 * np.arange(C) if rows_mixed else C + C * q + np.arange(C)
            c = C + q + 3 * np.arange(C) if cols_mixed else C + C * q + np.arange(C)
            m[np.ix_(r, c)] = w1
        return m

    by_name = {
        "l0_w1": f[L0 + "W1"].T, "l0_w2": f[L0 + "W2"].T, "l1_w1": f[L1 + "W1"].T, "l1_w2": f[L1 + "W2"].T,
        "e2": f[L2 + "W_e2"], "le": f[L2 + "W_le"].T, "g1": f[L2 + "W_g1"].T, "g2": f[L2 + "W_g2"].T,
        "up": blocks(f[L3 + "W_up0"], f[L3 + "W_up1"], True, False),
        "lin": blocks(f[L3 + "W_lin0"], f[L3 + "W_lin1"], False, False),
        "wb": blocks(f[L3 + "WB0"], f[L3 + "WB1"], False, True),
        "sc": blocks(f[L3 + "Wsc0"], f[L3 + "Wsc1"], True, True),
    }
    d["weights"] = np.stack([by_name[n] for n in WEIGHTS])
    w0, w1, z = f[L3 + "Wc0"], f[L3 + "Wc1"], np.zeros(C, np.float32)
    rowd = {
        "b_le": f[L2 + "b_le"], "b_g1": f[L2 + "b_g1"],
        "ln_g": f[L2 + "ln_g"], "ln_b": f[L2 + "ln_b"], "b_g2": f[L2 + "b_g2"],
        "wc0a": np.concatenate([w0[:, 3], w1[:, 2], w0[:, 1], w1[:, 1]]),
        "wc0b": np.concatenate([w0[:, 0], w1[:, 0], w0[:, 4], w1[:, 3]]),
        "wc1": np.concatenate([w0[:, 2], z, z, z]),
        "norm": np.concatenate([f[L3 + "gamma0"], f[L3 + "beta0"], f[L3 + "gamma1"], z]),
    }
    d["b12"] = np.concatenate([f[L0 + "b1"], f[L0 + "b2"]])
    d["rowc"] = np.concatenate([rowd[n] for n in ROWS])
    d["we1"] = np.concatenate([f[L2 + "W_e1"].T, f[L2 + "b_e1"][None, :]])
    d["be2"] = f[L2 + "b_e2"].reshape(2, P).T

    def twice(w):
        r, c = w.shape
        m = np.zeros((2 * r, 2 * c), np.float32)
        m[:r, :c] = w
        m[r:, c:] = w
        return m

    d["m1"], d["m2"], d["m3"] = twice(f[L3 + "M1"]), twice(f[L3 + "M2"]), twice(f[L3 + "M3"])
    d["m4"] = np.concatenate([f[L3 + "M4"], f[L3 + "M4"]])
    return {k: np.ascontiguousarray(v) for k, v in d.items()}


def kernel(**inputs):
    import concourse.bacc as _bacc
    from concourse import mybir as _mybir
    from concourse.bass_utils import run_bass_kernel_spmd as _run

    n_nodes, n_edges = inputs["x"].shape[0], inputs["src"].shape[0]
    nb, _ = shapes(n_nodes, n_edges)
    nc = _bacc.Bacc("TRN2", target_bir_lowering=False, num_devices=1)
    arrays, io = {}, {}
    for name, a in layouts(inputs, n_nodes, n_edges).items():
        arrays[f"in_{name}"] = a
        io[name] = nc.dram_tensor(f"in_{name}", a.shape, _mybir.dt.from_np(a.dtype), kind="ExternalInput").ap()
    io["out"] = nc.dram_tensor("out_x", (nb * P, D), _mybir.dt.float32, kind="ExternalOutput").ap()
    build(nc, io, n_nodes, n_edges)
    r = _run(nc, [arrays], core_ids=[0])
    return r.results[0]["out_x"][:n_nodes]
```

```python
from contextlib import ExitStack

import numpy as np

import concourse.bass as bass
from concourse import mybir

F32 = mybir.dt.float32
F32R = mybir.dt.float32r
BF16 = mybir.dt.bfloat16
I32 = mybir.dt.int32
ALU = mybir.AluOpType
ACT = mybir.ActivationFunctionType
AX_X = mybir.AxisListType.X
RMAX = bass.bass_isa.ReduceOp.max

P = 128
D = 256
C = 64
LN_EPS = 1e-5
NORM_EPS = 1e-12
LEAKY = 0.2
WIN = 64
GROUPS = [(0, 3), (3, 3), (6, 3), (9, 3), (12, 3), (15, 2)]
TPI = 17
NG = len(GROUPS)
BPAD = 8
NODE_AT = 2
U_PLACE = [0, 1, 2, 3, 4, 5, 0, 6, 7, 1, 2, 3, 0, 4, 5, 6, 7]
TPW_BANK = [0, 1, 2, 0, 3, 1, 2, 0, 3, 1, 0, 2, 3, 0, 1, 2, 3]
WARM = (4, 2)
LAG = 2
HALVES = ((0, 9, (0, 1, 2)), (9, 8, (3, 4, 5)))
MB = 3
MW = 384

WEIGHTS = ["l0_w1", "l0_w2", "l1_w1", "l1_w2", "g1", "g2", "up", "e2", "le", "lin", "wb", "sc"]
PLACE = {"l0_w1": 0, "l0_w2": 1, "l1_w1": 2, "l1_w2": 3, "g1": 4, "g2": 5, "up": 6, "lin": 0, "wb": 1, "sc": 2}
ROWS = ["b_le", "b_g1", "ln_g", "ln_b", "b_g2", "wc0a", "wc0b", "wc1_norm"]


def shapes(n_nodes, n_edges):
    nb = -(-n_nodes // P)
    ni = -(-n_edges // (P * TPI))
    assert nb == ni
    return nb, ni


def rounded(ap):
    return ap.bitcast(F32R)


def build(nc, io, n_nodes, n_edges):
    NB, NI = shapes(n_nodes, n_edges)
    T = NI * TPI
    LAST = n_nodes - (NB - 1) * P
    NCOL = NB * P + WIN
    ALLWIN = NCOL // WIN
    CH = max(c for c in range(1, 8) if NB % c == 0)

    with ExitStack() as ctx:
        def sb(name, shape, dt=F32):
            return ctx.enter_context(nc.sbuf_tensor(name, shape, dt))

        def also(name, shape):
            with nc.sbuf_tensor(name, shape, F32) as t:
                return t

        def psum(name, shape, dt=F32):
            return ctx.enter_context(nc.psum_tensor(name, shape, dt))

        def sem(name):
            return ctx.enter_context(nc.semaphore(name))

        table = [nc.dram_tensor(f"table{l}", [NB * P, D], F32, kind="Internal").ap() for l in range(4)]
        h_t_dram = [nc.dram_tensor(f"h_t{l}", [NB, P, D], F32, kind="Internal").ap() for l in range(4)]
        r3_dram = nc.dram_tensor("r3", [NI, 2, 2, C, MB * MW], F32, kind="Internal").ap()

        x_all = sb("x_all", [P, NB, D])
        acc = sb("acc", [P, 2, NCOL])
        w_all = sb("w_all", [P, 7, 2, D])
        rowc = sb("rowc", [P, len(ROWS), D])
        rel = sb("rel", [P, T])
        ew = sb("ew", [P, T])
        sh = sb("sh", [P, TPI, 4])
        base_i = sb("base_i", [1, (NI + 1) * BPAD], I32)
        ident = sb("ident", [P, P])
        iota = sb("iota", [P, WIN])
        ones = sb("ones", [P, P])
        flag_i = sb("flag_i", [P, 1], I32)
        eps = sb("eps", [P, 1])
        zeros = sb("zeros", [P, 2, P])
        we1_hi = sb("we1_hi", [P, D])
        we1_lo = sb("we1_lo", [P, D])
        be1 = sb("be1", [P, 2])
        wc_hi = sb("wc_hi", [P, 2, D])
        wc_lo = sb("wc_lo", [P, 2, D])
        bc3 = sb("bc3", [3, D], BF16)
        ones3 = sb("ones3", [3, P], BF16)
        m_sums = sb("m_sums", [P, 2 * D])
        m1, m2, m3 = m_sums[0:2 * 16, 0:P], m_sums[:, P:2 * P], m_sums[:, 2 * P:3 * P]
        o_sum, o_sq = m_sums[:, 0:D], m_sums[:, D:2 * D]
        m4_hi = sb("m4_hi", [P, D])
        m4_lo = sb("m4_lo", [P, D])
        idx = sb("idx", [P, TPI], I32)
        rows = sb("rows", [P, TPI, D])
        hot = sb("hot", [P, TPI, WIN])
        split = also("split", [P, 8 * 4 * WIN + 8 * 8 * C])
        arena = sb("arena", [P, 8 * 4 * WIN + 8 * 8 * C])
        raw = arena[:, 0:3 * MW].rearrange("p (b n) -> p b n", b=3)
        x_t = split[:, 3 * MW:5 * MW].rearrange("p (b n) -> p b n", b=2)
        r_full = arena[:, 5 * MW:7 * MW].rearrange("p (c n) -> p c n", c=2)
        r_hi = split[:, 7 * MW:11 * MW].rearrange("p (b c n) -> p b c n", b=2, c=2)
        r_lo = split[:, 11 * MW:15 * MW].rearrange("p (b c n) -> p b c n", b=2, c=2)
        hot4 = arena[:, 0:8 * 4 * WIN].rearrange("p (t k w) -> p t k w", t=8, k=4)
        u_ring = arena[:, 8 * 4 * WIN:].rearrange("p (t j c) -> p t j c", t=8, j=8)
        rbf = arena[0:32, 0:MB * MW]
        ra = arena[:, MB * MW:MB * MW + 2 * MW].rearrange("p (b n) -> p b n", b=2)
        rb = arena[:, (MB + 2) * MW:(MB + 4) * MW].rearrange("p (b n) -> p b n", b=2)
        rc = arena[:, (MB + 4) * MW:(MB + 6) * MW].rearrange("p (b n) -> p b n", b=2)
        r_out = arena[:, (MB + 6) * MW:(3 * MB + 6) * MW].rearrange("p (b h n) -> p b h n", b=MB, h=2)
        r3 = sb("r3_sb", [P, 2, MB * MW])
        r3_parts = sb("r3_parts", [P, 2, MW])
        h_t = sb("h_t_in", [P, 2, P])
        q_t = sb("q_t", [P, 2, P])
        y = sb("y", [P, D])
        y2 = sb("y2", [P, D])
        y_t = sb("y_t", [P, 2, P])
        h_new = sb("h_new", [P, D])
        h_new_t = sb("h_new_t", [P, 2, P])
        t_out = sb("t_out", [P, D])
        small = sb("small", [P, 32])
        bias0 = arena[:, 8 * 4 * WIN + 8 * 8 * C - D:]
        poly = rowc[:, ROWS.index("b_le"), 0:2 * C].rearrange("p (j c) -> p j c", j=2)
        poly2 = rowc[:, ROWS.index("b_le"), 2 * C:4 * C].rearrange("p (j c) -> p j c", j=2)
        vv = h_new_t[:, 0, :].rearrange("p (j c) -> p j c", j=2)
        fin = arena[:, 0:8 * D].rearrange("p (j d) -> p j d", d=D)
        wbase = sb("wbase", [P, 1])
        relw = sb("relw", [P, 4])

        def W(name):
            return w_all[:, PLACE[name], :, :]

        def R(name):
            return rowc[:, ROWS.index(name), :]

        ps_even = psum("ps_even", [P, 2, 2 * P])
        ps_odd = psum("ps_odd", [P, 2, 2 * P])
        ps_node = psum("ps_node", [P, 2, D])
        ps_tp = psum("ps_tp", [P, 4, P])
        ps_edge = psum("ps_edge", [P, 4, 512])

        def ps_acc(k):
            return (ps_odd if k % 2 else ps_even)[:, :, 0:WIN]

        ps_up = ps_tp[:, 2:4, :].rearrange("p c n -> p (c n)")
        ps_z = ps_edge[:, 2:4, 0:D]
        ps_tpw = ps_edge[:, :, 0:D]

        s_weights = sem("s_weights")
        s_scalars = sem("s_scalars")
        s_x = [sem(f"s_x{c}") for c in range(NB // CH)]
        s_const = sem("s_const")
        s_pre = sem("s_pre")
        s_prep_mm = sem("s_prep_mm")
        s_bc = sem("s_bc")
        s_flag_part = sem("s_flag_part")
        s_flag_all = sem("s_flag_all")
        s_flag = sem("s_flag")
        s_root = sem("s_root")
        s_scale = sem("s_scale")
        s_ph = sem("s_ph")
        s_ph_t = sem("s_ph_t")
        s_pht_copied = sem("s_pht_copied")
        s_pstore = [sem("s_pstore0"), sem("s_pstore1")]
        s_pstore_t = [sem("s_pstore_t0"), sem("s_pstore_t1")]
        idx_in = [sem("idx_in0"), sem("idx_in1")]
        rows_in = [sem(f"rows_in{k}") for k in range(NG)]
        hot_ready = sem("hot_ready")
        hot_part = sem("hot_part")
        summed = sem("summed")
        added = sem("added")
        relw_done = sem("relw_done")
        wbase_done = sem("wbase_done")
        rbf_in = [sem(f"rbf_in{m}") for m in range(MB)]
        mlp_mm = [sem(f"mlp_mm{s}") for s in range(3)]
        mlp_act = [sem(f"mlp_act{s}") for s in range(3)]
        r3_out = [sem(f"r3_out{m}") for m in range(MB)]
        r3_in = [sem(f"r3_in{m}") for m in range(MB)]
        raw_in = [sem(f"raw_in{k}") for k in range(NG)]
        x_hi_done = sem("x_hi_done")
        x_done = sem("x_done")
        r_lo_done = sem("r_lo_done")
        r3_lo_done = sem("r3_lo_done")
        r3_copied = sem("r3_copied")
        a_done = sem("a_done")
        r_done = sem("r_done")
        z_done = sem("z_done")
        z_read = sem("z_read")
        msg_done = sem("msg_done")
        tpw_done = sem("tpw_done")
        u_done = sem("u_done")
        ht_in = sem("ht_in")
        q_ready = sem("q_ready")
        acc_free = sem("acc_free")
        n_mm = sem("n_mm")
        n_y = sem("n_y")
        n_lk = sem("n_lk")
        n_ss = sem("n_ss")
        n_root = sem("n_root")
        n_mx = sem("n_mx")
        n_rn = sem("n_rn")
        x_new = sem("x_new")
        t_bn = sem("t_bn")
        t_mv = sem("t_mv")
        t_root = sem("t_root")
        t_rstd = sem("t_rstd")
        t_scale = sem("t_scale")
        t_h = sem("t_h")
        t_tp = sem("t_tp")
        t_ht = sem("t_ht")
        t_tab = sem("t_tab")
        t_up = sem("t_up")
        table_out = sem("table_out")
        ht_out = sem("ht_out")
        g_bn = sem("g_bn")
        g_mv = sem("g_mv")
        g_root = sem("g_root")
        g_rstd = sem("g_rstd")
        g_lg = sem("g_lg")
        g_lb = sem("g_lb")
        g_tp = sem("g_tp")
        g_yt = sem("g_yt")
        g_mm2 = sem("g_mm2")
        g_x1 = sem("g_x1")
        o_acopy = sem("o_acopy")
        o_step = sem("o_step")
        o_b = sem("o_b")
        o_tp = sem("o_tp")
        o_bt = sem("o_bt")
        o_mm = sem("o_mm")
        o_copied = sem("o_copied")
        o_sqd = sem("o_sqd")
        o_kept = sem("o_kept")
        o_summed = sem("o_summed")
        f_mm = sem("f_mm")
        f_step = sem("f_step")
        f_root = sem("f_root")
        s_out = sem("s_out")

        def by_pairs(eng, chunk):
            n = NB // CH
            if n > 1:
                with eng.Fori(0, n // 2) as pair:
                    chunk(pair * 2, 0, pair)
                    chunk(pair * 2 + 1, 1, pair)
            if n % 2:
                chunk(n - 1, 0, n // 2)

        def stored(half):
            return 16 * ((NB // CH + 1 - half) // 2) + 16

        def pass_waits(eng):
            eng.sem_inc(passed, 1)

        def last_use(t, ring, total):
            return t - ring if t >= ring else max(u for u in range(total) if u % ring == t % ring) - total

        def last_in(t, places):
            same = [u for u in range(TPI) if places[u] == places[t]]
            return max([u for u in same if u < t] or [same[-1] - TPI])

        def ahead(i, k):
            return (i + 1, k - NG) if k >= NG else (i, k)

        def group_of(t):
            g = next(k for k, (t0, n) in enumerate(GROUPS) if t0 <= t % TPI < t0 + n)
            return g - (NG if t < 0 else 0)

        N_WEIGHT_LOADS = 9 + 9
        MLP_IN = [(0,), (1, 2), (), ()]
        MLP_AT = [[[(0, 0)], [(1, 0)], [(2, 0)], [], [], []],
                  [[(0, 1), (0, 2)], [(1, 1), (1, 2)], [(2, 1), (2, 2)], [], [], []], [[]] * NG, [[]] * NG]
        MLP_REST_AT = [[[], [], [], [0], [], []], [[], [], [], [1, 2], [], []], [[]] * NG, [[]] * NG]
        MLP_OUT_AT = [[[], [], [], [], [0], []], [[], [], [], [], [1, 2], []], [[]] * NG, [[]] * NG]

        def mlp_number(l, i, m):
            return NI * sum(len(MLP_IN[q]) for q in range(l)) + i * len(MLP_IN[l]) + MLP_IN[l].index(m)

        def mlp_before(l, i, m):
            return mlp_number(l, i, m) + 3 - len(MLP_IN[l])

        layer_its = [(l * NI, (l + 1) * NI) for l in range(4)]

        def sp_setup(sp):
            for c in range(NB // CH):
                sp.dma_start(x_all[:, c * CH:(c + 1) * CH, :],
                             io["x"][c * CH * P:(c + 1) * CH * P, :].rearrange("(b p) d -> p b d", p=P)).then_inc(s_x[c], 16)
            for dst, name in ((rel[:, :].bitcast(I32), "dst"), (ew[:, :], "ew"), (base_i[:, :], "base")):
                sp.dma_start(dst, io[name]).then_inc(s_scalars, 16)
            for n, name in enumerate(WEIGHTS[:9]):
                place = {"e2": w_e2, "le": w_le}[name] if name in ("e2", "le") else W(name)
                sp.dma_start(place, io["weights"][n, :, :].rearrange("(c p) d -> p c d", p=P)).then_inc(s_weights, 16)
            sp.dma_start(b12.rearrange("p r d -> p (r d)"), io["b12"].partition_broadcast(P)).then_inc(s_weights, 16)
            sp.dma_start(rowc[:, :, :].rearrange("p r d -> p (r d)"),
                         io["rowc"].partition_broadcast(P)).then_inc(s_weights, 16)
            for dst, name in ((we1, "we1"), (m1[:, :], "m1"), (m2[:, :], "m2"), (m3[:, :], "m3"), (m4, "m4"),
                              (be2, "be2"), (be1[:, :], "be1")):
                sp.dma_start(dst, io[name]).then_inc(s_weights, 16)
            sp.wait_ge(s_pre, PRE["bc_lo"])
            for j in range(3):
                sp.dma_start(bc3[j:j + 1, :], bc_parts[0:1, j, :]).then_inc(s_bc, 16)
            sp.wait_ge(s_bc, 48)

        def sp_indices(sp, half, i, landed):
            t0, n, groups = HALVES[half]
            if landed is not None:
                for k in groups:
                    sp.wait_ge(rows_in[k], landed * (16 * GROUPS[k][1]))
                    pass_waits(sp)
            sp.dma_start(idx[:, t0:t0 + n], io["src"][:, bass.ds(i * TPI + t0, n)]).then_inc(idx_in[half], 16)

        def sp_sh(sp, half, i, it, nw):
            t0, n, groups = HALVES[half]
            if it is not None:
                sp.wait_ge(hot_ready, (it * NG + groups[-1] + 1) * nw)
                pass_waits(sp)
            sp.dma_start(sh[:, t0:t0 + n, :], io["sh"][:, bass.ds(i * TPI + t0, n), :]).then_inc(sh_in[half], 16)

        def sp_edges(sp, l, it, i, more):
            for m in MLP_IN[l]:
                sp.wait_ge(mlp_mm[0], mlp_before(l, i, m))
                pass_waits(sp)
                sp.dma_start(rbf[:, m * MW:(m + 1) * MW],
                             io["rbf"][bass.ds(i, 1), :, m * MW:(m + 1) * MW].rearrange("a p n -> p (a n)")).then_inc(rbf_in[m], 16)
            if more:
                for half in range(2):
                    sp_indices(sp, half, i + 1, it + 1)

        def sp_r3(sp, i, m):
            sp.wait_ge(r3_copied, i * NG + 2 * m + 2)
            pass_waits(sp)
            for q in range(2):
                sp.dma_start(r3[:, q, m * MW:(m + 1) * MW],
                             r3_dram[bass.ds(i, 1), q, :, :, m * MW:(m + 1) * MW].rearrange("a h j n -> (a h j) n")).then_inc(r3_in[m], 16)

        def sp_edges_3(sp, it, i, nw, left):
            if left:
                sp_indices(sp, 1, i + 1, it + 1)
                sp_r3(sp, i + 1, 0)
                sp_sh(sp, 0, i + 1, it, nw)
                sp_r3(sp, i + 1, 1)
                sp_r3(sp, i + 1, 2)
            if left > 1:
                sp_indices(sp, 0, i + 2, it + 2)
            if left:
                sp_sh(sp, 1, i + 1, it, nw)

        def sp_raw(sp, i, groups):
            for k in groups:
                t0, n = GROUPS[k]
                sp.wait_ge(x_done, i * NG + k - 2 + NG)
                pass_waits(sp)
                for half in range(2):
                    sp.dma_start(raw[half * C:(half + 1) * C, k % 3, 0:n * P],
                                 io["raw"][bass.ds(i, 1), :, t0 * P:(t0 + n) * P].rearrange("a p n -> p (a n)")).then_inc(raw_in[k], 16)

        def sp_edges_2(sp, it, i, left):
            if left:
                sp_indices(sp, 1, i + 1, it + 1)
            sp_raw(sp, i + 1, range(3))
            if left > 1:
                sp_indices(sp, 0, i + 2, it + 2)
            if left:
                sp_raw(sp, i + 1, range(3, NG))

        def sp_layer_2(sp):
            a, z = layer_its[2]
            sp.wait_ge(table_out, 16 * 2 * NB + 16)
            for name in ("lin", "wb", "sc"):
                sp.dma_start(W(name), io["weights"][WEIGHTS.index(name), :, :].rearrange("(c p) d -> p c d", p=P)).then_inc(s_w3, 16)
            for m in range(MB):
                sp.wait_ge(r3_out[m], 32 * NI + 16)
            for half in range(2):
                sp_indices(sp, half, 0, a)
            sp_raw(sp, 0, range(NG))
            sp_indices(sp, 0, 1, a + 1)
            with sp.Fori(a, z - 2) as it:
                sp_edges_2(sp, it, it - a, 2)
            sp_edges_2(sp, z - 2, NI - 2, 1)
            sp_edges_2(sp, z - 1, NI - 1, 0)

        def sp_layer_3(sp, nw):
            a, z = layer_its[3]
            for half in range(2):
                sp_indices(sp, half, 0, a)
                sp_sh(sp, half, 0, None, nw)
            for m in range(MB):
                sp_r3(sp, 0, m)
            sp_indices(sp, 0, 1, a + 1)
            with sp.Fori(a, z - 2) as it:
                sp_edges_3(sp, it, it - a, nw, 2)
            sp_edges_3(sp, z - 2, NI - 2, nw, 1)

        def sp_layer(sp, l, nw):
            a, z = layer_its[l]
            if l == 0:
                for half in range(2):
                    sp.wait_ge(s_pstore_t[half], stored(half))
            if l == 1:
                sp.wait_ge(hot_ready, NI * NG * nw)
                sp.dma_start(ew[:, :], io["pol"]).then_inc(s_pol, 16)
            for half in range(2):
                sp_indices(sp, half, 0, a if l else None)
            with sp.Fori(a, z - 1) as it:
                sp_edges(sp, l, it, it - a, True)
            sp_edges(sp, l, z - 1, z - 1 - a, False)

        def pool_setup(pool):
            pool.memset(ident[:, :], 0.0).then_inc(s_const, 1)
            pool.iota(iota_i[:, :], [[1, WIN]], base=0, channel_multiplier=0).then_inc(s_const, 1)
            pool.memset(ones[:, :], 1.0).then_inc(s_const, 1)
            pool.memset(ones3[:, :], 1.0).then_inc(s_const, 1)
            pool.memset(eps[:, :], LN_EPS).then_inc(s_const, 1)
            pool.wait_ge(s_const, 5)
            pool.affine_select(out=ident[:, :], in_=ident[:, :], compare_op=ALU.not_equal, fill=1.0, base=0,
                               pattern=[[-1, P]], channel_multiplier=1).then_inc(s_const, 1)
            pool.tensor_copy(iota[:, :], iota_i[:, :]).then_inc(s_const, 1)
            pool.wait_ge(s_flag_part, 1)
            pool.partition_all_reduce(flag_f[:, 1:2], flag_f[:, 0:1], P, RMAX).then_inc(s_flag_all, 1)

        poly_a0 = y[:, 0:C]
        poly_a0b = poly_a0.unsqueeze(1).broadcast_to([P, 2, C])
        poly_a1 = y[:, C:D].rearrange("p (x c) -> p x c", x=3)
        poly_sq = y2[:, C:D].rearrange("p (x c) -> p x c", x=3)
        w_c3, w_c1, w_c0, w_cv, w_c2 = [R(name)[:, j * C:(j + n) * C].rearrange("p (j c) -> p j c", c=C) for name, j, n in (
            ("wc0a", 0, 2), ("wc0a", 2, 2), ("wc0b", 0, 2), ("wc0b", 2, 2), ("wc1_norm", 0, 1))]

        def poly_step(pool, b, n, ins):
            ins.then_inc(o_step, 1)
            pool.wait_ge(o_step, b * POLY + n)

        def pool_poly(pool, l, b):
            pool.wait_ge(o_acopy, b + 2)
            pool.wait_ge(o_tp, b + 1)
            poly_step(pool, b, 1, pool.tensor_tensor(poly_sq, poly_a1, poly_a1, ALU.mult))
            poly_step(pool, b, 2, pool.tensor_tensor(vv[:, 1, :], poly_sq[:, 0, :], poly_sq[:, 1, :], ALU.add))
            poly_step(pool, b, 3, pool.tensor_tensor(vv[:, 0, :], vv[:, 1, :], poly_sq[:, 2, :], ALU.add))
            poly_step(pool, b, 4, pool.tensor_tensor(poly[:, :, :], w_c3, poly_a0b, ALU.mult))
            poly_step(pool, b, 5, pool.tensor_tensor(poly[:, :, :], poly[:, :, :], w_c1, ALU.add))
            poly_step(pool, b, 6, pool.tensor_tensor(poly[:, :, :], poly[:, :, :], poly_a0b, ALU.mult))
            poly_step(pool, b, 7, pool.tensor_tensor(poly[:, :, :], poly[:, :, :], w_c0, ALU.add))
            poly_step(pool, b, 8, pool.tensor_tensor(poly2[:, :, :], w_cv, vv[:, 0:1, :].broadcast_to([P, 2, C]), ALU.mult))
            poly_step(pool, b, 9, pool.tensor_tensor(poly[:, :, :], poly[:, :, :], poly2[:, :, :], ALU.add))
            poly_step(pool, b, 10, pool.tensor_tensor(poly2[:, 0, :], poly[:, 0, :], poly_a0, ALU.mult))
            poly_step(pool, b, 11, pool.tensor_tensor(poly2[:, 1, :], w_c2[:, 0, :], vv[:, 0, :], ALU.mult))
            poly_step(pool, b, 12, pool.tensor_tensor(y2[:, 0:C], poly2[:, 0, :], poly2[:, 1, :], ALU.add))
            pool.tensor_tensor(poly_sq, poly_a1, poly[:, 1:2, :].broadcast_to([P, 3, C]), ALU.mult).then_inc(o_b, 1)

        def pool_edges(pool, l, it, nw, node, first):
            for k, (t0, n) in enumerate(GROUPS):
                if k % 3 == 0:
                    pool.wait_ge(idx_in[k // 3], it * 16 + 16)
                pool.wait_ge(summed, (it * NG + k + 1) * nw)
                pass_waits(pool)
                for t in range(t0, t0 + n):
                    pool.indirect_dma_start(rows[:, t, :], None, table[l],
                                            bass.IndirectOffsetOnAxis(ap=idx[:, t:t + 1], axis=0)).then_inc(rows_in[k], 16)
                if node:
                    node(2 * k)
                    node(2 * k + 1)

        def pool_layer(pool, l, nw):
            a, z = layer_its[l]
            if l == 0:
                for half in range(2):
                    pool.wait_ge(s_pstore[half], stored(half))
            else:
                pool.wait_ge(table_out, 16 * l * NB + 16)
            if l < 3:
                with pool.Fori(a, z) as it:
                    pool_edges(pool, l, it, nw, None, False)
            else:
                run_layer(pool, l, nw, pool_edges, [(20, pool_poly)])

        def mm2(pe, out, lhs_t, w, start=True, stop=True):
            pe.matmul(out, lhs_t[:, 0, :], w[:, 0, :], start=start, stop=False)
            return pe.matmul(out, lhs_t[:, 1, :], w[:, 1, :], start=False, stop=stop)

        def pe_setup(pe):
            pe.wait_ge(s_weights, 16 * N_WEIGHT_LOADS)
            for c in range(2):
                for j in range(2):
                    mm = pe.matmul(ps_edge[:, c, 0:D], w_e2[:, j, c * P:(c + 1) * P], w_le[:, j, :],
                                   start=(j == 0), stop=(j == 1))
                mm.then_inc(s_prep_mm, 1)
            for j in range(2):
                mm = pe.matmul(ps_edge[0:1, 2, 0:D], be2[:, j:j + 1], w_le[:, j, :], start=(j == 0), stop=(j == 1))
            mm.then_inc(s_prep_mm, 1)
            pe.wait_ge(s_const, 7)
            pe.wait_ge(s_pre, PRE["base_f"])
            pe.matmul(ps_edge[:, 3, 0:(NI + 1) * BPAD], ones[0:1, :], base_f[0:1, :], start=True, stop=True).then_inc(s_prep_mm, 1)
            pe.wait_ge(s_pre, PRE["early"])
            def chunk(c, half, pair):
                for j in range(CH):
                    pe.wait_ge(s_ph, c * CH + j + 1)
                    pe.wait_ge(s_pht_copied, c * CH + last_use(j, 4, CH) + 1 + CH)
                    for d in range(2):
                        mm = pe.transpose(tp_of(j, d), rows[:, half * CH + j, d * P:(d + 1) * P], ident[:, :])
                    mm.then_inc(s_ph_t, 1)

            by_pairs(pe, chunk)

        def tp_of(j, d):
            return ps_edge[:, j % 4, d * P:(d + 1) * P]

        def pe_sum(pe, l, it, k, w, nw):
            t0, n = GROUPS[k]
            a = layer_its[l][0]
            if l < 2:
                pe.wait_ge(rows_in[k], (it + 1) * 16 * n)
            elif l == 2:
                pe.wait_ge(msg_done, (it - a) * NG + k + 1)
            else:
                pe.wait_ge(u_done, (it - a) * TPI + t0 + n + TPI)
            pe.wait_ge(hot_ready, (it * NG + k) * nw + (w + 1))
            if nw == 1:
                pe.wait_ge(added, it * NG + k - 1 + NG)
            else:
                pe.wait_ge(added, (it * NG + k) * nw + w + NG * nw)
            out = ps_acc(k)
            for t in range(t0, t0 + n):
                first, last = t == t0, t == t0 + n - 1
                if l < 3:
                    for c in range(2):
                        mm = pe.matmul(out[:, c, :], rows[:, t, c * P:(c + 1) * P], hot[:, t, :],
                                       start=(first and c == 0), stop=last, skip_group_check=True)
                else:
                    u = u_ring[:, U_PLACE[t], :, :]
                    s = hot4[:, U_PLACE[t], :, :]
                    pe.matmul(out[:, 0, :], u[:, 0:2, :], s[:, 0, :], start=first, stop=False, skip_group_check=True)
                    pe.matmul(out[:, 1, :], u[:, 2:4, :], s[:, 0, :], start=False, stop=False, skip_group_check=True)
                    pe.matmul(out[0:C, 0, :], u[:, 4, :], s[:, 1, :], start=False, stop=False, skip_group_check=True)
                    pe.matmul(out[C:P, 0, :], u[:, 7, :], s[:, 1, :], start=False, stop=False, skip_group_check=True)
                    pe.matmul(out[0:C, 0, :], u[:, 5, :], s[:, 2, :], start=False, stop=False, skip_group_check=True)
                    pe.matmul(out[0:C, 1, :], u[:, 7, :], s[:, 2, :], start=False, stop=False, skip_group_check=True)
                    pe.matmul(out[0:C, 0, :], u[:, 6, :], s[:, 3, :], start=False, stop=last, skip_group_check=True)
                    mm = pe.matmul(out[C:P, 1, :], u[:, 7, :], s[:, 3, :], start=False, stop=last, skip_group_check=True)
            mm.then_inc(summed, 1)

        def pe_mlp(pe, l, i, stage, m):
            q = mlp_number(l, i, m)
            if stage == 0:
                pe.wait_ge(rbf_in[m], i * 16 + 16)
                src, w = rbf[:, m * MW:(m + 1) * MW], m1
            else:
                pe.wait_ge(mlp_act[stage - 1], q + 1)
                src, w = (ra, rb)[stage - 1][:, m % 2, :], (m2, m3)[stage - 1]
            if stage == 0:
                pe.wait_ge(mlp_act[2], mlp_before(l, i, m))
            pe.matmul(ps_edge[:, m % 2, 0:MW], w[:, :], src, start=True, stop=True).then_inc(mlp_mm[stage], 1)

        def pe_a(pe, i, k):
            t0, n = GROUPS[k]
            pe.wait_ge(x_done, i * NG + k + 1 + NG)
            for c in range(2):
                pe.wait_ge(r_done, (i * NG + k) * 2 + c + 1)
                out = ps_edge[:, c, 0:n * P]
                pe.matmul(out, rounded(we1_hi[:, c * P:(c + 1) * P]), rounded(x_t[:, k % 2, 0:n * P]), start=True, stop=False)
                pe.matmul(out, rounded(we1_lo[:, c * P:(c + 1) * P]), rounded(x_t[:, k % 2, 0:n * P]),
                          start=False, stop=True).then_inc(a_done, 1)

        def pe_z(pe, i, k):
            t0, n = GROUPS[k]
            pe.wait_ge(r_lo_done, i * NG + k + 1 + 1)
            for t in range(t0, t0 + n):
                pe.wait_ge(z_read, i * TPI + last_use(t, 2, TPI) + 1 + TPI)
                z = ps_z[:, t % 2, :]
                pe.matmul(z, ones3[:, :], bc3[:, :], start=True, stop=False)
                cols = slice((t - t0) * P, (t - t0 + 1) * P)
                for c in range(2):
                    pe.matmul(z, rounded(r_hi[:, k % 2, c, cols]), rounded(wc_hi[:, c, :]), start=False, stop=False)
                    pe.matmul(z, rounded(r_hi[:, k % 2, c, cols]), rounded(wc_lo[:, c, :]), start=False, stop=False)
                    mm = pe.matmul(z, rounded(r_lo[:, k % 2, c, cols]), rounded(wc_hi[:, c, :]), start=False, stop=(c == 1))
                mm.then_inc(z_done, 1)

        def pe_tpw(pe, i, k):
            t0, n = GROUPS[k]
            pe.wait_ge(r3_copied, i * NG + k + 1 + NG)
            for t in range(t0, t0 + n):
                pe.wait_ge(u_done, i * TPI + last_in(t, TPW_BANK) + 1 + TPI)
                both = rounded(r3_parts[:, k % 2, (t - t0) * P:(t - t0 + 1) * P])
                pe.matmul(ps_tpw[:, TPW_BANK[t], :], both, rounded(m4_hi[:, :]), start=True, stop=False)
                pe.matmul(ps_tpw[:, TPW_BANK[t], :], both, rounded(m4_lo[:, :]), start=False, stop=True).then_inc(tpw_done, 1)

        def pe_node_a(pe, l, b):
            n = b + (l * NB + 1)
            pe.wait_ge(q_ready, n)
            if l < 3:
                pe.wait_ge(ht_in, n * 16)
            out = ps_node[:, 0, :]
            if l < 3:
                pe.wait_ge(x_new, n)
            if l < 2:
                mm2(pe, out, h_t, W(f"l{l}_w1"), stop=False)
                mm2(pe, out, q_t, W(f"l{l}_w2"), start=False).then_inc(n_mm, 1)
            elif l == 2:
                mm2(pe, out, q_t, W("g1")).then_inc(n_mm, 1)
            else:
                pe.wait_ge(o_acopy, b + 1)
                pe.wait_ge(o_kept, b + 1)
                for c in range(2):
                    mm = pe.matmul(ps_node[:, 0, c * P:(c + 1) * P], q_t[:, c, :], W("lin")[:, c, c * P:(c + 1) * P],
                                   start=True, stop=True)
                mm.then_inc(n_mm, 1)

        def pe_transpose(pe, out, src):
            for c in range(2):
                mm = pe.transpose(out[:, c, :], src[:, c * P:(c + 1) * P], ident[:, :])
            return mm

        def pe_turn_y(pe, l, b):
            if l == 2:
                pe.wait_ge(g_lb, b + 1)
                pe.wait_ge(g_yt, b + 1)
                pe.wait_ge(t_up, b + 1)
            else:
                pe.wait_ge(o_b, b + 1)
                pe.wait_ge(o_bt, b + 1)
            pe_transpose(pe, ps_tp[:, 2:4, :], y2).then_inc(g_tp if l == 2 else o_tp, 1)

        def pe_second(pe, l, b):
            if l == 2:
                pe.wait_ge(g_yt, b + 2)
                pe.wait_ge(g_x1, b + 1)
                mm2(pe, ps_node[:, 1, :], y_t, W("g2")).then_inc(g_mm2, 1)
            else:
                pe.wait_ge(o_bt, b + 2)
                pe.wait_ge(o_kept, b + 1)
                pe.wait_ge(ht_in, (b + (3 * NB + 1)) * 16)
                mm2(pe, ps_node[:, 1, :], h_t, W("sc"), stop=False)
                mm2(pe, ps_node[:, 1, :], y_t, W("wb"), start=False).then_inc(o_mm, 1)

        def pe_turn(pe, l, b):
            n = b + (l * NB + 1)
            pe.wait_ge(t_h, n)
            pe.wait_ge(t_ht, n)
            pe_transpose(pe, ps_tp[:, 0:2, :], h_new).then_inc(t_tp, 1)

        def pe_up(pe, l, b):
            pe.wait_ge(t_ht, b + (l * NB + 2))
            mm2(pe, ps_up, h_new_t, W("up")).then_inc(t_tab, 1)

        def pe_edges(pe, l, it, nw, node, first):
            i = it - layer_its[l][0]
            if nw > 1:
                for k in range(NG):
                    for stage, m in MLP_AT[l][k]:
                        pe_mlp(pe, l, i, stage, m)
                    if l == 2:
                        pe_a(pe, i, k)
                        pe_z(pe, i, k)
                    if l == 3:
                        pe_tpw(pe, i, k)
                    with pe.Fori(0, nw) as w:
                        pe_sum(pe, l, it, k, w, nw)
                return
            if l == 2 and first:
                pe_a(pe, i, 0)
            for k in range(NG):
                for stage, m in MLP_AT[l][k]:
                    pe_mlp(pe, l, i, stage, m)
                if l == 2:
                    pe_a(pe, *ahead(i, k + 1))
                    pe_z(pe, i, k)
                if l == 3:
                    pe_tpw(pe, i, k)
                node(2 * k)
                if l < 2:
                    pe_keep_warm(pe, WARM[l])
                    pe_sum(pe, l, it, k, 0, 1)
                elif k:
                    pe_sum(pe, l, it, k - 1, 0, 1)
                elif not first:
                    pe_sum(pe, l, it - 1, NG - 1, 0, 1)
                node(2 * k + 1)

        def pe_keep_warm(pe, n):
            for _ in range(n):
                pe.matmul(ps_edge[:, 3, :], ident[:, 0:P // 2].bitcast(BF16),
                          zeros[:, :, :].rearrange("p c n -> p (c n)").bitcast(BF16), start=True, stop=True)

        def pe_close(pe, l):
            if l >= 2:
                pe_sum(pe, l, layer_its[l][1] - 1, NG - 1, 0, 1)

        def run_layer(eng, l, nw, edges, parts, close=None):
            a, z = layer_its[l]

            def among(early, late):
                def node(p):
                    for position, part in parts:
                        if position == p + 2 * NG and late is not None:
                            part(eng, l, late)
                    for position, part in parts:
                        if position == p and early is not None:
                            part(eng, l, early)
                return node

            if nw == 1:
                edges(eng, l, a, nw, among(None, None), True)
                edges(eng, l, a + 1, nw, among(0, None), False)
                with eng.Fori(a + 2, z) as it:
                    edges(eng, l, it, nw, among(it - (a + 1), it - (a + 2)), False)
                if close:
                    close(eng, l)
                for position, part in parts:
                    if position >= 2 * NG:
                        part(eng, l, NB - 2)
                for _, part in parts:
                    part(eng, l, NB - 1)
            else:
                with eng.Fori(a, z) as it:
                    edges(eng, l, it, nw, None, False)
                with eng.Fori(0, NB - 1) as b:
                    for _, part in parts:
                        part(eng, l, b)
                for _, part in parts:
                    part(eng, l, NB - 1)

        PE_PARTS = [[(8, pe_node_a), (16, pe_turn)], [(8, pe_node_a), (14, pe_turn)],
                    [(8, pe_node_a), (12, pe_turn_y), (14, pe_second), (20, pe_turn), (22, pe_up)],
                    [(8, pe_node_a), (16, pe_turn_y), (18, pe_second)]]

        def pe_final(pe):
            pe.wait_ge(o_summed, 2 * NB + 2)
            pe.matmul(ps_edge[:, 0, 0:D], ones[:, :], o_sum[:, :], start=True, stop=True)
            pe.matmul(ps_edge[:, 1, 0:D], ones[:, :], o_sq[:, :], start=True, stop=True).then_inc(f_mm, 1)
            pe.wait_ge(f_step, FIN["var_part"])
            pe.matmul(ps_edge[:, 2, 0:C], ones[:, :], fin[:, 2, 0:C], start=True, stop=True).then_inc(f_mm, 1)

        def ve_setup(ve):
            steps = []

            def step(name, ins):
                steps.append(name)
                assert PRE[name] == len(steps)
                ins.then_inc(s_pre, 1)

            step("zeros", ve.memset(zeros[:, :, :], 0.0))
            step("base0", ve.memset(base_f, 0.0))
            for c in range(NB // CH):
                ve.wait_ge(s_x[c], 16)
            with ve.Fori(0, NB // CH) as c:
                ve.wait_ge(t_mv, c + 1)
                for j in range(CH):
                    pass_waits(ve)
                    ve.bn_stats(bn_c[:, j, :], x_all[:, bass.ds(c * CH + j, 1), :].rearrange("p a d -> p (a d)")).then_inc(bn_part, 1)
                ve.wait_ge(bn_part, (c + 1) * CH)
                pass_waits(ve)
                for j in range(CH):
                    ve.bn_aggr(mv_c[:, j, :], bn_c[:, j, :]).then_inc(mv_part, 1)
                ve.wait_ge(mv_part, (c + 1) * CH)
                pass_waits(ve)
                ve.tensor_copy(mv_all[:, bass.ds(c * CH, CH), :], mv_c[:, :, :]).then_inc(t_mv, 1)
            ve.wait_ge(s_root, 1)
            ve.reciprocal(stats_all[:, 1, :], stats_all[:, 0, :]).then_inc(s_scale, 1)
            ve.wait_ge(s_scale, 1)
            ve.scalar_tensor_tensor(out=stats_all[:, 2, :], in0=mv_all[:, :, 0], scalar=-1.0, in1=stats_all[:, 1, :],
                                    op0=ALU.mult, op1=ALU.mult).then_inc(s_scale, 1)
            step("acc0", ve.memset(acc[:, :, :], 0.0))
            ve.wait_ge(s_scalars, 16 * 3)
            step("dst_f", ve.tensor_copy(rel[:, :], rel[:, :].bitcast(I32)))
            ve.wait_ge(s_pre, PRE["dst_f"])
            step("base_f", ve.tensor_copy(base_f[0:1, :], base_i[:, :]))
            ve.wait_ge(s_weights, 16 * N_WEIGHT_LOADS)
            step("m4", ve.tensor_scalar(m4[:, 3 * C:4 * C], m4[:, 3 * C:4 * C], float(1.0 / np.sqrt(np.float32(3.0))), None, ALU.mult))
            step("bias0", ve.tensor_tensor(bias0[:, :], b12[:, 0, :], b12[:, 1, :], ALU.add))
            ve.wait_ge(s_pre, PRE["m4"])
            step("m4_hi", ve.tensor_copy(rounded(m4_hi[:, :]), m4[:, :]))
            ve.wait_ge(s_pre, PRE["m4_hi"])
            step("m4_lo", ve.tensor_tensor(rounded(m4_lo[:, :]), m4[:, :], m4_hi[:, :], ALU.subtract))
            step("we1_hi", ve.tensor_copy(rounded(we1_hi[:, :]), we1))
            ve.wait_ge(s_pre, PRE["we1_hi"])
            step("we1_lo", ve.tensor_tensor(rounded(we1_lo[:, :]), we1, we1_hi[:, :], ALU.subtract))
            ve.wait_ge(s_prep_mm, 2)
            step("wc_hi", ve.tensor_copy(rounded(wc_hi[:, :, :]), ps_edge[:, 0:2, 0:D]))
            ve.wait_ge(s_pre, PRE["wc_hi"])
            step("wc_lo", ve.tensor_tensor(rounded(wc_lo[:, :, :]), ps_edge[:, 0:2, 0:D], wc_hi[:, :, :], ALU.subtract))
            ve.wait_ge(s_prep_mm, 3)
            bc = ps_edge[0:1, 2, 0:D]
            step("bc_hi", ve.tensor_copy(bc_parts[0:1, 0, :], bc))
            ve.wait_ge(s_pre, PRE["bc_hi"])
            step("bc_r1", ve.tensor_tensor(bc_rest[0:1, 0, :], bc, bc_parts[0:1, 0, :], ALU.subtract))
            ve.wait_ge(s_pre, PRE["bc_r1"])
            step("bc_mid", ve.tensor_copy(bc_parts[0:1, 1, :], bc_rest[0:1, 0, :]))
            ve.wait_ge(s_pre, PRE["bc_mid"])
            step("bc_r2", ve.tensor_tensor(bc_rest[0:1, 1, :], bc_rest[0:1, 0, :], bc_parts[0:1, 1, :], ALU.subtract))
            ve.wait_ge(s_pre, PRE["bc_r2"])
            step("bc_lo", ve.tensor_copy(bc_parts[0:1, 2, :], bc_rest[0:1, 1, :]))
            ve.wait_ge(s_prep_mm, 4)
            bases = ps_edge[:, 3, 0:(NI + 1) * BPAD].rearrange("p (i g) -> p i g", g=BPAD)
            for k, (t0, n) in enumerate(GROUPS):
                step(f"rel{k}", ve.tensor_tensor(
                    rel[:, :].rearrange("p (i t) -> p i t", t=TPI)[:, :, t0:t0 + n],
                    rel[:, :].rearrange("p (i t) -> p i t", t=TPI)[:, :, t0:t0 + n],
                    bases[:, (k + LAG) // NG:NI + (k + LAG) // NG, (k + LAG) % NG:(k + LAG) % NG + 1].broadcast_to([P, NI, n]), ALU.subtract))
            ve.wait_ge(s_pre, PRE[f"rel{NG - 1}"])
            step("rel_max", ve.tensor_reduce(fl[:, 0:1], rel[:, :], AX_X, ALU.max))
            step("rel_min", ve.tensor_reduce(fl[:, 1:2], rel[:, :], AX_X, ALU.min))
            ve.wait_ge(s_pre, PRE["rel_min"])
            step("over", ve.tensor_scalar(fl[:, 2:3], fl[:, 0:1], float(1 - WIN), None, ALU.add))
            step("under", ve.tensor_scalar(fl[:, 3:4], fl[:, 1:2], -1.0, None, ALU.mult))
            step("early", ve.tensor_tensor(early, early, ps_edge[:, 3, 0:(NI + 1) * BPAD], ALU.subtract))
            ve.wait_ge(s_pre, PRE["early"])
            step("early_max", ve.tensor_reduce(fl[:, 4:5], early, AX_X, ALU.max))
            ve.wait_ge(s_pre, PRE["early_max"])
            ve.tensor_reduce(flag_f[:, 0:1], fl[:, 2:5], AX_X, ALU.max).then_inc(s_flag_part, 1)
            def chunk(c, half, pair):
                for j in range(CH):
                    ve.wait_ge(s_ph_t, c * CH + j + 1 + 2 * CH)
                    if j == 0:
                        ve.wait_ge(s_pstore_t[half], pair * 16 + 16)
                    ve.tensor_copy(pt[half][:, j, :], tp_both(j)).then_inc(s_pht_copied, 1)

            by_pairs(ve, chunk)
            ve.wait_ge(s_flag_all, 1)
            ve.tensor_copy(flag_i[:, :], flag_f[:, 1:2]).then_inc(s_flag, 1)

        def tp_both(j):
            return ps_edge[:, j % 4, 0:D]

        def ve_hot(ve, l, it, k, w, nw):
            t0, n = GROUPS[k]
            i = it - layer_its[l][0]
            if nw == 1:
                users = [k - NG] + [group_of(last_in(t, U_PLACE)) for t in range(t0, t0 + n) if l == 3]
                ve.wait_ge(summed, it * NG + (max(users) + 1 + NG))
                where = rel[:, bass.ds(i * TPI + t0, n)]
            else:
                g = (it * NG + k) * nw + w
                ve.wait_ge(summed, g + NG * nw)
                ve.wait_ge(wbase_done, g + (it * NG + k) + 2)
                ve.tensor_scalar(relw[:, 0:n], rel[:, bass.ds(i * TPI + t0, n)], wbase[:, 0:1], None,
                                 ALU.subtract).then_inc(relw_done, 1)
                ve.wait_ge(relw_done, g + 1)
                ve.tensor_scalar(wbase[:, :], wbase[:, :], float(WIN), None, ALU.add).then_inc(wbase_done, 1)
                where = relw[:, 0:n]
            ready = hot_ready if l in (1, 2) else hot_part
            ve.tensor_tensor(hot[:, t0:t0 + n, :], iota[:, :].unsqueeze(1).broadcast_to([P, n, WIN]),
                             where.unsqueeze(2).broadcast_to([P, n, WIN]), ALU.is_equal).then_inc(ready, 1)
            q = i * NG + k + (0 if l == 0 else NI * NG)
            part = q * nw + (w + 1)
            if l == 0:
                ve.wait_ge(hot_part, part)
                ve.tensor_tensor(hot[:, t0:t0 + n, :], hot[:, t0:t0 + n, :],
                                 ew[:, bass.ds(i * TPI + t0, n)].unsqueeze(2).broadcast_to([P, n, WIN]),
                                 ALU.mult).then_inc(hot_ready, 1)
            if l == 3:
                ve.wait_ge(sh_in[k // 3], i * 16 + 16)
                ve.wait_ge(hot_part, part)
                for t in range(t0, t0 + n):
                    ins = ve.tensor_tensor(hot4[:, U_PLACE[t], :, :], hot[:, t:t + 1, :].broadcast_to([P, 4, WIN]),
                                           sh[:, t, :].unsqueeze(2).broadcast_to([P, 4, WIN]), ALU.mult)
                ins.then_inc(hot_ready, 1)

        def ve_add(ve, l, it, k, w, nw, start):
            if nw == 1:
                g = it * NG + k
                ve.wait_ge(summed, g + 1 + NG)
                ve.wait_ge(added, g + NG)
            else:
                g = (it * NG + k) * nw + w
                ve.wait_ge(summed, g + 1 + NG * nw)
                ve.wait_ge(added, g + NG * nw)
            ve.tensor_tensor(acc[:, :, bass.ds(start, WIN)], acc[:, :, bass.ds(start, WIN)], ps_acc(k),
                             ALU.add).then_inc(added, 1)

        def ve_x_lo(ve, i, k):
            n = GROUPS[k][1]
            ve.wait_ge(x_hi_done, i * NG + k + 1)
            lower = x_t[C:P, k % 2, 0:n * P]
            ve.tensor_tensor(rounded(lower), raw[C:P, k % 3, 0:n * P], lower, ALU.subtract).then_inc(x_done, 1)

        def ve_r_lo(ve, i, k):
            n = GROUPS[k][1]
            ve.wait_ge(r_done, (i * NG + k) * 2 + 2 + 2)
            ve.tensor_tensor(rounded(r_lo[:, k % 2, :, 0:n * P]), r_full[:, :, 0:n * P], r_hi[:, k % 2, :, 0:n * P],
                             ALU.subtract).then_inc(r_lo_done, 1)

        def ve_r3_lo(ve, l, i, m):
            q = mlp_number(l, i, m)
            ve.wait_ge(mlp_act[2], q + 1 + 2)
            ve.tensor_tensor(rounded(r_out[:, m, 1, :]), rc[:, m % 2, :], r_out[:, m, 0, :], ALU.subtract).then_inc(r3_lo_done, 1)

        def ve_msg(ve, i, it, k):
            t0, n = GROUPS[k]
            ve.wait_ge(rows_in[k], (it + 1) * 16 * n)
            for t in range(t0, t0 + n):
                ve.wait_ge(z_done, i * TPI + t + 1 + TPI)
                ve.scalar_tensor_tensor(out=rows[:, t, :], in0=ps_z[:, t % 2, :], scalar=ew[:, bass.ds(i * TPI + t, 1)],
                                        in1=rows[:, t, :], op0=ALU.mult, op1=ALU.add).then_inc(z_read, 1)

        def ve_u(ve, i, it, k, nw):
            t0, n = GROUPS[k]
            ve.wait_ge(rows_in[k], (it + 1) * 16 * n)
            for t in range(t0, t0 + n):
                ve.wait_ge(summed, (it * NG + group_of(last_in(t, U_PLACE)) + 1 + NG) * nw)
                ve.wait_ge(tpw_done, i * TPI + t + 1 + TPI)
                tp = ps_tpw[:, TPW_BANK[t], :].rearrange("p (k c) -> p k c", k=4)
                x = rows[:, t, :].rearrange("p (k c) -> p k c", k=4)
                u = u_ring[:, U_PLACE[t], :, :]
                ve.tensor_tensor(u[:, 0:8:7, :], tp[:, 0:2, :], x[:, 0:1, :].broadcast_to([P, 2, C]), ALU.mult)
                ve.tensor_tensor(u[:, 1:7, :].rearrange("p (k x) c -> p k x c", k=2),
                                 tp[:, 2:4, :].unsqueeze(2).broadcast_to([P, 2, 3, C]),
                                 x[:, 1:4, :].unsqueeze(1).broadcast_to([P, 2, 3, C]), ALU.mult).then_inc(u_done, 1)

        def ve_sums_in(ve, l, b, nw):
            n = b + (l * NB + 1)
            cols = acc[:, :, bass.ds(b * P, P)]
            if nw == 1 and not (isinstance(b, int) and b == NB - 1):
                ve.wait_ge(added, (b + (l * NI + 1)) * NG + (NODE_AT + NG))
            else:
                ve.wait_ge(added, ((l + 1) * NI * NG + NG) * nw)
            if l < 3:
                ve.wait_ge(ht_in, n * 16)
            ve.wait_ge(n_mm, n)
            pass_waits(ve)
            if l == 0:
                ins = ve.scalar_tensor_tensor(out=q_t[:, :, :], in0=h_t[:, :, :], scalar=1.0, in1=cols, op0=ALU.add, op1=ALU.mult)
            elif l == 2:
                ins = ve.tensor_tensor(q_t[:, :, :], h_t[:, :, :], cols, ALU.add)
            else:
                ins = ve.tensor_copy(q_t[:, :, :], cols)
            ins.then_inc(q_ready, 1)
            if l < 3:
                ve.wait_ge(q_ready, n)
                pass_waits(ve)
                ve.tensor_copy(cols, zeros[:, :, :]).then_inc(acc_free, 1)

        def block_of(b):
            return x_all[:, bass.ds(b, 1), :].rearrange("p a d -> p (a d)")

        def ve_stats(ve, l, b):
            n = b + (l * NB + 1)
            ve.wait_ge(x_new, n + 1)
            pass_waits(ve)
            ve.bn_stats(small[:, 8:14], block_of(b)).then_inc(t_bn, 1)
            ve.wait_ge(t_bn, n)
            pass_waits(ve)
            ve.bn_aggr(small[:, 14:16], small[:, 8:14]).then_inc(t_mv, 1)

        def ve_scale(ve, l, b):
            n = b + (l * NB + 1)
            ve.wait_ge(t_root, n)
            ve.reciprocal(small[:, 17:18], small[:, 16:17]).then_inc(t_rstd, 1)
            ve.wait_ge(t_rstd, n)
            ve.scalar_tensor_tensor(out=small[:, 18:19], in0=small[:, 14:15], scalar=-1.0, in1=small[:, 17:18],
                                    op0=ALU.mult, op1=ALU.mult).then_inc(t_scale, 1)

        def ve_table(ve, l, b):
            n = b + (l * NB + 1)
            ve.wait_ge(t_h, n)
            ve.wait_ge(table_out, n * 16)
            ve.tensor_tensor(t_out[:, :], h_new[:, :], R("b_le"), ALU.add).then_inc(t_lb, 1)

        t_lb = sem("t_lb")

        def ve_first(ve, l, b):
            no = ps_node[:, 0, :]
            ve.wait_ge(n_mm, b + (l * NB + 2))
            if l == 0:
                ve.tensor_tensor(y[:, :], no, bias0[:, :], ALU.add).then_inc(n_y, 1)
                ve.wait_ge(n_y, b + 1)
                ve.scalar_tensor_tensor(out=y2[:, :], in0=y[:, :], scalar=LEAKY, in1=y[:, :], op0=ALU.mult,
                                        op1=ALU.max).then_inc(n_lk, 1)
            if l == 1:
                xb = block_of(b)
                ve.scalar_tensor_tensor(out=xb, in0=no, scalar=0.0, in1=xb, op0=ALU.max, op1=ALU.add).then_inc(x_new, 1)
                ve_stats(ve, l, b)
            if l == 2:
                ve.tensor_tensor(y[:, :], no, R("b_g1"), ALU.add).then_inc(g_y, 1)
                ve.wait_ge(g_y, b + 1)
                ve.bn_stats(small[:, 8:14], y[:, :]).then_inc(g_bn, 1)
                ve.wait_ge(g_bn, b + 1)
                pass_waits(ve)
                ve.bn_aggr(small[:, 24:26], small[:, 8:14]).then_inc(g_mv, 1)

        def ve_norm(ve, l, b):
            xb = block_of(b)
            ve.wait_ge(n_root, b + 1)
            ve.tensor_scalar(small[:, 22:23], small[:, 21:22], NORM_EPS, None, ALU.max).then_inc(n_mx, 1)
            ve.wait_ge(n_mx, b + 1)
            ve.reciprocal(small[:, 23:24], small[:, 22:23]).then_inc(n_rn, 1)
            ve.wait_ge(n_rn, b + 1)
            ve.scalar_tensor_tensor(out=xb, in0=y2[:, :], scalar=small[:, 23:24], in1=xb, op0=ALU.mult,
                                    op1=ALU.add).then_inc(x_new, 1)
            ve_stats(ve, l, b)

        def ve_layer_norm(ve, l, b):
            ve.wait_ge(g_root, b + 1)
            ve.reciprocal(small[:, 27:28], small[:, 26:27]).then_inc(g_rstd, 1)
            ve.scalar_tensor_tensor(out=y[:, :], in0=y[:, :], scalar=small[:, 24:25], in1=R("ln_g"), op0=ALU.subtract,
                                    op1=ALU.mult).then_inc(g_lg, 1)
            ve.wait_ge(g_rstd, b + 1)
            ve.wait_ge(g_lg, b + 1)
            ve.scalar_tensor_tensor(out=y2[:, :], in0=y[:, :], scalar=small[:, 27:28], in1=R("ln_b"), op0=ALU.mult,
                                    op1=ALU.add).then_inc(g_lb, 1)

        def ve_second(ve, l, b):
            xb = block_of(b)
            ve.wait_ge(g_mm2, b + 1)
            ve.tensor_tensor(y[:, :], ps_node[:, 1, :], R("b_g2"), ALU.add).then_inc(g_x1, 1)
            ve.wait_ge(g_x1, b + 2)
            ve.tensor_tensor(xb, xb, y[:, :], ALU.add).then_inc(x_new, 1)

        g_y = sem("g_y")

        def ve_node_sums(ve, l, b):
            m = LAST if isinstance(b, int) and b == NB - 1 else P
            ve.wait_ge(o_copied, b + 1)
            ve.wait_ge(o_summed, (b + 1) * 2)
            ve.tensor_tensor(o_sum[0:m, :], o_sum[0:m, :], t_out[0:m, :], ALU.add).then_inc(o_summed, 1)
            ve.wait_ge(o_sqd, b + 1)
            ve.tensor_tensor(o_sq[0:m, :], o_sq[0:m, :], h_new[0:m, :], ALU.add).then_inc(o_summed, 1)

        def ve_parts(l, nw):
            def sums_in(ve, l, b):
                ve_sums_in(ve, l, b, nw)

            return [[(7, sums_in), (9, ve_first), (12, ve_norm), (14, ve_scale)],
                    [(7, sums_in), (9, ve_first), (12, ve_scale), (14, ve_table)],
                    [(7, sums_in), (9, ve_first), (11, ve_layer_norm), (15, ve_second), (16, ve_stats), (18, ve_scale)],
                    [(7, sums_in), (20, ve_node_sums)]][l]

        def load_starts(ve, i, n):
            regs = ve_base_regs
            ve.reg_load(regs[0:min(n, 4)], base_i[0:1, bass.ds(i * BPAD, min(n, 4))])
            if n > 4:
                ve.reg_load(regs[4:n], base_i[0:1, bass.ds(i * BPAD + 4, n - 4)])
            return [ve.snap(r, min_val=0, max_val=NCOL - WIN) for r in regs[0:n]]

        def ve_edges(ve, l, it, nw, node, first):
            i = it - layer_its[l][0]
            if nw > 1:
                for k in range(NG):
                    for m in MLP_REST_AT[l][k]:
                        ve_r3_lo(ve, l, i, m)
                    if l == 2:
                        ve_x_lo(ve, i, k)
                        ve_r_lo(ve, i, k)
                        ve_msg(ve, i, it, k)
                    if l == 3:
                        ve_u(ve, i, it, k, nw)
                    g = it * NG + k
                    ve.wait_ge(wbase_done, g * (nw + 1) + 1)
                    ve.memset(wbase[:, :], 0.0).then_inc(wbase_done, 1)
                    with ve.Fori(0, nw) as w:
                        ve_hot(ve, l, it, k, w, nw)
                        ve_add(ve, l, it, k, w, nw, w * WIN)
                return
            if l == 2 and first:
                ve_x_lo(ve, i, 0)
                ve_x_lo(ve, i, 1)
                ve_r_lo(ve, i, 0)
                ve_x_lo(ve, i, 2)
            if l < 3:
                ve_hot(ve, l, it, 0, 0, 1)
                ve_hot(ve, l, it, 1, 0, 1)
            for k in range(NG):
                if l == 2:
                    ve_msg(ve, i, it, k)
                    ve_r_lo(ve, *ahead(i, k + 1))
                if l < 3 and k + 2 < NG:
                    ve_hot(ve, l, it, k + 2, 0, 1)
                if k == 0 and l < 3:
                    starts = load_starts(ve, i, NG)
                for m in MLP_REST_AT[l][k]:
                    ve_r3_lo(ve, l, i, m)
                if l == 3:
                    ve_u(ve, i, it, k, 1)
                node(2 * k)
                if l == 2:
                    ve_x_lo(ve, *ahead(i, k + 3))
                if l == 3:
                    ve_hot(ve, l, it, k, 0, 1)
                if k == 0 and l == 3:
                    starts = load_starts(ve, i, NG)
                if k >= LAG or not first:
                    ve_add(ve, l, it, k - LAG, 0, 1, starts[k])
                node(2 * k + 1)

        def ve_close(ve, l):
            starts = load_starts(ve, NI, LAG)
            for k in range(LAG):
                ve_add(ve, l, layer_its[l][1], k - LAG, 0, 1, starts[k])

        def ve_final(ve):
            o4 = acc[:, :, 0:NB * P].rearrange("p h (b c) -> p b h c", c=P)
            o0 = o4[:, :, 0, 0:C]
            done = []

            def step(name, ins):
                done.append(name)
                assert FIN[name] == len(done)
                ins.then_inc(f_step, 1)
                ve.wait_ge(f_step, len(done))

            inv_n = float(np.float32(1.0) / np.float32(n_nodes))
            mu, a0, b0, s1 = fin[:, 0, 0:C], fin[:, 1, 0:C], fin[:, 1, C:2 * C], fin[:, 3, 0:C]
            gam0, bet0, gam1 = (R("wc1_norm")[:, j * C:(j + 1) * C] for j in (1, 2, 3))
            ve.wait_ge(o_kept, NB + 1)
            ve.wait_ge(f_mm, 1)
            step("mu", ve.tensor_scalar(mu, ps_edge[:, 0, 0:C], inv_n, None, ALU.mult))
            step("centre", ve.tensor_tensor(o0, o0, mu.unsqueeze(1).broadcast_to([P, NB, C]), ALU.subtract))
            sq = rows[:, 0:-(-NB * C // D), :].rearrange("p t d -> p (t d)")[:, 0:NB * C].rearrange("p (b c) -> p b c", c=C)
            step("square", ve.tensor_tensor(sq, o0, o0, ALU.mult))
            step("var_sum", ve.tensor_reduce(fin[:, 2, 0:C], sq[:, 0:NB - 1, :].rearrange("p b c -> p c b"), AX_X, ALU.add))
            step("var_part", ve.tensor_tensor(fin[0:LAST, 2, 0:C], fin[0:LAST, 2, 0:C], sq[0:LAST, NB - 1, :], ALU.add))
            step("nrm", ve.tensor_reduce(fin[:, 4, C:2 * C], ps_edge[:, 1, C:D].rearrange("p (c x) -> p c x", x=3), AX_X, ALU.add))
            step("nrm_mean", ve.tensor_scalar(fin[:, 4, C:2 * C], fin[:, 4, C:2 * C], float(1.0 / (3.0 * n_nodes)), None, ALU.mult))
            ve.wait_ge(f_mm, 2)
            step("var_mean", ve.tensor_scalar(fin[:, 4, 0:C], ps_edge[:, 2, 0:C], inv_n, None, ALU.mult))
            ve.wait_ge(f_root, 1)
            step("rstd", ve.reciprocal(fin[:, 6, 0:2 * C], fin[:, 5, 0:2 * C]))
            step("a0", ve.tensor_tensor(a0, fin[:, 6, 0:C], gam0, ALU.mult))
            step("s1", ve.tensor_tensor(s1, fin[:, 6, C:2 * C], gam1, ALU.mult))
            step("n0", ve.tensor_tensor(o0, o0, a0.unsqueeze(1).broadcast_to([P, NB, C]), ALU.mult))
            step("x0", ve.tensor_tensor(x_all[:, :, 0:C], x_all[:, :, 0:C], o0, ALU.add))
            step("x0b", ve.tensor_tensor(x_all[:, :, 0:C], x_all[:, :, 0:C], bet0.unsqueeze(1).broadcast_to([P, NB, C]), ALU.add))
            step("s1x", ve.tensor_copy(fin[:, 7, 0:3 * C].rearrange("p (c x) -> p c x", x=3), s1.unsqueeze(2).broadcast_to([P, C, 3])))
            o1a, o1b = o4[:, :, 0, C:P], o4[:, :, 1, :]
            sa, sb_ = fin[:, 7, 0:C], fin[:, 7, C:3 * C]
            step("n1a", ve.tensor_tensor(o1a, o1a, sa.unsqueeze(1).broadcast_to([P, NB, C]), ALU.mult))
            step("n1b", ve.tensor_tensor(o1b, o1b, sb_.unsqueeze(1).broadcast_to([P, NB, P]), ALU.mult))
            step("x1a", ve.tensor_tensor(x_all[:, :, C:P], x_all[:, :, C:P], o1a, ALU.add))
            step("x1b", ve.tensor_tensor(x_all[:, :, P:D], x_all[:, :, P:D], o1b, ALU.add))

        def act_setup(act):
            act.wait_ge(s_const, 7)
            act.wait_ge(t_mv, NB // CH + 1)
            act.activation(stats_all[:, 0, :], mv_all[:, :, 1], ACT.Sqrt, bias=eps[:, 0:1]).then_inc(s_root, 1)
            act.wait_ge(s_scale, 2)
            def chunk(c, half, pair):
                act.wait_ge(s_pstore[half], pair * 16 + 16)
                act.wait_ge(s_ph_t, c * CH + CH)
                for j in range(CH):
                    b = c * CH + j
                    act.activation(rows[:, half * CH + j, :], block_of(b), ACT.Relu,
                                   bias=stats_all[:, 2, bass.ds(b, 1)], scale=stats_all[:, 1, bass.ds(b, 1)]).then_inc(s_ph, 1)
                act.wait_ge(s_ph, c * CH + CH)
                act.dma_start(table[0][bass.ds(c * (CH * P), CH * P), :].rearrange("(b p) d -> p b d", p=P),
                              rows[:, half * CH:(half + 1) * CH, :]).then_inc(s_pstore[half], 16)
                act.wait_ge(s_pht_copied, c * CH + CH + CH)
                act.dma_start(h_t_dram[0][bass.ds(c * CH, CH), :, :].rearrange("b p d -> p b d"),
                              pt[half]).then_inc(s_pstore_t[half], 16)

            by_pairs(act, chunk)

        def act_mlp(act, l, i, stage, m):
            q = mlp_number(l, i, m)
            act.wait_ge(mlp_mm[stage], q + 1 + (2 if stage == 0 else 0))
            if stage == 2:
                act.wait_ge(r3_out[m], i * 32 + 16)
                act.wait_ge(r3_lo_done, mlp_before(l, i, m))
                act.activation(rounded(r_out[:, m, 0, :]), ps_edge[:, m % 2, 0:MW], ACT.Silu)
            dst = (ra, rb, rc)[stage][:, m % 2, :]
            act.activation(dst, ps_edge[:, m % 2, 0:MW], ACT.Silu).then_inc(mlp_act[stage], 1)

        def act_r3_out(act, l, i, m):
            act.wait_ge(r3_lo_done, mlp_number(l, i, m) + 1 + 2)
            for q in range(2):
                act.dma_start(r3_dram[bass.ds(i, 1), q, :, :, m * MW:(m + 1) * MW].rearrange("a h j n -> (a j) h n"),
                              r_out[q * C:(q + 1) * C, m, :, :]).then_inc(r3_out[m], 16)

        def act_x_hi(act, i, k):
            n = GROUPS[k][1]
            act.wait_ge(raw_in[k], i * 32 + 32)
            act.wait_ge(a_done, (i * NG + k) * 2 - 2 + 2 * NG)
            act.copy(rounded(x_t[:, k % 2, 0:n * P]), raw[:, k % 3, 0:n * P]).then_inc(x_hi_done, 1)

        def act_r3_copy(act, i, k):
            t0, n = GROUPS[k]
            act.wait_ge(r3_in[k // 2], i * 32 + 32)
            last = GROUPS[(k - 2) % NG][0] + GROUPS[(k - 2) % NG][1] - (TPI if k < 2 else 0)
            act.wait_ge(tpw_done, i * TPI + last + TPI)
            for t in range(t0, t0 + n):
                ins = act.copy(rounded(r3_parts[:, k % 2, (t - t0) * P:(t - t0 + 1) * P]),
                               r3[:, t % 2, (t // 2) * P:(t // 2 + 1) * P])
            ins.then_inc(r3_copied, 1)

        def act_relu_a(act, i, k):
            t0, n = GROUPS[k]
            for c in range(2):
                act.wait_ge(a_done, (i * NG + k) * 2 + c + 1 + 2 * NG)
                u = last_use(k, 2, NG)
                ug = u % NG
                tiles = GROUPS[ug][0] + GROUPS[ug][1] - (TPI if u < 0 else 0)
                act.wait_ge(z_done, i * TPI + tiles + TPI)
                if c == 0:
                    act.wait_ge(r_lo_done, i * NG + k + 1)
                act.activation(rounded(r_hi[:, k % 2, c, 0:n * P]), ps_edge[:, c, 0:n * P], ACT.Relu, bias=be1[:, c:c + 1])
                act.activation(r_full[:, c, 0:n * P], ps_edge[:, c, 0:n * P], ACT.Relu, bias=be1[:, c:c + 1]).then_inc(r_done, 1)

        def act_relu_msg(act, i, k):
            t0, n = GROUPS[k]
            act.wait_ge(z_read, i * TPI + t0 + n + TPI)
            act.activation(rows[:, t0:t0 + n, :], rows[:, t0:t0 + n, :], ACT.Relu).then_inc(msg_done, 1)

        def act_load_ht(act, l, b):
            n = b + (l * NB + 1)
            act.wait_ge(n_mm, n)
            if l == 3:
                act.wait_ge(o_mm, b + 1)
            act.dma_start(h_t[:, :, :].rearrange("p c n -> p (c n)"),
                          h_t_dram[l][bass.ds(b, 1), :, :].rearrange("a p d -> p (a d)")).then_inc(ht_in, 16)

        def act_square(act, l, b):
            act.wait_ge(n_lk, b + 1)
            act.activation(y[:, :], y2[:, :], ACT.Square, accum_out=small[:, 20:21]).then_inc(n_ss, 1)
            act.wait_ge(n_ss, b + 1)
            act.activation(small[:, 21:22], small[:, 20:21], ACT.Sqrt).then_inc(n_root, 1)

        def act_g_root(act, l, b):
            act.wait_ge(g_mv, b + 1)
            act.activation(small[:, 26:27], small[:, 25:26], ACT.Sqrt, bias=eps[:, 0:1]).then_inc(g_root, 1)

        def act_y_t(act, l, b):
            if l == 2:
                act.wait_ge(g_tp, b + 1)
                act.activation(y_t[:, :, :], ps_tp[:, 2:4, :], ACT.Relu).then_inc(g_yt, 1)
            else:
                act.wait_ge(o_tp, b + 2)
                act.copy(y_t[:, :, :], ps_tp[:, 2:4, :]).then_inc(o_bt, 1)

        def act_a(act, l, b):
            act.wait_ge(n_mm, b + (3 * NB + 2))
            act.copy(y[:, :], ps_node[:, 0, :]).then_inc(o_acopy, 1)

        def act_root(act, l, b):
            act.wait_ge(t_mv, b + (l * NB + 1) + (NB // CH + 1))
            act.activation(small[:, 16:17], small[:, 15:16], ACT.Sqrt, bias=eps[:, 0:1]).then_inc(t_root, 1)

        def act_h(act, l, b):
            n = b + (l * NB + 1)
            act.wait_ge(t_scale, n)
            act.wait_ge(table_out, n * 16)
            act.activation(h_new[:, :], block_of(b), ACT.Relu, bias=small[:, 18:19], scale=small[:, 17:18]).then_inc(t_h, 1)
            if l == 0:
                act.wait_ge(t_h, n)
                act.dma_start(table[1][bass.ds(b * P, P), :], h_new[:, :]).then_inc(table_out, 16)

        def act_h_t(act, l, b):
            n = b + (l * NB + 1)
            if l == 1:
                act.wait_ge(t_lb, b + 1)
                act.dma_start(table[2][bass.ds(b * P, P), :], t_out[:, :]).then_inc(table_out, 16)
            act.wait_ge(t_tp, n)
            act.wait_ge(ht_out, n * 16)
            act.copy(h_new_t[:, :, :], ps_tp[:, 0:2, :]).then_inc(t_ht, 1)
            act.wait_ge(t_ht, n + 1)
            act.dma_start(h_t_dram[l + 1][bass.ds(b, 1), :, :].rearrange("a p d -> p (a d)"),
                          h_new_t[:, :, :].rearrange("p c n -> p (c n)")).then_inc(ht_out, 16)

        def act_up(act, l, b):
            act.wait_ge(t_tab, b + 1)
            act.copy(t_out[:, :], ps_up).then_inc(t_up, 1)
            act.wait_ge(t_up, b + 2)
            act.dma_start(table[3][bass.ds(b * P, P), :], t_out[:, :]).then_inc(table_out, 16)

        def act_o(act, l, b):
            act.wait_ge(o_mm, b + 2)
            act.wait_ge(o_summed, (b + 1) * 2)
            act.copy(t_out[:, :], ps_node[:, 1, :]).then_inc(o_copied, 1)
            act.activation(h_new[:, :], ps_node[:, 1, :], ACT.Square).then_inc(o_sqd, 1)
            act.copy(acc[:, :, bass.ds(b * P, P)], ps_node[:, 1, :].rearrange("p (h c) -> p h c", h=2)).then_inc(o_kept, 1)

        ACT_PARTS = [[(4, act_load_ht), (10, act_square), (13, act_root), (15, act_h), (17, act_h_t)],
                     [(4, act_load_ht), (10, act_root), (13, act_h), (15, act_h_t)],
                     [(4, act_load_ht), (10, act_g_root), (13, act_y_t), (17, act_root), (19, act_h), (21, act_h_t), (23, act_up)],
                     [(9, act_a), (9, act_load_ht), (17, act_y_t), (19, act_o)]]

        def act_edges(act, l, it, nw, node, first):
            i = it - layer_its[l][0]
            if nw > 1:
                for k in range(NG):
                    for stage, m in MLP_AT[l][k]:
                        act_mlp(act, l, i, stage, m)
                    for m in MLP_OUT_AT[l][k]:
                        act_r3_out(act, l, i, m)
                    if l == 2:
                        act_x_hi(act, i, k)
                        act_relu_a(act, i, k)
                        act_relu_msg(act, i, k)
                    if l == 3:
                        act_r3_copy(act, i, k)
                return
            if l == 3:
                act_r3_copy(act, i, 0)
            if l == 2 and first:
                act_x_hi(act, i, 0)
                act_x_hi(act, i, 1)
                act_relu_a(act, i, 0)
                act_x_hi(act, i, 2)
            for k in range(NG):
                for stage, m in MLP_AT[l][k]:
                    act_mlp(act, l, i, stage, m)
                for m in MLP_OUT_AT[l][k]:
                    act_r3_out(act, l, i, m)
                if l == 2:
                    act_relu_a(act, *ahead(i, k + 1))
                if l == 2:
                    node(2 * k)
                    act_relu_msg(act, i, k)
                    act_x_hi(act, *ahead(i, k + 3))
                    node(2 * k + 1)
                else:
                    if l == 3 and k + 1 < NG:
                        act_r3_copy(act, i, k + 1)
                    node(2 * k)
                    node(2 * k + 1)

        def act_layer(act, l, nw):
            if l:
                act.wait_ge(ht_out, 16 * l * NB + 16)
            else:
                for half in range(2):
                    act.wait_ge(s_pstore_t[half], stored(half))
            if l == 2:
                for m in range(MB):
                    act.wait_ge(r3_out[m], 32 * NI + 16)
            if l == 3:
                act.wait_ge(table_out, 16 * 3 * NB + 16)
            run_layer(act, l, nw, act_edges, ACT_PARTS[l])

        def act_final(act):
            act.wait_ge(f_step, FIN["var_mean"])
            act.activation(fin[:, 5, 0:2 * C], fin[:, 4, 0:2 * C], ACT.Sqrt, bias=eps[:, 0:1]).then_inc(f_root, 1)

        taken = [0]

        def carve(*dims):
            n = int(np.prod(dims))
            piece = arena[:, taken[0]:taken[0] + n]
            taken[0] += n + n % 2
            return piece if len(dims) == 1 else piece.rearrange("p (a b) -> p a b", a=dims[0])

        early = carve((NI + 1) * BPAD)
        base_f = carve((NI + 1) * BPAD)
        bn_c = carve(CH, 6)
        mv_c = carve(CH, 2)
        mv_all = carve(NB, 2)
        stats_all = carve(3, NB)
        pt = [carve(CH, D), r3[:, :, :].rearrange("p q n -> p (q n)")[:, 0:CH * D].rearrange("p (b d) -> p b d", d=D)]
        w_e2 = carve(2, D)
        w_le = carve(2, D)
        b12 = carve(2, D)
        be2 = carve(2)
        we1 = carve(D)
        m4 = carve(D)
        bc_rest = carve(2, D)
        bc_parts = carve(3, D // 2).bitcast(BF16)
        fl = carve(8)
        flag_f = carve(2)
        assert taken[0] <= 8 * 4 * WIN + 8 * 8 * C - D
        iota_i = sb("iota_i", [P, WIN], I32)
        spare = sb("spare", [1, 10])
        s_pol = sem("s_pol")
        s_w3 = sem("s_w3")
        s_dst_again = sem("s_dst_again")
        gate_step = sem("gate_step")
        sums_clear = sem("sums_clear")
        dst_step = sem("dst_step")
        sh_in = [sem("sh_in0"), sem("sh_in1")]
        passed = sem("passed")
        bn_part = sem("bn_part")
        mv_part = sem("mv_part")
        early_in = sem("early_in")
        ve_base_regs = []

        PRE = {n: i + 1 for i, n in enumerate(
            ["zeros", "base0", "acc0", "dst_f", "base_f", "m4", "bias0", "m4_hi", "m4_lo", "we1_hi",
             "we1_lo", "wc_hi", "wc_lo", "bc_hi", "bc_r1",
             "bc_mid", "bc_r2", "bc_lo"] + [f"rel{k}" for k in range(NG)] +
            ["rel_max", "rel_min", "over", "under", "early", "early_max"])}
        FIN = {n: i + 1 for i, n in enumerate(
            ["mu", "centre", "square", "var_sum", "var_part", "nrm", "nrm_mean", "var_mean", "rstd", "a0", "s1", "n0", "x0",
             "x0b", "s1x", "n1a", "n1b", "x1a", "x1b"])}
        POLY = 12

        block = ctx.enter_context(nc.Block())
        paths = ((1, "a window for each group"), (ALLWIN, "all windows"))

        def credits(nw):
            return {
                "pe": [(summed, NG * nw), (a_done, 2 * NG), (tpw_done, TPI), (z_done, TPI), (mlp_mm[0], 2), (n_mm, 1), (o_tp, 1), (o_mm, 1)],
                "ve": [(added, NG * nw), (z_read, TPI), (u_done, TPI), (x_new, 1), (x_done, NG), (r_lo_done, 1), (r3_lo_done, 2), (wbase_done, 1), (g_x1, 1), (o_summed, 2)],
                "act": [(r_done, 2), (mlp_act[2], 2), (t_up, 1), (o_acopy, 1), (g_yt, 1), (o_bt, 1), (t_ht, 1), (o_kept, 1), (r3_copied, NG)],
            }

        def branch(eng, program):
            eng.wait_ge(s_flag, 1)
            reg = eng.value_load(flag_i[0:1, 0:1], min_val=-(1 << 24), max_val=1 << 24)
            with eng.If(reg < 1):
                program(1)
            with eng.Else():
                program(ALLWIN)

        @block.sync
        def _(sp):
            sp.dma_start(early, io["early"].partition_broadcast(P)).then_inc(early_in, 16)
            for j, s in enumerate([*s_pstore, *s_pstore_t, table_out, ht_out, *r3_out]):
                sp.dma_start(spare[0:1, j:j + 1], io["early"][0:1]).then_inc(s, 16)
            sp_setup(sp)

            def program(nw):
                if nw > 1:
                    sp.dma_start(rel[:, :].bitcast(I32), io["dst"]).then_inc(s_dst_again, 16)
                sp_layer(sp, 0, nw)
                sp_layer(sp, 1, nw)
                sp_layer_2(sp)
                sp_layer_3(sp, nw)

            branch(sp, program)
            sp.wait_ge(f_step, FIN["x1b"])
            sp.dma_start(io["out"].rearrange("(b p) d -> p b d", p=P), x_all[:, :, :]).then_inc(s_out, 16)
            sp.wait_ge(s_out, 16)

        @block.gpsimd
        def _(pool):
            pool_setup(pool)

            def program(nw):
                for l in range(4):
                    pool_layer(pool, l, nw)

            branch(pool, program)

        @block.tensor
        def _(pe):
            pe_setup(pe)

            def program(nw):
                for s, v in credits(nw)["pe"]:
                    pe.sem_inc(s, v)
                for l in range(4):
                    if l == 2:
                        pe.wait_ge(s_bc, 48)
                    if l == 3:
                        pe.wait_ge(t_up, NB + 1)
                        pe.wait_ge(s_w3, 48)
                    run_layer(pe, l, nw, pe_edges, PE_PARTS[l], pe_close)

            branch(pe, program)
            pe_final(pe)

        @block.vector
        def _(ve):
            ve.sem_inc(s_pht_copied, CH)
            ve.sem_inc(t_mv, 1)
            ve.wait_ge(early_in, 16)
            ve_setup(ve)
            ve_base_regs.extend(ve.alloc_register(f"window_start{k}") for k in range(NG))

            def program(nw):
                for s, v in credits(nw)["ve"]:
                    ve.sem_inc(s, v)
                if nw > 1:
                    ve.wait_ge(s_dst_again, 16)
                    ve.tensor_copy(rel[:, :], rel[:, :].bitcast(I32)).then_inc(dst_step, 1)
                    ve.wait_ge(dst_step, 1)

                for l in range(4):
                    if l == 2:
                        ve.wait_ge(s_pol, 16)
                        ve.tensor_scalar(ew[:, :], ew[:, :], 0.0, 1.0, ALU.max, ALU.min).then_inc(gate_step, 1)
                        ve.wait_ge(gate_step, 1)
                        ve.tensor_scalar(ew[:, :], ew[:, :], 0.01, None, ALU.add).then_inc(gate_step, 1)
                        ve.wait_ge(gate_step, 2)
                    if l == 3:
                        for k in range(3):
                            ve.wait_ge(raw_in[k], (NI + 1) * 32)
                        ve.memset(m_sums[:, :], 0.0).then_inc(sums_clear, 1)
                        ve.wait_ge(sums_clear, 1)
                    run_layer(ve, l, nw, ve_edges, ve_parts(l, nw), ve_close)

            branch(ve, program)
            ve_final(ve)

        @block.scalar
        def _(act):
            act.sem_inc(s_ph_t, 2 * CH)
            act_setup(act)

            def program(nw):
                for s, v in credits(nw)["act"]:
                    act.sem_inc(s, v)
                for l in range(4):
                    act_layer(act, l, nw)

            branch(act, program)
            act_final(act)


def layouts(a, n_nodes, n_edges):
    f = {k: np.asarray(v) for k, v in a.items()}
    NB, NI = shapes(n_nodes, n_edges)
    ep = NI * TPI * P

    def edges(v, fill=0):
        out = np.full((ep,) + v.shape[1:], fill, v.dtype)
        out[:n_edges] = v
        return out

    def tiles(v):
        return np.ascontiguousarray(np.moveaxis(v.reshape((NI * TPI, P) + v.shape[1:]), 0, 1))

    d = {}
    x = np.zeros((NB * P, D), np.float32)
    x[:n_nodes] = f["x"]
    d["x"] = x
    src = edges(f["src"])
    dst = edges(f["dst"], n_nodes)
    d["src"], d["dst"] = tiles(src), tiles(dst)
    base = np.zeros((NI + 1, BPAD), np.int32)
    early = np.zeros((NI + 1, BPAD), np.float32)
    for k, (t0, n) in enumerate(GROUPS):
        row, slot = (k + LAG) // NG, (k + LAG) % NG
        base[row:NI + row, slot] = dst.reshape(NI, TPI, P)[:, t0, 0]
        early[row:NI + row, slot] = np.maximum(0, P * (np.arange(NI) - (0 if k >= NODE_AT else 1)))
    d["base"] = base.reshape(1, (NI + 1) * BPAD)
    d["early"] = early.reshape((NI + 1) * BPAD)
    d["ew"] = tiles(edges(f["edge_weight"]))
    d["sh"] = tiles(edges(f["edge_attr_4"]))
    d["pol"] = tiles(edges(np.ascontiguousarray(f["edge_attr_65"][:, 0])))
    raw = edges(np.ascontiguousarray(f["edge_attr_65"][:, 1:]))
    d["raw"] = np.zeros((NI + 1, C, TPI * P), np.float32)
    d["raw"][:NI] = raw.reshape(NI, TPI * P, C).transpose(0, 2, 1)
    rbf = np.zeros((NI, TPI + 1, P, 16), np.float32)
    rbf[:, :TPI] = edges(f["edge_attr_16"]).reshape(NI, TPI, P, 16)
    d["rbf"] = np.ascontiguousarray(rbf.reshape(NI, 9, 2, P, 16).transpose(0, 2, 4, 1, 3)).reshape(NI, 32, 9 * P)
    L0, L1, L2, L3 = "L0_gnn_", "L1_gnn_", "L2_gnn_", "L3_gnn_"

    def blocks(w0, w1, rows_mixed, cols_mixed):
        m = np.zeros((D, D), np.float32)
        m[:C, :C] = w0
        for q in range(3):
            r = C + q + 3 * np.arange(C) if rows_mixed else C + C * q + np.arange(C)
            c = C + q + 3 * np.arange(C) if cols_mixed else C + C * q + np.arange(C)
            m[np.ix_(r, c)] = w1
        return m

    by_name = {
        "l0_w1": f[L0 + "W1"].T, "l0_w2": f[L0 + "W2"].T, "l1_w1": f[L1 + "W1"].T, "l1_w2": f[L1 + "W2"].T,
        "e2": f[L2 + "W_e2"], "le": f[L2 + "W_le"].T, "g1": f[L2 + "W_g1"].T, "g2": f[L2 + "W_g2"].T,
        "up": blocks(f[L3 + "W_up0"], f[L3 + "W_up1"], True, False),
        "lin": blocks(f[L3 + "W_lin0"], f[L3 + "W_lin1"], False, False),
        "wb": blocks(f[L3 + "WB0"], f[L3 + "WB1"], False, True),
        "sc": blocks(f[L3 + "Wsc0"], f[L3 + "Wsc1"], True, True),
    }
    d["weights"] = np.stack([by_name[n] for n in WEIGHTS])
    w0, w1 = f[L3 + "Wc0"], f[L3 + "Wc1"]
    rowd = {
        "b_le": f[L2 + "b_le"], "b_g1": f[L2 + "b_g1"],
        "ln_g": f[L2 + "ln_g"], "ln_b": f[L2 + "ln_b"], "b_g2": f[L2 + "b_g2"],
        "wc0a": np.concatenate([w0[:, 3], w1[:, 2], w0[:, 1], w1[:, 1]]),
        "wc0b": np.concatenate([w0[:, 0], w1[:, 0], w0[:, 4], w1[:, 3]]),
        "wc1_norm": np.concatenate([w0[:, 2], f[L3 + "gamma0"], f[L3 + "beta0"], f[L3 + "gamma1"]]),
    }
    d["b12"] = np.concatenate([f[L0 + "b1"], f[L0 + "b2"]])
    d["rowc"] = np.concatenate([rowd[n] for n in ROWS])
    d["we1"] = np.concatenate([f[L2 + "W_e1"].T, f[L2 + "W_e1"].T])
    d["be1"] = f[L2 + "b_e1"].reshape(2, P).T
    d["be2"] = f[L2 + "b_e2"].reshape(2, P).T

    def twice(w):
        r, c = w.shape
        m = np.zeros((2 * r, 2 * c), np.float32)
        m[:r, :c] = w
        m[r:, c:] = w
        return m

    d["m1"], d["m2"], d["m3"] = twice(f[L3 + "M1"]), twice(f[L3 + "M2"]), twice(f[L3 + "M3"])
    d["m4"] = np.concatenate([f[L3 + "M4"], f[L3 + "M4"]])
    return {k: np.ascontiguousarray(v) for k, v in d.items()}


def kernel(**inputs):
    import concourse.bacc as _bacc
    from concourse import mybir as _mybir
    from concourse.bass_utils import run_bass_kernel_spmd as _run

    n_nodes, n_edges = inputs["x"].shape[0], inputs["src"].shape[0]
    nb, _ = shapes(n_nodes, n_edges)
    nc = _bacc.Bacc("TRN2", target_bir_lowering=False, num_devices=1)
    arrays, io = {}, {}
    for name, a in layouts(inputs, n_nodes, n_edges).items():
        arrays[f"in_{name}"] = a
        io[name] = nc.dram_tensor(f"in_{name}", a.shape, _mybir.dt.from_np(a.dtype), kind="ExternalInput").ap()
    io["out"] = nc.dram_tensor("out_x", (nb * P, D), _mybir.dt.float32, kind="ExternalOutput").ap()
    build(nc, io, n_nodes, n_edges)
    r = _run(nc, [arrays], core_ids=[0])
    return r.results[0]["out_x"][:n_nodes]
```
